# Optimizing a Trainium2 kernel written in Bass

```python
import numpy as np
import jax
import jax.numpy as jnp

def _softmax(x, axis=-1):
    return jax.nn.softmax(x, axis=axis)

def _gelu(x):
    return jax.nn.gelu(x, approximate=True)

def _silu(x):
    return jax.nn.silu(x)

def _sigmoid(x):
    return jax.nn.sigmoid(x)

def _layernorm(x, axis=-1, eps=1e-05):
    m = jnp.mean(x, axis=axis, keepdims=True)
    v = jnp.var(x, axis=axis, keepdims=True)
    return (x - m) / jnp.sqrt(v + eps)

def _scatter_add(tgt, idx, src, axis=0):
    return tgt.at[idx].add(src)

def _segment_sum(src, seg, n):
    return jax.ops.segment_sum(src, seg, n)
kernel_name = 'mk_gnn_ffn_d2_gnn_r32_ace2a0'

def setup_inputs(seed: int=0):
    np.random.seed(seed)
    _w = jnp.asarray

    def _rec_inputs():
        import jax
        import jax.numpy as jnp
        _gk = jax.random.key(seed)
        x = -0.0002117 + 1 * jax.random.normal(jax.random.fold_in(_gk, 1), (3125, 256), jnp.float32)
        src = jax.random.randint(jax.random.fold_in(_gk, 2), (50000,), 0, 3125, jnp.int32)
        dst = jnp.minimum((3125 * jax.random.uniform(jax.random.fold_in(_gk, 3), (50000,)) ** 2.0).astype(jnp.int32), 99999)
        _o = jnp.argsort(dst, stable=True)
        src = src[_o]
        dst = dst[_o]
        return (x, src, dst)
    x, src, dst = _rec_inputs()

    def _L0_gnn_setup():
        import jax, jax.numpy as jnp
        import numpy as np
        N = 3125
        D = 256
        E = 9375
        BN_EPS = 1e-05

        def _batchnorm(x, gamma, beta):
            mean = jnp.mean(x, axis=0)
            var = jnp.var(x, axis=0)
            return (x - mean) * jax.lax.rsqrt(var + BN_EPS) * gamma + beta
        key = jax.random.key(seed)
        ks = jax.random.split(key, 8)
        h = jax.random.normal(ks[0], (N, D), dtype=jnp.float32)
        edge_index = jax.random.randint(ks[1], (2, E), 0, N, dtype=jnp.int64)
        W1 = jax.random.normal(ks[2], (D, 2 * D), dtype=jnp.float32) / np.sqrt(D)
        b1 = jnp.zeros((2 * D,), dtype=jnp.float32)
        g1 = jnp.ones((2 * D,), dtype=jnp.float32)
        bt1 = jnp.zeros((2 * D,), dtype=jnp.float32)
        W2 = jax.random.normal(ks[3], (2 * D, D), dtype=jnp.float32) / np.sqrt(2 * D)
        b2 = jnp.zeros((D,), dtype=jnp.float32)
        g2 = jnp.ones((D,), dtype=jnp.float32)
        bt2 = jnp.zeros((D,), dtype=jnp.float32)
        eps_gin = jnp.zeros((), dtype=jnp.float32)
        return {'h': h, 'edge_index': edge_index, 'W1': W1, 'b1': b1, 'g1': g1, 'bt1': bt1, 'W2': W2, 'b2': b2, 'g2': g2, 'bt2': bt2, 'eps_gin': eps_gin}
    _L0_gnn_all = _L0_gnn_setup()
    _L0_gnn_in = {k: v for k, v in _L0_gnn_all.items() if k in ('W1', 'b1', 'g1', 'bt1', 'W2', 'b2', 'g2', 'bt2', 'eps_gin')}
    del _L0_gnn_all

    def _L0_ffn_setup():
        import jax, jax.numpy as jnp
        import numpy as np
        B, N, D = (16, 128, 256)
        NUM_EXPERTS, TOP_K, HEADS = (4, 2, 4)
        N_EDGES = 32768
        LN_EPS = 1e-05

        def _layernorm(x, g, b):
            mu = x.mean(-1, keepdims=True)
            var = ((x - mu) ** 2).mean(-1, keepdims=True)
            return (x - mu) * jax.lax.rsqrt(var + LN_EPS) * g + b

        def _forward(x, edge_index, W_gat, att_src, att_dst, b_gat, ln_gamma, ln_beta, W1, b1, W2, b2):
            Bc, Nc, Dc = x.shape
            M = Bc * Nc
            x_flat = x.reshape(M, Dc)
            h = (x_flat @ W_gat).reshape(M, HEADS, NUM_EXPERTS)
            loops = jnp.arange(M, dtype=edge_index.dtype)
            src = jnp.concatenate([edge_index[0], loops])
            dst = jnp.concatenate([edge_index[1], loops])
            a_src = (h * att_src).sum(-1)
            a_dst = (h * att_dst).sum(-1)
            e = jax.nn.leaky_relu(a_src[src] + a_dst[dst], negative_slope=0.2)
            e_max = jax.ops.segment_max(e, dst, num_segments=M)
            ee = jnp.exp(e - e_max[dst])
            denom = jax.ops.segment_sum(ee, dst, num_segments=M)
            alpha = ee / (denom[dst] + 1e-16)
            msg = h[src] * alpha[:, :, None]
            agg = jax.ops.segment_sum(msg, dst, num_segments=M).reshape(M, HEADS * NUM_EXPERTS) + b_gat
            scores = _layernorm(agg, ln_gamma, ln_beta).reshape(M, HEADS, NUM_EXPERTS).mean(1)
            scores = scores.reshape(Bc, Nc, NUM_EXPERTS)
            topk_s, topk_i = jax.lax.top_k(scores, TOP_K)
            w = jax.nn.softmax(topk_s, axis=-1)
            out = jnp.zeros_like(x)
            for ei in range(NUM_EXPERTS):
                g = jnp.where(topk_i == ei, w, 0.0).sum(-1)
                hh = jax.nn.gelu(x @ W1[ei] + b1[ei], approximate=False)
                out = out + g[..., None] * (hh @ W2[ei] + b2[ei])
            return out
        key = jax.random.key(seed)
        ks = jax.random.split(key, 8)
        s = 0.05
        return {'x': jax.random.normal(ks[0], (B, N, D), jnp.float32), 'W_gat': jax.random.normal(ks[1], (D, HEADS * NUM_EXPERTS), jnp.float32) * s, 'att_src': jax.random.normal(ks[2], (HEADS, NUM_EXPERTS), jnp.float32) * s, 'att_dst': jax.random.normal(ks[3], (HEADS, NUM_EXPERTS), jnp.float32) * s, 'b_gat': jnp.zeros((HEADS * NUM_EXPERTS,), jnp.float32), 'ln_gamma': jnp.ones((HEADS * NUM_EXPERTS,), jnp.float32), 'ln_beta': jnp.zeros((HEADS * NUM_EXPERTS,), jnp.float32), 'W1': jax.random.normal(ks[4], (NUM_EXPERTS, D, 2 * D), jnp.float32) * s, 'b1': jnp.zeros((NUM_EXPERTS, 2 * D), jnp.float32), 'W2': jax.random.normal(ks[5], (NUM_EXPERTS, 2 * D, D), jnp.float32) * s, 'b2': jnp.zeros((NUM_EXPERTS, D), jnp.float32), 'edge_index': jax.random.randint(ks[6], (2, N_EDGES), 0, B * N, jnp.int32)}
    _L0_ffn_all = _L0_ffn_setup()
    _L0_ffn_in = {k: v for k, v in _L0_ffn_all.items() if k in ('W_gat', 'att_src', 'att_dst', 'b_gat', 'ln_gamma', 'ln_beta', 'W1', 'b1', 'W2', 'b2', 'edge_index')}
    del _L0_ffn_all

    def _L1_gnn_setup():
        import jax, jax.numpy as jnp
        import numpy as np
        N_NODES = 3125
        N_EDGES = 50000
        IN_FEATS = 256
        OUT_FEATS = 256
        key = jax.random.key(seed)
        k1, k2, k3, k4, k5, k6 = jax.random.split(key, 6)
        h = jax.random.normal(k1, (N_NODES, IN_FEATS), dtype=jnp.float32)
        norm = jax.random.uniform(k2, (N_NODES, 1), dtype=jnp.float32)
        W = jax.random.normal(k3, (OUT_FEATS, IN_FEATS), dtype=jnp.float32) * (1.0 / np.sqrt(IN_FEATS))
        b = jax.random.normal(k4, (OUT_FEATS,), dtype=jnp.float32) * 0.01
        src = jax.random.randint(k5, (N_EDGES,), 0, N_NODES, dtype=jnp.int32)
        dst = jax.random.randint(k6, (N_EDGES,), 0, N_NODES, dtype=jnp.int32)
        return {'h': h, 'norm': norm, 'W': W, 'b': b, 'src': src, 'dst': dst}
    _L1_gnn_all = _L1_gnn_setup()
    _L1_gnn_in = {k: v for k, v in _L1_gnn_all.items() if k in ('W', 'b')}
    del _L1_gnn_all

    def _L1_ffn_setup():
        import math
        import jax, jax.numpy as jnp
        import numpy as np
        CAPACITY_FACTOR = 1.25
        TOP_K = 2
        LN_EPS = 1e-05

        def _layer_norm(x, gamma, beta):
            mu = jnp.mean(x, axis=-1, keepdims=True)
            var = jnp.var(x, axis=-1, keepdims=True)
            return (x - mu) * jax.lax.rsqrt(var + LN_EPS) * gamma + beta
        key = jax.random.key(seed)
        ks = jax.random.split(key, 4)
        B, S, D, F, E = (8, 128, 256, 512, 8)
        x = jax.random.normal(ks[0], (B, S, D), dtype=jnp.float32)
        Wr = jax.random.normal(ks[1], (D, E), dtype=jnp.float32) / np.sqrt(D)
        br = jnp.zeros((E,), jnp.float32)
        W1 = jax.random.normal(ks[2], (E, D, F), dtype=jnp.float32) / np.sqrt(D)
        b1 = jnp.zeros((E, F), jnp.float32)
        W2 = jax.random.normal(ks[3], (E, F, D), dtype=jnp.float32) / np.sqrt(F)
        b2 = jnp.zeros((E, D), jnp.float32)
        gamma = jnp.ones((D,), jnp.float32)
        beta = jnp.zeros((D,), jnp.float32)
        return {'x': x, 'Wr': Wr, 'br': br, 'W1': W1, 'b1': b1, 'W2': W2, 'b2': b2, 'gamma': gamma, 'beta': beta}
    _L1_ffn_all = _L1_ffn_setup()
    _L1_ffn_in = {k: v for k, v in _L1_ffn_all.items() if k in ('Wr', 'br', 'W1', 'b1', 'W2', 'b2', 'gamma', 'beta')}
    del _L1_ffn_all
    return {'x': x, 'src': src, 'dst': dst, 'L0_gnn_W1': _L0_gnn_in['W1'], 'L0_gnn_b1': _L0_gnn_in['b1'], 'L0_gnn_g1': _L0_gnn_in['g1'], 'L0_gnn_bt1': _L0_gnn_in['bt1'], 'L0_gnn_W2': _L0_gnn_in['W2'], 'L0_gnn_b2': _L0_gnn_in['b2'], 'L0_gnn_g2': _L0_gnn_in['g2'], 'L0_gnn_bt2': _L0_gnn_in['bt2'], 'L0_gnn_eps_gin': _L0_gnn_in['eps_gin'], 'L0_ffn_W_gat': _L0_ffn_in['W_gat'], 'L0_ffn_att_src': _L0_ffn_in['att_src'], 'L0_ffn_att_dst': _L0_ffn_in['att_dst'], 'L0_ffn_b_gat': _L0_ffn_in['b_gat'], 'L0_ffn_ln_gamma': _L0_ffn_in['ln_gamma'], 'L0_ffn_ln_beta': _L0_ffn_in['ln_beta'], 'L0_ffn_W1': _L0_ffn_in['W1'], 'L0_ffn_b1': _L0_ffn_in['b1'], 'L0_ffn_W2': _L0_ffn_in['W2'], 'L0_ffn_b2': _L0_ffn_in['b2'], 'L0_ffn_edge_index': _L0_ffn_in['edge_index'], 'L1_gnn_W': _L1_gnn_in['W'], 'L1_gnn_b': _L1_gnn_in['b'], 'L1_ffn_Wr': _L1_ffn_in['Wr'], 'L1_ffn_br': _L1_ffn_in['br'], 'L1_ffn_W1': _L1_ffn_in['W1'], 'L1_ffn_b1': _L1_ffn_in['b1'], 'L1_ffn_W2': _L1_ffn_in['W2'], 'L1_ffn_b2': _L1_ffn_in['b2'], 'L1_ffn_gamma': _L1_ffn_in['gamma'], 'L1_ffn_beta': _L1_ffn_in['beta']}

def reference(x, src, dst, L0_gnn_W1, L0_gnn_b1, L0_gnn_g1, L0_gnn_bt1, L0_gnn_W2, L0_gnn_b2, L0_gnn_g2, L0_gnn_bt2, L0_gnn_eps_gin, L0_ffn_W_gat, L0_ffn_att_src, L0_ffn_att_dst, L0_ffn_b_gat, L0_ffn_ln_gamma, L0_ffn_ln_beta, L0_ffn_W1, L0_ffn_b1, L0_ffn_W2, L0_ffn_b2, L0_ffn_edge_index, L1_gnn_W, L1_gnn_b, L1_ffn_Wr, L1_ffn_br, L1_ffn_W1, L1_ffn_b1, L1_ffn_W2, L1_ffn_b2, L1_ffn_gamma, L1_ffn_beta):
    import jax
    import jax.numpy as jnp

    def _L0_gnn_ref(h, edge_index, W1, b1, g1, bt1, W2, b2, g2, bt2, eps_gin):
        import jax, jax.numpy as jnp
        import numpy as np
        N = 3125
        D = 256
        E = 9375
        BN_EPS = 1e-05

        def _batchnorm(x, gamma, beta):
            mean = jnp.mean(x, axis=0)
            var = jnp.var(x, axis=0)
            return (x - mean) * jax.lax.rsqrt(var + BN_EPS) * gamma + beta
        src, dst = (edge_index[0], edge_index[1])
        agg = jax.ops.segment_sum(h[src], dst, num_segments=N)
        z = (1.0 + eps_gin) * h + agg
        t = jnp.dot(z, W1) + b1
        t = jax.nn.relu(_batchnorm(t, g1, bt1))
        conv_out = jnp.dot(t, W2) + b2
        out = jax.nn.relu(_batchnorm(conv_out + h, g2, bt2))
        return out

    def _L0_ffn_ref(x, W_gat, att_src, att_dst, b_gat, ln_gamma, ln_beta, W1, b1, W2, b2, edge_index):
        import jax, jax.numpy as jnp
        import numpy as np
        B, N, D = (16, 128, 256)
        NUM_EXPERTS, TOP_K, HEADS = (4, 2, 4)
        N_EDGES = 32768
        LN_EPS = 1e-05

        def _layernorm(x, g, b):
            mu = x.mean(-1, keepdims=True)
            var = ((x - mu) ** 2).mean(-1, keepdims=True)
            return (x - mu) * jax.lax.rsqrt(var + LN_EPS) * g + b

        def _forward(x, edge_index, W_gat, att_src, att_dst, b_gat, ln_gamma, ln_beta, W1, b1, W2, b2):
            Bc, Nc, Dc = x.shape
            M = Bc * Nc
            x_flat = x.reshape(M, Dc)
            h = (x_flat @ W_gat).reshape(M, HEADS, NUM_EXPERTS)
            loops = jnp.arange(M, dtype=edge_index.dtype)
            src = jnp.concatenate([edge_index[0], loops])
            dst = jnp.concatenate([edge_index[1], loops])
            a_src = (h * att_src).sum(-1)
            a_dst = (h * att_dst).sum(-1)
            e = jax.nn.leaky_relu(a_src[src] + a_dst[dst], negative_slope=0.2)
            e_max = jax.ops.segment_max(e, dst, num_segments=M)
            ee = jnp.exp(e - e_max[dst])
            denom = jax.ops.segment_sum(ee, dst, num_segments=M)
            alpha = ee / (denom[dst] + 1e-16)
            msg = h[src] * alpha[:, :, None]
            agg = jax.ops.segment_sum(msg, dst, num_segments=M).reshape(M, HEADS * NUM_EXPERTS) + b_gat
            scores = _layernorm(agg, ln_gamma, ln_beta).reshape(M, HEADS, NUM_EXPERTS).mean(1)
            scores = scores.reshape(Bc, Nc, NUM_EXPERTS)
            topk_s, topk_i = jax.lax.top_k(scores, TOP_K)
            w = jax.nn.softmax(topk_s, axis=-1)
            out = jnp.zeros_like(x)
            for ei in range(NUM_EXPERTS):
                g = jnp.where(topk_i == ei, w, 0.0).sum(-1)
                hh = jax.nn.gelu(x @ W1[ei] + b1[ei], approximate=False)
                out = out + g[..., None] * (hh @ W2[ei] + b2[ei])
            return out
        return _forward(x, edge_index, W_gat, att_src, att_dst, b_gat, ln_gamma, ln_beta, W1, b1, W2, b2)

    def _L1_gnn_ref(h, norm, W, b, src, dst):
        import jax, jax.numpy as jnp
        import numpy as np
        N_NODES = 3125
        N_EDGES = 50000
        IN_FEATS = 256
        OUT_FEATS = 256
        x = h @ W.T + b
        x = norm * x
        msg = x[src]
        agg = jax.ops.segment_sum(msg, dst, num_segments=h.shape[0])
        return agg * norm

    def _L1_ffn_ref(x, Wr, br, W1, b1, W2, b2, gamma, beta):
        import math
        import jax, jax.numpy as jnp
        import numpy as np
        CAPACITY_FACTOR = 1.25
        TOP_K = 2
        LN_EPS = 1e-05

        def _layer_norm(x, gamma, beta):
            mu = jnp.mean(x, axis=-1, keepdims=True)
            var = jnp.var(x, axis=-1, keepdims=True)
            return (x - mu) * jax.lax.rsqrt(var + LN_EPS) * gamma + beta
        B, S, D = x.shape
        E = Wr.shape[1]
        N = B * S
        K = TOP_K
        logits = jnp.mean(x, axis=1) @ Wr + br
        routing_weights = jax.nn.softmax(logits, axis=-1)
        capacity = float(math.ceil(N * CAPACITY_FACTOR / E))
        expected_loads = routing_weights.sum(axis=0) * (N / B)
        scale = jnp.where(expected_loads > capacity, capacity / expected_loads, 1.0)
        routing_weights = jax.nn.softmax(routing_weights * scale, axis=-1)
        rw_tok = jnp.broadcast_to(routing_weights[:, None, :], (B, S, E)).reshape(N, E)
        top_w, top_i = jax.lax.top_k(rw_tok, K)
        top_w = jax.nn.softmax(top_w, axis=-1)
        xf = x.reshape(N, D)
        h = jax.nn.gelu(jnp.einsum('nd,edf->enf', xf, W1) + b1[:, None, :], approximate=False)
        y = jnp.einsum('enf,efd->end', h, W2) + b2[:, None, :]
        w_dense = jnp.zeros((N, E), x.dtype).at[jnp.arange(N)[:, None], top_i].add(top_w)
        out = jnp.einsum('ne,end->nd', w_dense, y).reshape(B, S, D)
        out = _layer_norm(out + x, gamma, beta)
        return out
    edge_index = jnp.stack([src, dst])
    deg = jnp.maximum(jax.ops.segment_sum(jnp.ones(dst.shape, jnp.float32), dst, num_segments=3125), 1.0)
    deg_isqrt = deg ** (-0.5)
    x = x + _L0_gnn_ref(_layernorm(x, axis=-1), edge_index, L0_gnn_W1, L0_gnn_b1, L0_gnn_g1, L0_gnn_bt1, L0_gnn_W2, L0_gnn_b2, L0_gnn_g2, L0_gnn_bt2, L0_gnn_eps_gin)
    x = x + _L0_ffn_ref(_layernorm(x, axis=-1)[None], L0_ffn_W_gat, L0_ffn_att_src, L0_ffn_att_dst, L0_ffn_b_gat, L0_ffn_ln_gamma, L0_ffn_ln_beta, L0_ffn_W1, L0_ffn_b1, L0_ffn_W2, L0_ffn_b2, L0_ffn_edge_index)[0]
    x = x + _L1_gnn_ref(_layernorm(x, axis=-1), deg_isqrt[:, None], L1_gnn_W, L1_gnn_b, src, dst)
    x = x + _L1_ffn_ref(_layernorm(x, axis=-1)[None], L1_ffn_Wr, L1_ffn_br, L1_ffn_W1, L1_ffn_b1, L1_ffn_W2, L1_ffn_b2, L1_ffn_gamma, L1_ffn_beta)[0]
    return x

_drawn_inputs = setup_inputs


def setup_inputs(seed=0):
    import zlib

    import numpy as np

    out = dict(_drawn_inputs(seed))
    spreads = {'L0_gnn_b1': (0.0, 0.8),
     'L0_gnn_g1': (1.0, 0.2),
     'L0_gnn_bt1': (0.0, 0.1),
     'L0_gnn_b2': (0.0, 0.8),
     'L0_gnn_g2': (1.0, 0.2),
     'L0_gnn_bt2': (0.0, 0.1),
     'L0_ffn_b_gat': (0.0, 0.1),
     'L0_ffn_ln_gamma': (1.0, 0.2),
     'L0_ffn_ln_beta': (0.0, 0.1),
     'L0_ffn_b1': (0.0, 0.1),
     'L0_ffn_b2': (0.0, 0.1),
     'L1_ffn_br': (0.0, 0.8),
     'L1_ffn_b1': (0.0, 0.436),
     'L1_ffn_b2': (0.0, 0.34),
     'L1_ffn_gamma': (1.0, 0.2),
     'L1_ffn_beta': (0.0, 0.1)}
    factors = {'L1_gnn_b': 8.0}
    for name, (base, spread) in spreads.items():
        noise = np.random.default_rng([zlib.crc32(name.encode()), seed]).standard_normal(out[name].shape)
        drawn = base * np.exp(spread * noise) if base else spread * noise
        out[name] = jnp.asarray(drawn.astype(out[name].dtype))
    for name, factor in factors.items():
        out[name] = (out[name] * factor).astype(out[name].dtype)
    return out
```

```python
import numpy as np
import concourse.bass as bass
from concourse import mybir
from contextlib import ExitStack

f32 = mybir.dt.float32
bf16 = mybir.dt.bfloat16
i32 = mybir.dt.int32
ALU = mybir.AluOpType
ACT = mybir.ActivationFunctionType
AX = mybir.AxisListType

P = 128
N = 3125
D = 256
KD = D // P
F = 512
KF = F // P
NT = -(-N // P)
NP = NT * P
FULL = N // P
TAIL = N - FULL * P
GT = 5
NG = NT // GT
GN = GT * P
CH = 512
NCH = N // CH
CTAIL = N - NCH * CH

E1 = 50000
ET = 400
EROWS = E1 // ET
NB = NT + 1
PAD_DST = NT * P
HIST = NB * ET
HCH = 512
HCHUNKS = 3 * (-(-HIST // (3 * HCH)))
HISTP = HCHUNKS * HCH
TILES = P * ET // P
TCH = -(-TILES // P)
TLAST = TILES - (TCH - 1) * P
GROUP = 2
HALF = 8
PAIRS = HALF // GROUP
MAXPAIRS = (-(-E1 // P) + (NT - 1) + NT) // GROUP
ITERS = -(-MAXPAIRS // (2 * PAIRS))
NPAIR = ITERS * 2 * PAIRS
SLOTS = NPAIR * GROUP
RW = D + 1

E2 = 32768
ET2 = E2 // P
HEADS = 4
NE = 4
HK = HEADS * NE
TW = HK + HEADS
DW = 2 * HEADS
NE1 = 8
CAPACITY = float(-(-N * 5 // (4 * NE1)))
EPS = 1e-5


class Chain:

    def __init__(self, eng, sem):
        self.eng, self.sem, self.n = eng, sem, 0

    def __call__(self, ins):
        self.n += 1
        ins.then_inc(self.sem, 1)
        self.eng.wait_ge(self.sem, self.n)


def build(nc, a, out):
    ctx = ExitStack()
    names = set()
    stage_sems = []

    def sb(name, shape, dt=f32):
        return ctx.enter_context(nc.sbuf_tensor(name, shape, dt))

    def sem(name):
        assert name not in names
        names.add(name)
        stage_sems.append(nc.alloc_semaphore(name))
        return stage_sems[-1]

    def end_stage():
        nc.clear_and_free_semaphores(stage_sems)
        nc.all_engine_barrier()
        del stage_sems[:]

    def dram(name, shape, dt=f32):
        return nc.dram_tensor(name, shape, dt, kind="Internal").ap()

    with ctx:
        ring_a = [ctx.enter_context(nc.semaphore(f"ring_a_{k}")) for k in range(2 * HALF)]
        ring_b = [ctx.enter_context(nc.semaphore(f"ring_b_{k}")) for k in range(2 * HALF)]
        done = {"a": 0, "b": 0}
        x_d = a["x"]
        edges_d = dram("edges_sorted", [P * ET, 2], i32)
        rows_d = dram("rows_table", [NP, D])
        srct_d = dram("gat_src_table", [NP, TW])
        dstt_d = dram("gat_dst_table", [NP, DW])
        y_d = dram("expert_outputs", [NE, P, NT * D])

        iota = sb("iota", [P, P])
        pidx = sb("pidx", [P, 1])
        ident = sb("ident", [P, P])
        tri = sb("tri", [P, P], bf16)
        ones_bf = sb("ones_bf", [P, P], bf16)
        ones = sb("ones", [P, P])
        valid = sb("valid", [P, 2])
        X = sb("X", [P, NT, D])
        H = sb("H", [P, NT, D])
        stats = sb("stats", [P, NT, 6])
        mv = sb("mv", [P, NT, 2])
        rstd = sb("rstd", [P, NT])
        eps_col = sb("eps_col", [P, 1])
        norm = sb("norm", [P, NT])
        slot_src = sb("slot_src", [P, GROUP * NPAIR], i32)
        slot_dst = sb("slot_dst", [P, GROUP * NPAIR])
        slot_bkt = sb("slot_bkt", [1, NPAIR // PAIRS], i32)

        def stage_consts():
            s_iota, s_c = sem("iota_made"), sem("const_step")
            with nc.sbuf_tensor("iota_i", [P, P], i32) as iota_i, nc.sbuf_tensor("pidx_i", [P, 1], i32) as pidx_i, \
                    nc.Block() as block:
                @block.gpsimd
                def _(pool):
                    nc.gpsimd.iota(iota_i[:, :], [[1, P]], base=0, channel_multiplier=0).then_inc(s_iota, 1)
                    nc.gpsimd.iota(pidx_i[:, :], [[1, 1]], base=0, channel_multiplier=1).then_inc(s_iota, 1)

                @block.vector
                def _(dve):
                    step = Chain(dve, s_c)
                    nc.vector.memset(ones[:, :], 1.0)
                    nc.vector.memset(ones_bf[:, :], 1.0)
                    nc.vector.memset(eps_col[:, :], EPS)
                    nc.vector.memset(valid[:, :], 1.0)
                    dve.wait_ge(s_iota, 2)
                    nc.vector.tensor_copy(iota[:, :], iota_i[:, :])
                    step(nc.vector.tensor_copy(pidx[:, :], pidx_i[:, :]))
                    nc.vector.tensor_scalar(ident[:, :], iota[:, :], pidx[:, 0:1], None, ALU.is_equal)
                    nc.vector.tensor_scalar(tri[:, :], iota[:, :], pidx[:, 0:1], None, ALU.is_gt)
                    nc.vector.tensor_scalar(valid[:, 1:2], pidx[:, :], float(TAIL), None, ALU.is_lt)

        def stage_sort():
            tmp = ExitStack()

            def t(name, shape, dt=f32):
                return tmp.enter_context(nc.sbuf_tensor(name, shape, dt))

            with tmp:
                dst_i = t("dst_i", [P, ET], i32)
                src_i = t("src_i", [P, ET], i32)
                hi_i = t("hi_i", [P, ET], i32)
                hi_f = t("hi_f", [P, ET])
                pair = t("pair", [P, ET, 2], i32)
                onehot = t("onehot", [P, HISTP], bf16)
                before = t("before", [P, HISTP], bf16)
                total = t("total", [P, HISTP], bf16)
                start = t("start", [P, 1 + HISTP])
                pos_f = t("pos_f", [P, ET])
                pos_i = t("pos_i", [P, ET], i32)
                st_pos = t("st_pos", [P, 2 * HALF], i32)
                st_pair = t("st_pair", [P, 2 * HALF, 2], i32)
                row = t("row", [1, 6, NB])
                rowst = t("rowst", [1, NB])
                bnd = t("bnd", [1, 2, NB], i32)
                col3 = t("col3", [P, 3])
                wid = t("wid", [P, 2, P])
                iota_j = t("iota_j", [P, NPAIR])
                iota_ji = t("iota_ji", [P, NPAIR], i32)
                selb = t("selb", [P, NPAIR])
                tile_j = t("tile_j", [P, NPAIR])
                bkt_j = t("bkt_j", [P, NPAIR])
                val_j = t("val_j", [P, NPAIR])
                nat_i = t("nat_i", [P, TCH, 2 * P], i32)
                nat = t("nat", [P, TCH, 2 * P])
                tcol = t("tcol", [P, TCH, GROUP])
                sel = t("sel", [P, TCH, GROUP, NPAIR])
                pk = t("pk", [1, NPAIR])
                ps = tmp.enter_context(nc.psum_tensor("ps_sort", [P, 8, 512], f32))

                s_pad, s_ld, s_st = sem("sort_pad"), sem("sort_loaded"), sem("sort_step")
                s_oh, s_ct = sem("onehot_made"), sem("counts_made")
                s_be, s_to = sem("before_copied"), sem("total_copied")
                s_pos = sem("positions_made")
                s_begun = sem("scatter_begun")
                s_stg = [sem("scatter_staged_a"), sem("scatter_staged_b")]
                base = done["a"]
                done["a"] += 16 * ET // (2 * HALF)
                flat = lambda ap: ap.rearrange("p b t -> p (b t)")
                with nc.Block() as block:
                    @block.sync
                    def _(sp):
                        sp.wait_ge(s_pad, 2)
                        sp.dma_start(dst_i[0:EROWS, :], a["dst"].rearrange("(p t) -> p t", t=ET)).then_inc(s_ld, 16)
                        sp.dma_start(src_i[0:EROWS, :], a["src"].rearrange("(p t) -> p t", t=ET)).then_inc(s_ld, 16)

                    @block.vector
                    def _(dve):
                        dve.sem_inc(s_to, 1)
                        step = Chain(dve, s_st)
                        nc.vector.memset(dst_i[:, :], PAD_DST).then_inc(s_pad, 1)
                        nc.vector.memset(src_i[:, :], 0).then_inc(s_pad, 1)
                        nc.vector.memset(onehot[:, HIST:HISTP], 0.0)
                        nc.vector.memset(start[:, 0:1], 0.0)
                        dve.wait_ge(s_ld, 32)
                        step(nc.vector.tensor_scalar(hi_i[:, :], dst_i[:, :], 7, None, ALU.logical_shift_right))
                        step(nc.vector.tensor_copy(hi_f[:, :], hi_i[:, :]))
                        nc.vector.tensor_tensor(
                            onehot[:, 0:HIST].rearrange("p (b t) -> p b t", t=ET),
                            hi_f[:, :].unsqueeze(1).to_broadcast([P, NB, ET]),
                            iota[:, 0:NB].unsqueeze(2).to_broadcast([P, NB, ET]), ALU.is_equal).then_inc(s_oh, 1)
                        nc.vector.tensor_copy(pair[:, :, 0], src_i[:, :])
                        step(nc.vector.tensor_copy(pair[:, :, 1], dst_i[:, :]))
                        with dve.Fori(0, HCHUNKS // 3) as i:
                            dve.wait_ge(s_ct, 3 * i + 3)
                            nc.vector.tensor_copy(total[:, bass.ds(i * (3 * HCH), 3 * HCH)],
                                                  flat(ps[:, 3:6, :])).then_inc(s_to, 1)
                        dve.wait_ge(s_to, HCHUNKS // 3 + 1)
                        step(nc.vector.tensor_tensor_scan(
                            start[:, 1:1 + HIST], ones[:, 0:1].to_broadcast([P, HIST]), total[:, 0:HIST],
                            0.0, ALU.mult, ALU.add))
                        dve.wait_ge(s_be, HCHUNKS // 3 + 1)
                        starts = start[:, 0:HIST]
                        step(nc.vector.tensor_copy(rowst[:, :], start[0:1, 0:HIST].rearrange("p (b t) -> p b t", t=ET)[:, :, 0]))
                        step(nc.vector.tensor_tensor(starts, starts, before[:, 0:HIST], ALU.add))
                        step(nc.vector.tensor_tensor(starts, starts, onehot[:, 0:HIST], ALU.mult))
                        step(nc.vector.tensor_reduce(
                            pos_f[:, :], starts.rearrange("p (b t) -> p t b", t=ET), AX.X, ALU.add))
                        nc.vector.tensor_copy(pos_i[:, :], pos_f[:, :]).then_inc(s_pos, 1)

                    @block.tensor
                    def _(pe):
                        pe.wait_ge(s_oh, 1)
                        with pe.Fori(0, HCHUNKS // 3) as i:
                            pe.wait_ge(s_be, i + 1)
                            pe.wait_ge(s_to, i + 1)
                            for k in range(3):
                                rhs = onehot[:, bass.ds(i * (3 * HCH) + k * HCH, HCH)]
                                nc.tensor.matmul(ps[:, k, :], tri[:, :], rhs, start=True, stop=True)
                                nc.tensor.matmul(ps[:, 3 + k, :], ones_bf[:, :], rhs, start=True,
                                                 stop=True).then_inc(s_ct, 1)

                    @block.scalar
                    def _(act):
                        act.sem_inc(s_be, 1)
                        with act.Fori(0, HCHUNKS // 3) as i:
                            act.wait_ge(s_ct, 3 * i + 3)
                            nc.scalar.copy(before[:, bass.ds(i * (3 * HCH), 3 * HCH)],
                                           flat(ps[:, 0:3, :])).then_inc(s_be, 1)
                        act.wait_ge(s_pos, 1)

                        def put(h, at):
                            r = slice(h * HALF, (h + 1) * HALF)
                            nc.scalar.copy(st_pos[:, r], pos_i[:, bass.ds(at, HALF)])
                            nc.scalar.copy(st_pair[:, r, :], pair[:, bass.ds(at, HALF), :]).then_inc(s_stg[h], 1)

                        for h in range(2):
                            put(h, h * HALF)
                        with act.Fori(0, ET // (2 * HALF) - 1) as i:
                            for h in range(2):
                                for k in range(h * HALF, (h + 1) * HALF):
                                    act.wait_ge(ring_a[k], i * 16 + (base + 16))
                                put(h, (i + 1) * (2 * HALF) + h * HALF)

                    @block.gpsimd
                    def _(pool):
                        with pool.Fori(0, ET // (2 * HALF)) as i:
                            for h in range(2):
                                pool.wait_ge(s_stg[h], i + 1)
                                pool.sem_inc(s_begun, 1)
                                for k in range(h * HALF, (h + 1) * HALF):
                                    pool.indirect_dma_start(
                                        out=edges_d, out_offset=bass.IndirectOffsetOnAxis(ap=st_pos[:, k:k + 1], axis=0),
                                        in_=st_pair[:, k, :], in_offset=None).then_inc(ring_a[k], 16)
                        for k in range(2 * HALF):
                            pool.wait_ge(ring_a[k], done["a"])

                s_ij, s_nat, s_sl = sem("iota_j_made"), sem("sorted_loaded"), sem("slot_step")
                s_c3, s_row, s_sb, s_tj = sem("cols_made"), sem("rows_made"), sem("bucket_sel"), sem("tile_made")
                s_wid, s_npad = sem("wide_made"), sem("sorted_pad")
                s_sel, s_slot = sem("tile_sel"), sem("slots_made")
                with nc.Block() as block:
                    @block.gpsimd
                    def _(pool):
                        nc.gpsimd.iota(iota_ji[:, :], [[1, NPAIR]], base=0, channel_multiplier=0).then_inc(s_ij, 1)

                    @block.sync
                    def _(sp):
                        full = (TCH - 1) * P * P
                        sp.dma_start(nat_i[:, 0:TCH - 1, :],
                                     edges_d[0:full, :].rearrange("(c p e) k -> p c (e k)", p=P, e=P)).then_inc(s_nat, 16)
                        sp.wait_ge(s_npad, 1)
                        sp.dma_start(nat_i[0:TLAST, TCH - 1, :],
                                     edges_d[full:P * ET, :].rearrange("(p e) k -> p (e k)", e=P)).then_inc(s_nat, 16)

                    @block.vector
                    def _(dve):
                        step = Chain(dve, s_sl)
                        V = nc.vector
                        V.memset(nat_i[:, TCH - 1, :], PAD_DST).then_inc(s_npad, 1)
                        V.memset(col3[:, :], 0.0)
                        st = rowst[:, :]
                        step(V.tensor_copy(bnd[:, 0, :], st))
                        step(V.tensor_scalar(row[:, 0, 0:NT], bnd[:, 0, 1:NB], -1.0, None, ALU.add))
                        step(V.tensor_copy(bnd[:, 1, 0:NT], row[:, 0, 0:NT]))
                        step(V.tensor_scalar(row[:, 3, 0:NT], st[:, 0:NT], 1.0, None, ALU.add))
                        step(V.tensor_tensor(row[:, 5, 0:NT], row[:, 3, 0:NT], row[:, 0, 0:NT], ALU.subtract))
                        step(V.tensor_scalar(row[:, 5, 0:NT], row[:, 5, 0:NT], 1.5, None, ALU.is_lt))
                        step(V.tensor_scalar(bnd[:, 0, 0:NT], bnd[:, 0, 0:NT], 7, None, ALU.logical_shift_right))
                        step(V.tensor_scalar(bnd[:, 1, 0:NT], bnd[:, 1, 0:NT], 7, None, ALU.arith_shift_right))
                        step(V.tensor_copy(row[:, 0, 0:NT], bnd[:, 0, 0:NT]))
                        step(V.tensor_copy(row[:, 1, 0:NT], bnd[:, 1, 0:NT]))
                        step(V.tensor_tensor(row[:, 2, 0:NT], row[:, 1, 0:NT], row[:, 0, 0:NT], ALU.subtract))
                        step(V.tensor_scalar(row[:, 2, 0:NT], row[:, 2, 0:NT], float(GROUP), None, ALU.add))
                        step(V.tensor_tensor(row[:, 2, 0:NT], row[:, 2, 0:NT], row[:, 5, 0:NT], ALU.mult))
                        step(V.tensor_copy(bnd[:, 1, 0:NT], row[:, 2, 0:NT]))
                        step(V.tensor_scalar(bnd[:, 1, 0:NT], bnd[:, 1, 0:NT], GROUP.bit_length() - 1, None,
                                             ALU.logical_shift_right))
                        step(V.tensor_copy(row[:, 2, 0:NT], bnd[:, 1, 0:NT]))
                        step(V.tensor_tensor_scan(row[:, 3, 0:NT], ones[0:1, 0:1].to_broadcast([1, NT]),
                                                  row[:, 2, 0:NT], 0.0, ALU.mult, ALU.add))
                        step(V.tensor_tensor(row[:, 4, 0:NT], row[:, 3, 0:NT], row[:, 2, 0:NT], ALU.subtract))
                        step(V.tensor_scalar(row[:, 5, 0:NT], row[:, 4, 0:NT], -float(GROUP), None, ALU.mult))
                        V.tensor_tensor(row[:, 5, 0:NT], row[:, 5, 0:NT], row[:, 0, 0:NT], ALU.add).then_inc(s_row, 1)
                        dve.wait_ge(s_ij, 1)
                        step(V.tensor_copy(iota_j[:, :], iota_ji[:, :]))
                        dve.wait_ge(s_c3, 1)
                        step(V.tensor_copy(col3[0:NT, :], ps[0:NT, 0, 0:3]))
                        step(V.tensor_scalar(selb[:, :], iota_j[:, :], col3[:, 1:2], None, ALU.is_ge))
                        step(V.tensor_scalar(tile_j[:, :], iota_j[:, :], col3[:, 0:1], None, ALU.is_lt))
                        step(V.tensor_tensor(selb[:, :], selb[:, :], tile_j[:, :], ALU.mult))
                        V.tensor_copy(wid[:, 0, :], col3[:, 2:3].to_broadcast([P, P]))
                        V.tensor_copy(wid[:, 1, :], pidx[:, 0:1].to_broadcast([P, P])).then_inc(s_wid, 1)
                        dve.wait_ge(s_sb, 1)
                        V.tensor_copy(tile_j[:, :], ps[:, 1, 0:NPAIR])
                        V.tensor_copy(bkt_j[:, :], ps[:, 2, 0:NPAIR])
                        step(V.tensor_copy(val_j[:, :], ps[:, 3, 0:NPAIR]))
                        step(V.scalar_tensor_tensor(tile_j[:, :], iota_j[:, :], float(GROUP), tile_j[:, :], ALU.mult, ALU.add))
                        step(V.tensor_scalar(val_j[:, :], val_j[:, :], -1.0, 4096.0, ALU.add, ALU.mult))
                        step(V.tensor_tensor(tile_j[:, :], tile_j[:, :], val_j[:, :], ALU.add))
                        for c in range(TCH):
                            for g in range(GROUP):
                                last = V.tensor_scalar(tcol[:, c, g:g + 1], pidx[:, :], float(c * P - g), None, ALU.add)
                        step(last)
                        for c in range(TCH):
                            for g in range(GROUP):
                                last = V.tensor_scalar(sel[:, c, g, :], tile_j[:, :], tcol[:, c, g:g + 1], None, ALU.is_equal)
                        dve.wait_ge(s_nat, 32)
                        V.tensor_copy(nat[:, :, :], nat_i[:, :, :]).then_inc(s_sel, 1)
                        pv = pk[:, :].rearrange("p (q k) -> p q k", k=PAIRS)
                        bv = bkt_j[0:1, :].rearrange("p (q k) -> p q k", k=PAIRS)
                        step(V.tensor_copy(pv[:, :, 0], bv[:, :, PAIRS - 1]))
                        for k in range(PAIRS - 2, -1, -1):
                            step(V.scalar_tensor_tensor(pv[:, :, 0], pv[:, :, 0], 32.0, bv[:, :, k], ALU.mult, ALU.add))
                        step(V.tensor_copy(slot_bkt[:, :], pv[:, :, 0]))
                        dve.wait_ge(s_slot, 1)
                        sv = slot_src[:, :].rearrange("p (j g) -> p j g", g=GROUP)
                        dv = slot_dst[:, :].rearrange("p (j g) -> p j g", g=GROUP)
                        step(V.scalar_tensor_tensor(bkt_j[:, :], bkt_j[:, :], -float(P), val_j[:, :], ALU.mult, ALU.add))
                        for g in range(GROUP):
                            V.tensor_copy(sv[:, :, g], ps[:, 4 + g, 0:NPAIR])
                            V.tensor_tensor(dv[:, :, g], ps[:, 6 + g, 0:NPAIR], bkt_j[:, :], ALU.add)

                    @block.tensor
                    def _(pe):
                        pe.wait_ge(s_row, 1)
                        for k in range(3):
                            last = nc.tensor.matmul(ps[0:NT, 0, k:k + 1], row[0:1, 3 + k, 0:NT], ones[0:1, 0:1],
                                                    start=True, stop=True)
                        last.then_inc(s_c3, 1)
                        pe.wait_ge(s_wid, 1)
                        nc.tensor.matmul(ps[:, 1, 0:NPAIR], wid[0:NT, 0, :], selb[0:NT, :], start=True, stop=True)
                        nc.tensor.matmul(ps[:, 2, 0:NPAIR], wid[0:NT, 1, :], selb[0:NT, :], start=True, stop=True)
                        nc.tensor.matmul(ps[:, 3, 0:NPAIR], ones[0:NT, :], selb[0:NT, :], start=True,
                                         stop=True).then_inc(s_sb, 1)
                        pe.wait_ge(s_sel, 1)
                        for k in range(2):
                            for g in range(GROUP):
                                for c in range(TCH):
                                    lhs = nat[:, c, :].rearrange("p (e k) -> p e k", k=2)[:, :, k]
                                    last = nc.tensor.matmul(ps[:, 4 + 2 * k + g, 0:NPAIR], lhs, sel[:, c, g, :],
                                                            start=(c == 0), stop=(c == TCH - 1))
                        last.then_inc(s_slot, 1)

        def rows_norm(tag, load=False, table=False):
            s_x, s_mv, s_std, s_h = sem(tag + "_x"), sem(tag + "_stats"), sem(tag + "_std"), sem(tag + "_h")
            s_t, s_ms = sem(tag + "_table"), sem(tag + "_moment_step")
            with nc.Block() as block:
                @block.sync
                def _(sp):
                    if load:
                        sp.wait_ge(s_h, 1)
                        sp.dma_start(X[:, 0:FULL, :], x_d[0:FULL * P, :].rearrange("(t p) d -> p t d", p=P)).then_inc(s_x, 16)
                        sp.dma_start(X[0:TAIL, FULL, :], x_d[FULL * P:N, :]).then_inc(s_x, 16)
                    if table:
                        sp.wait_ge(s_h, NT + 1)
                        sp.dma_start(rows_d.rearrange("(t p) d -> p t d", p=P), H[:, :, :]).then_inc(s_t, 16)
                        sp.wait_ge(s_t, 16)

                @block.vector
                def _(dve):
                    if load:
                        nc.vector.memset(X[:, FULL, :], 0.0).then_inc(s_h, 1)
                        dve.wait_ge(s_x, 32)
                    else:
                        nc.vector.memset(rstd[:, 0:1], 0.0).then_inc(s_h, 1)
                    with dve.Fori(0, NG) as g:
                        for k in range(GT):
                            nc.vector.bn_stats(stats[:, bass.ds(g * GT + k, 1), :].rearrange("p a b -> p (a b)"),
                                               X[:, bass.ds(g * GT + k, 1), :].rearrange("p a b -> p (a b)"))
                    dve.drain()
                    step = Chain(dve, s_ms)
                    mean_e, sq_e, mean_o, sq_o = (stats[:, :, k] for k in (1, 2, 4, 5))
                    nc.vector.tensor_tensor(sq_e, sq_e, sq_o, ALU.add)
                    nc.vector.tensor_tensor(mv[:, :, 0], mean_e, mean_o, ALU.add)
                    step(nc.vector.tensor_tensor(mean_e, mean_e, mean_o, ALU.subtract))
                    nc.vector.tensor_scalar(mv[:, :, 0], mv[:, :, 0], 0.5, None, ALU.mult)
                    nc.vector.tensor_scalar(sq_e, sq_e, 1.0 / D, EPS, ALU.mult, ALU.add)
                    step(nc.vector.tensor_tensor(mean_o, mean_e, mean_e, ALU.mult))
                    nc.vector.scalar_tensor_tensor(mv[:, :, 1], mean_o, 0.25, sq_e, ALU.mult, ALU.add).then_inc(s_mv, 1)
                    dve.wait_ge(s_std, 1)
                    nc.vector.reciprocal(rstd[:, :], rstd[:, :])
                    dve.drain()
                    with dve.Fori(0, NG) as g:
                        for k in range(GT):
                            i = g * GT + k
                            nc.vector.tensor_scalar(
                                H[:, bass.ds(i, 1), :].rearrange("p a b -> p (a b)"),
                                X[:, bass.ds(i, 1), :].rearrange("p a b -> p (a b)"),
                                mv[:, bass.ds(i, 1), 0], rstd[:, bass.ds(i, 1)],
                                ALU.subtract, ALU.mult).then_inc(s_h, 1)

                @block.scalar
                def _(act):
                    act.wait_ge(s_mv, 1)
                    nc.scalar.activation(rstd[:, :], mv[:, :, 1], ACT.Sqrt).then_inc(s_std, 1)

        def message_pass(tag, acc):
            tmp = ExitStack()
            with tmp:
                rows = tmp.enter_context(nc.sbuf_tensor(tag + "_rows", [P, 2 * HALF, RW], f32))
                hot = tmp.enter_context(nc.sbuf_tensor(tag + "_hot", [P, 2 * HALF, P], f32))
                idx = tmp.enter_context(nc.sbuf_tensor(tag + "_idx", [P, 2 * HALF], i32))
                drel = tmp.enter_context(nc.sbuf_tensor(tag + "_drel", [P, 2 * HALF], f32))
                ps = tmp.enter_context(nc.psum_tensor(tag + "_ps", [P, 2 * PAIRS, 512], f32))
                s_idx = [sem(tag + "_idx_a"), sem(tag + "_idx_b")]
                base = done["a"]
                done["a"] += 16 * ITERS
                s_hot = [sem(tag + "_hot_a"), sem(tag + "_hot_b")]
                s_mm = [sem(tag + "_summed_a"), sem(tag + "_summed_b")]
                s_acc = [sem(tag + "_added_a"), sem(tag + "_added_b")]
                s_one = sem(tag + "_ones")
                s_begun = sem(tag + "_begun")
                with nc.Block() as block:
                    @block.scalar
                    def _(act):
                        with act.Fori(0, ITERS) as i:
                            for h in range(2):
                                act.wait_ge(s_mm[h], i + 1)
                                nc.scalar.copy(idx[:, h * HALF:(h + 1) * HALF],
                                               slot_src[:, bass.ds(i * (2 * HALF) + h * HALF, HALF)]).then_inc(s_idx[h], 1)

                    @block.gpsimd
                    def _(pool):
                        with pool.Fori(0, ITERS) as i:
                            for h in range(2):
                                pool.wait_ge(s_idx[h], i + 1)
                                pool.sem_inc(s_begun, 1)
                                for k in range(h * HALF, (h + 1) * HALF):
                                    pool.indirect_dma_start(
                                        out=rows[:, k, 0:D], out_offset=None, in_=rows_d,
                                        in_offset=bass.IndirectOffsetOnAxis(ap=idx[:, k:k + 1], axis=0),
                                    ).then_inc(ring_a[k], 16)

                    @block.vector
                    def _(dve):
                        dve.sem_inc(s_acc[0], 1)
                        dve.sem_inc(s_acc[1], 1)
                        nc.vector.memset(rows[:, :, D:RW], 1.0).then_inc(s_one, 1)
                        nc.vector.memset(acc[:, :], 0.0)

                        def add(h, i, bkt):
                            dve.drain()
                            dve.wait_ge(s_mm[h], i + 1 + 1)
                            for q in range(PAIRS):
                                b = nc.s_assert_within(bkt[q], 0, NT - 1, skip_runtime_bounds_check_because="a pair's bucket is one of NT")
                                to = acc[:, bass.ds(b * RW, RW)]
                                if q:
                                    dve.drain()
                                last = nc.vector.tensor_tensor(to, to, ps[:, h * PAIRS + q, 0:RW], ALU.add)
                            last.then_inc(s_acc[h], 1)

                        with dve.Fori(0, ITERS) as i:
                            word = [dve.value_load(slot_bkt[0:1, bass.ds(i * 2 + h, 1)], min_val=0, max_val=(1 << 20) - 1)
                                    for h in range(2)]
                            for h in range(2):
                                at = i * (2 * HALF) + h * HALF
                                dve.wait_ge(s_mm[h], i + 1)
                                nc.vector.tensor_copy(drel[:, h * HALF:(h + 1) * HALF], slot_dst[:, bass.ds(at, HALF)])
                                dve.drain()
                                for k in range(h * HALF, (h + 1) * HALF):
                                    last = nc.vector.tensor_scalar(hot[:, k, :], iota[:, :], drel[:, k:k + 1], None, ALU.is_equal)
                                last.then_inc(s_hot[h], 1)
                            for h in range(2):
                                w = word[h]
                                add(h, i, [w % 32, (w // 32) % 32, (w // 1024) % 32, w // 32768])

                    @block.tensor
                    def _(pe):
                        pe.sem_inc(s_mm[0], 1)
                        pe.sem_inc(s_mm[1], 1)
                        pe.wait_ge(s_one, 1)
                        with pe.Fori(0, ITERS) as i:
                            for h in range(2):
                                pe.wait_ge(s_hot[h], i + 1)
                                pe.wait_ge(s_acc[h], i + 1)
                                for k in range(HALF):
                                    pe.wait_ge(ring_a[h * HALF + k], i * 16 + (base + 16))
                                    last = nc.tensor.matmul(ps[:, h * PAIRS + k // GROUP, 0:RW], hot[:, h * HALF + k, :],
                                                            rows[:, h * HALF + k, :], start=(k % GROUP == 0),
                                                            stop=(k % GROUP == GROUP - 1))
                                last.then_inc(s_mm[h], 1)

        def stage_gin(acc):
            accv = acc[:, :].rearrange("p (t d) -> p t d", d=RW)
            tmp = ExitStack()

            def t(name, shape, dt=f32):
                return tmp.enter_context(nc.sbuf_tensor(name, shape, dt))

            with tmp:
                w1 = t("gin_w1", [P, KD, F])
                w2 = t("gin_w2", [P, KF, D])
                vec1 = t("gin_vec1", [P, 3, KF])
                vec2 = t("gin_vec2", [P, 3, KD])
                eps1 = t("gin_eps1", [P, 1])
                deg = t("deg", [P, NT])
                stage = t("gin_stage", [P, 2, GT * D])
                stz = stage[:, 0, :].rearrange("p (t d) -> p t d", d=D)
                sth = stage[:, 1, :].rearrange("p (t d) -> p t d", d=D)
                ZT = t("gin_zt", [P, KD, NP])
                HT = t("gin_ht", [P, KD, NP])
                s_w, s_deg, s_z = sem("gin_weights"), sem("gin_deg"), sem("gin_z")
                s_zt, s_zc, s_hc = sem("gin_transposed"), sem("gin_zt_copied"), sem("gin_ht_copied")
                s_step = sem("gin_step")
                with nc.psum_tensor("gin_pst", [P, KD, GN], f32) as pz, nc.psum_tensor("gin_psh", [P, KD, GN], f32) as ph, \
                        nc.Block() as block:
                    @block.sync
                    def _(sp):
                        with nc.allow_non_contiguous_dma(reason="small vectors by feature"):
                            sp.dma_start(eps1[:, :], a["L0_gnn_eps_gin"].partition_broadcast(P)).then_inc(s_w, 16)
                            for k, v in enumerate(("b1", "g1", "bt1")):
                                sp.dma_start(vec1[:, k, :], a["L0_gnn_" + v].rearrange("(c p) -> p c", p=P)).then_inc(s_w, 16)
                            for k, v in enumerate(("b2", "g2", "bt2")):
                                sp.dma_start(vec2[:, k, :], a["L0_gnn_" + v].rearrange("(c p) -> p c", p=P)).then_inc(s_w, 16)
                        sp.dma_start(w1[:, :, :], a["L0_gnn_W1"].rearrange("(c p) f -> p c f", p=P)).then_inc(s_w, 16)
                        sp.dma_start(w2[:, :, :], a["L0_gnn_W2"].rearrange("(c p) f -> p c f", p=P)).then_inc(s_w, 16)

                    @block.vector
                    def _(dve):
                        dve.sem_inc(s_zc, 1)
                        step = Chain(dve, s_step)
                        step(nc.vector.tensor_scalar(deg[:, :], accv[:, :, D], 1.0, None, ALU.max))
                        nc.vector.reciprocal(deg[:, :], deg[:, :]).then_inc(s_deg, 1)
                        dve.wait_ge(s_w, 16 * 9)
                        step(nc.vector.tensor_scalar(eps1[:, :], eps1[:, :], 1.0, None, ALU.add))
                        with dve.Fori(0, NG) as g:
                            dve.wait_ge(s_zt, g + 1)
                            tl = bass.ds(g * GT, GT)
                            nc.vector.tensor_copy(sth[:, :, :], H[:, tl, :])
                            nc.vector.scalar_tensor_tensor(stz, H[:, tl, :], eps1[:, 0:1], accv[:, tl, 0:D],
                                                           ALU.mult, ALU.add).then_inc(s_z, 1)
                            dve.wait_ge(s_zt, g + 1 + 1)
                            nc.vector.tensor_copy(ZT[:, :, bass.ds(g * GN, GN)], pz[:, :, :]).then_inc(s_zc, 1)

                    @block.tensor
                    def _(pe):
                        pe.sem_inc(s_zt, 1)
                        with pe.Fori(0, NG) as g:
                            pe.wait_ge(s_z, g + 1)
                            pe.wait_ge(s_zc, g + 1)
                            pe.wait_ge(s_hc, g + 1)
                            for k in range(GT):
                                for c in range(KD):
                                    nc.tensor.transpose(pz[:, c, k * P:(k + 1) * P], stz[:, k, c * P:(c + 1) * P], ident[:, :])
                                    last = nc.tensor.transpose(ph[:, c, k * P:(k + 1) * P], sth[:, k, c * P:(c + 1) * P], ident[:, :])
                            last.then_inc(s_zt, 1)

                    @block.scalar
                    def _(act):
                        act.sem_inc(s_hc, 1)
                        act.wait_ge(s_deg, 1)
                        nc.scalar.activation(norm[:, :], deg[:, :], ACT.Sqrt)
                        with act.Fori(0, NG) as g:
                            act.wait_ge(s_zt, g + 1 + 1)
                            nc.scalar.copy(HT[:, :, bass.ds(g * GN, GN)], ph[:, :, :]).then_inc(s_hc, 1)

                TT = t("gin_tt", [P, KF, N])
                st1 = t("gin_st1", [P, KF, NCH + 1, 6])
                st2 = t("gin_st2", [P, KD, NCH + 1, 6])
                mv1 = t("gin_mv1", [P, KF, 2])
                mv2 = t("gin_mv2", [P, KD, 2])
                sc1 = t("gin_sc1", [P, 2, KF])
                sc2 = t("gin_sc2", [P, 2, KD])

                def bn_coefficients(dve, st, mv, sc, vec, s_var, s_sd, s_ready):
                    for m in range(mv.shape[1]):
                        nc.vector.bn_aggr(mv[:, m, :], st[:, m, :, :].rearrange("p a b -> p (a b)"))
                    dve.drain()
                    nc.vector.tensor_scalar(mv[:, :, 1], mv[:, :, 1], EPS, None, ALU.add).then_inc(s_var, 1)
                    dve.wait_ge(s_sd, 1)
                    nc.vector.reciprocal(sc[:, 1, :], sc[:, 0, :])
                    dve.drain()
                    nc.vector.tensor_tensor(sc[:, 0, :], sc[:, 1, :], vec[:, 1, :], ALU.mult)
                    dve.drain()
                    nc.vector.tensor_tensor(sc[:, 1, :], mv[:, :, 0], sc[:, 0, :], ALU.mult)
                    dve.drain()
                    nc.vector.tensor_tensor(sc[:, 1, :], vec[:, 2, :], sc[:, 1, :], ALU.subtract).then_inc(s_ready, 1)

                s_mm, s_ev, s_st = sem("gin_t_made"), sem("gin_t_copied"), sem("gin_t_stats")
                s_va, s_sd, s_sc = sem("gin_var1"), sem("gin_sd1"), sem("gin_scale1")
                with nc.psum_tensor("gin_ps1", [P, 2, KF, CH], f32) as ps, nc.Block() as block:
                    @block.tensor
                    def _(pe):
                        def chunk(b, lo, n, count):
                            pe.wait_ge(s_ev, count + 1)
                            for m in range(KF):
                                for c in range(KD):
                                    last = nc.tensor.matmul(ps[:, b, m, 0:n], w1[:, c, m * P:(m + 1) * P],
                                                            ZT[:, c, bass.ds(lo, n)], start=(c == 0), stop=(c == KD - 1))
                            last.then_inc(s_mm, 1)
                        with pe.Fori(0, NCH // 2) as i:
                            for b in range(2):
                                chunk(b, i * (2 * CH) + b * CH, CH, i * (2 * KF))
                        chunk(0, NCH * CH, CTAIL, (NCH - 1) * KF)

                    @block.scalar
                    def _(act):
                        act.sem_inc(s_ev, 1)
                        def chunk(b, lo, n, count):
                            act.wait_ge(s_mm, count)
                            for m in range(KF):
                                nc.scalar.activation(TT[:, m, bass.ds(lo, n)], ps[:, b, m, 0:n], ACT.Identity,
                                                     bias=vec1[:, 0, m:m + 1]).then_inc(s_ev, 1)
                        with act.Fori(0, NCH // 2) as i:
                            for b in range(2):
                                chunk(b, i * (2 * CH) + b * CH, CH, i * 2 + b + 1)
                        chunk(0, NCH * CH, CTAIL, NCH + 1)
                        act.wait_ge(s_va, 1)
                        nc.scalar.activation(sc1[:, 0, :], mv1[:, :, 1], ACT.Sqrt).then_inc(s_sd, 1)

                    @block.vector
                    def _(dve):
                        def chunk(j, lo, n, count):
                            for m in range(KF):
                                dve.wait_ge(s_ev, count + m + 1 + 1)
                                o = st1[:, m, j, :] if isinstance(j, int) else st1[:, m, bass.ds(j, 1), :].rearrange("p a b -> p (a b)")
                                nc.vector.bn_stats(o, TT[:, m, bass.ds(lo, n)])
                        with dve.Fori(0, NCH) as i:
                            chunk(i, i * CH, CH, i * KF)
                        chunk(NCH, NCH * CH, CTAIL, NCH * KF)
                        dve.drain()
                        bn_coefficients(dve, st1, mv1, sc1, vec1, s_va, s_sd, s_sc)

                s_rl, s_cv, s_cc = sem("gin_relu"), sem("gin_c_made"), sem("gin_c_copied")
                s_va2, s_sd2, s_sc2 = sem("gin_var2"), sem("gin_sd2"), sem("gin_scale2")
                with nc.psum_tensor("gin_ps2", [P, 2, KD, CH], f32) as ps, nc.Block() as block:
                    @block.scalar
                    def _(act):
                        def chunk(lo, n):
                            for m in range(KF):
                                nc.scalar.activation(TT[:, m, bass.ds(lo, n)], TT[:, m, bass.ds(lo, n)], ACT.Relu,
                                                     bias=sc1[:, 1, m:m + 1], scale=sc1[:, 0, m:m + 1]).then_inc(s_rl, 1)
                        with act.Fori(0, NCH) as i:
                            chunk(i * CH, CH)
                        chunk(NCH * CH, CTAIL)
                        act.wait_ge(s_va2, 1)
                        nc.scalar.activation(sc2[:, 0, :], mv2[:, :, 1], ACT.Sqrt).then_inc(s_sd2, 1)

                    @block.tensor
                    def _(pe):
                        def chunk(b, lo, n, r, c0):
                            pe.wait_ge(s_rl, r)
                            pe.wait_ge(s_cc, c0 + 1)
                            for m in range(KD):
                                for c in range(KF):
                                    last = nc.tensor.matmul(ps[:, b, m, 0:n], w2[:, c, m * P:(m + 1) * P],
                                                            TT[:, c, bass.ds(lo, n)], start=(c == 0), stop=(c == KF - 1))
                            last.then_inc(s_cv, 1)
                        with pe.Fori(0, NCH // 2) as i:
                            for b in range(2):
                                chunk(b, i * (2 * CH) + b * CH, CH, i * (2 * KF) + (b + 1) * KF, i * (2 * KD))
                        chunk(0, NCH * CH, CTAIL, (NCH + 1) * KF, (NCH - 1) * KD)

                    @block.vector
                    def _(dve):
                        dve.sem_inc(s_cc, 1)
                        nc.vector.memset(ZT[:, :, N:NP], 0.0)

                        def chunk(b, j, lo, n, count):
                            dve.wait_ge(s_cv, count)
                            for m in range(KD):
                                nc.vector.scalar_tensor_tensor(
                                    ZT[:, m, bass.ds(lo, n)], ps[:, b, m, 0:n], vec2[:, 0, m:m + 1],
                                    HT[:, m, bass.ds(lo, n)], ALU.add, ALU.add).then_inc(s_cc, 1)
                            dve.drain()
                            for m in range(KD):
                                o = st2[:, m, j, :] if isinstance(j, int) else st2[:, m, bass.ds(j, 1), :].rearrange("p a b -> p (a b)")
                                nc.vector.bn_stats(o, ZT[:, m, bass.ds(lo, n)])
                        with dve.Fori(0, NCH // 2) as i:
                            for b in range(2):
                                chunk(b, i * 2 + b, i * (2 * CH) + b * CH, CH, i * 2 + b + 1)
                        chunk(0, NCH, NCH * CH, CTAIL, NCH + 1)
                        dve.drain()
                        bn_coefficients(dve, st2, mv2, sc2, vec2, s_va2, s_sd2, s_sc2)

                s_r2, s_xt, s_xa = sem("gin_relu2"), sem("gin_back"), sem("gin_x_added")
                stc = stage[:, :, :].rearrange("p b (c n) -> p b c n", n=GN)
                with nc.psum_tensor("gin_ps3", [P, GT, D], f32) as ps, nc.Block() as block:
                    @block.scalar
                    def _(act):
                        def group(b, g):
                            for m in range(KD):
                                last = nc.scalar.activation(stc[:, b, m, :], ZT[:, m, bass.ds(g * GN, GN)], ACT.Relu,
                                                            bias=sc2[:, 1, m:m + 1], scale=sc2[:, 0, m:m + 1])
                            last.then_inc(s_r2, 1)
                        group(0, 0)
                        group(1, 1)
                        with act.Fori(0, NG // 2) as i:
                            act.wait_ge(s_xt, 2 * i + 1)
                            group(0, 2 * i + 2)
                            act.wait_ge(s_xt, 2 * i + 2)
                            group(1, (2 * i + 3) % NG)

                    @block.tensor
                    def _(pe):
                        def group(b, g):
                            pe.wait_ge(s_r2, g + 1)
                            pe.wait_ge(s_xa, g + 1)
                            for k in range(GT):
                                for c in range(KD):
                                    last = nc.tensor.transpose(ps[:, k, c * P:(c + 1) * P], stc[:, b, c, k * P:(k + 1) * P], ident[:, :])
                            last.then_inc(s_xt, 1)
                        group(0, 0)
                        with pe.Fori(0, NG // 2) as i:
                            group(1, 2 * i + 1)
                            group(0, 2 * i + 2)

                    @block.vector
                    def _(dve):
                        dve.sem_inc(s_xa, 1)
                        with dve.Fori(0, NG) as g:
                            dve.wait_ge(s_xt, g + 1)
                            xs = X[:, bass.ds(g * GT, GT), :]
                            nc.vector.tensor_tensor(xs, xs, ps[:, :, :], ALU.add).then_inc(s_xa, 1)

        def stage_gat():
            tmp = ExitStack()

            def t(name, shape, dt=f32):
                return tmp.enter_context(nc.sbuf_tensor(name, shape, dt))

            with tmp:
                wg = t("gat_w", [P, KD, HK])
                rowv = t("gat_rows", [P, 5, HK])
                HT = t("gat_ht", [P, KD, NP])
                TS = t("gat_ts", [P, NT, TW])
                TD = t("gat_td", [P, NT, DW])
                prod = t("gat_prod", [P, NT, HK])
                gmax = t("gat_gmax", [P, HEADS])
                gall = t("gat_gall", [P, HEADS])
                e_s = t("gat_es", [P, NT, HEADS])
                self_e = t("gat_self", [P, NT, HEADS])
                es_i = t("gat_es_i", [P, ET2], i32)
                ed_i = t("gat_ed_i", [P, ET2], i32)
                lo_i = t("gat_lo_i", [P, ET2], i32)
                lo_f = t("gat_lo_f", [P, ET2])
                hi_f = t("gat_hi_f", [P, ET2])
                sth = t("gat_sth", [P, GT, D])
                stt = t("gat_stt", [P, KD, GN])
                s_w, s_e = sem("gat_weights"), sem("gat_edges")
                s_h, s_t, s_c, s_c2 = sem("gat_h"), sem("gat_t"), sem("gat_ht_copied"), sem("gat_stage_copied")
                s_hh, s_hc = sem("gat_hh_made"), sem("gat_hh_copied")
                s_m, s_g, s_tab, s_st = sem("gat_max"), sem("gat_gmax"), sem("gat_tables"), sem("gat_step")
                s_out, s_ex = sem("gat_tables_out"), sem("gat_exp")
                with nc.psum_tensor("gat_pst", [P, KD, GN], f32) as pt, nc.psum_tensor("gat_psh", [P, GT, HK], f32) as ph, \
                        nc.Block() as block:
                    @block.sync
                    def _(sp):
                        sp.dma_start(wg[:, :, :], a["L0_ffn_W_gat"].rearrange("(c p) f -> p c f", p=P)).then_inc(s_w, 16)
                        for k, v in enumerate(("att_src", "att_dst")):
                            sp.dma_start(rowv[:, k, :], a["L0_ffn_" + v].rearrange("h k -> (h k)").partition_broadcast(P)).then_inc(s_w, 16)
                        for k, v in enumerate(("b_gat", "ln_gamma", "ln_beta")):
                            sp.dma_start(rowv[:, 2 + k, :], a["L0_ffn_" + v].partition_broadcast(P)).then_inc(s_w, 16)
                        for dst, k in ((es_i, 0), (ed_i, 1)):
                            sp.dma_start(dst[:, :], a["L0_ffn_edge_index"][k, :].rearrange("(p t) -> p t", p=P)).then_inc(s_e, 16)
                        sp.wait_ge(s_tab, 1)
                        sp.dma_start(srct_d.rearrange("(t p) k -> p t k", p=P), TS[:, :, :]).then_inc(s_out, 16)
                        sp.dma_start(dstt_d.rearrange("(t p) k -> p t k", p=P), TD[:, :, :]).then_inc(s_out, 16)
                        sp.wait_ge(s_out, 32)

                    @block.vector
                    def _(dve):
                        dve.sem_inc(s_c, 1)
                        dve.sem_inc(s_hc, 1)
                        V = nc.vector
                        with dve.Fori(0, NG) as g:
                            dve.wait_ge(s_t, g + 1)
                            V.tensor_copy(sth[:, :, :], H[:, bass.ds(g * GT, GT), :]).then_inc(s_h, 1)
                            dve.wait_ge(s_c2, g + 1 + 1)
                            V.tensor_copy(HT[:, :, bass.ds(g * GN, GN)], stt[:, :, :]).then_inc(s_c, 1)
                            dve.wait_ge(s_hh, g + 1 + 1)
                            V.tensor_copy(TS[:, bass.ds(g * GT, GT), HEADS:TW], ph[:, :, :]).then_inc(s_hc, 1)
                        step = Chain(dve, s_st)
                        dve.wait_ge(s_w, 16 * 6)
                        hv = TS[:, :, HEADS:TW]
                        for k, to in ((0, TS[:, :, 0:HEADS]), (1, TD[:, :, 0:HEADS])):
                            dve.drain()
                            step(V.tensor_tensor(prod[:, :, :], hv, rowv[:, k, :].unsqueeze(1).to_broadcast([P, NT, HK]), ALU.mult))
                            step(V.tensor_reduce(to, prod[:, :, :].rearrange("p t (h k) -> p t h k", k=NE), AX.X, ALU.add))
                        a_s, a_d, shift = TS[:, :, 0:HEADS], TD[:, :, 0:HEADS], TD[:, :, HEADS:DW]
                        V.tensor_reduce(gmax[:, :], a_s.rearrange("p t h -> p h t"), AX.X, ALU.max).then_inc(s_m, 1)
                        step(V.tensor_tensor(e_s[:, :, :], a_s, a_d, ALU.add))
                        step(V.scalar_tensor_tensor(e_s[:, :, :], e_s[:, :, :], 0.2, e_s[:, :, :], ALU.mult, ALU.max))
                        dve.wait_ge(s_g, 1)
                        step(V.tensor_tensor(self_e[:, :, :], a_d, gall[:, :].unsqueeze(1).to_broadcast([P, NT, HEADS]), ALU.add))
                        step(V.scalar_tensor_tensor(self_e[:, :, :], self_e[:, :, :], 0.2, self_e[:, :, :], ALU.mult, ALU.max))
                        step(V.tensor_scalar(self_e[:, :, :], self_e[:, :, :], -60.0, None, ALU.add))
                        step(V.tensor_tensor(shift, self_e[:, :, :], e_s[:, :, :], ALU.max))
                        step(V.tensor_tensor(e_s[:, :, :], e_s[:, :, :], shift, ALU.subtract))
                        V.tensor_copy(gmax[:, :], gall[:, :]).then_inc(s_tab, 1)
                        dve.wait_ge(s_e, 32)
                        step(V.tensor_scalar(lo_i[:, :], ed_i[:, :], P - 1, None, ALU.bitwise_and))
                        step(V.tensor_copy(lo_f[:, :], lo_i[:, :]))
                        step(V.tensor_scalar(lo_i[:, :], ed_i[:, :], 7, None, ALU.logical_shift_right))
                        step(V.tensor_copy(hi_f[:, :], lo_i[:, :]))

                    @block.gpsimd
                    def _(pool):
                        pool.wait_ge(s_m, 1)
                        nc.gpsimd.partition_all_reduce(gall[:, :], gmax[:, :], P, bass.bass_isa.ReduceOp.max).then_inc(s_g, 1)

                    @block.scalar
                    def _(act):
                        act.sem_inc(s_c2, 1)
                        with act.Fori(0, NG) as g:
                            act.wait_ge(s_t, g + 1 + 1)
                            act.wait_ge(s_hh, g + 1)
                            act.wait_ge(s_c, g + 1)
                            nc.scalar.copy(stt[:, :, :], pt[:, :, :]).then_inc(s_c2, 1)
                        act.wait_ge(s_tab, 1)
                        nc.scalar.activation(self_e[:, :, :], e_s[:, :, :], ACT.Exp).then_inc(s_ex, 1)

                    @block.tensor
                    def _(pe):
                        pe.sem_inc(s_t, 1)
                        pe.sem_inc(s_hh, 1)
                        pe.wait_ge(s_w, 16 * 6)
                        with pe.Fori(0, NG) as g:
                            pe.wait_ge(s_h, g + 1)
                            pe.wait_ge(s_c2, g + 1)
                            pe.wait_ge(s_hc, g + 1)
                            for k in range(GT):
                                for c in range(KD):
                                    last = nc.tensor.transpose(pt[:, c, k * P:(k + 1) * P], sth[:, k, c * P:(c + 1) * P], ident[:, :])
                            last.then_inc(s_t, 1)
                            pe.wait_ge(s_c2, g + 1 + 1)
                            for k in range(GT):
                                for c in range(KD):
                                    last = nc.tensor.matmul(ph[:, k, :], stt[:, c, k * P:(k + 1) * P], wg[:, c, :],
                                                            start=(c == 0), stop=(c == KD - 1))
                            last.then_inc(s_hh, 1)

                experts0(HT)

                gs = t("gat_gs", [P, 2 * HALF, TW])
                gd = t("gat_gd", [P, 2 * HALF, DW])
                ix = t("gat_ix", [P, 2, 2 * HALF], i32)
                lh = t("gat_lh", [P, 2, 2 * HALF])
                ev = t("gat_ev", [P, 2 * HALF, HEADS])
                msg = t("gat_msg", [P, 2 * HALF, TW])
                hot = t("gat_hot", [P, 2 * HALF, P])
                hih = t("gat_hih", [P, 2 * HALF, NT])
                mov = t("gat_mov", [P, 2 * HALF, NT * TW])
                sums = t("gat_sums", [P, NT, TW])
                IT2 = ET2 // (2 * HALF)
                s_ix = [sem("gat_ix_a"), sem("gat_ix_b")]
                base_a, base_b = done["a"], done["b"]
                done["a"] += 16 * IT2
                done["b"] += 16 * IT2
                s_ev = [sem("gat_score_a"), sem("gat_score_b")]
                s_ee = [sem("gat_weight_a"), sem("gat_weight_b")]
                s_mv = [sem("gat_moving_a"), sem("gat_moving_b")]
                s_mm = [sem("gat_summed_a"), sem("gat_summed_b")]
                s_begun = sem("gat_begun")
                s_z, s_fin = sem("gat_zero"), sem("gat_all_summed")
                with nc.psum_tensor("gat_acc", [P, NT * TW], f32) as ps, nc.Block() as block:
                    @block.scalar
                    def _(act):
                        def stage(h, at):
                            r = slice(h * HALF, (h + 1) * HALF)
                            nc.scalar.copy(ix[:, 0, r], es_i[:, bass.ds(at, HALF)])
                            nc.scalar.copy(ix[:, 1, r], ed_i[:, bass.ds(at, HALF)]).then_inc(s_ix[h], 1)
                        for h in range(2):
                            stage(h, h * HALF)
                        with act.Fori(0, IT2) as i:
                            for h in range(2):
                                r = slice(h * HALF, (h + 1) * HALF)
                                act.wait_ge(s_ev[h], i + 1)
                                nc.scalar.activation(msg[:, r, HK:TW], ev[:, r, :], ACT.Exp).then_inc(s_ee[h], 1)
                            for h in range(2):
                                act.wait_ge(s_mm[h], i + 1 + 1)
                                r = slice(h * HALF, (h + 1) * HALF)
                                at = bass.ds(((i + 1) % IT2) * (2 * HALF) + h * HALF, HALF)
                                nc.scalar.copy(ix[:, 0, r], es_i[:, at])
                                nc.scalar.copy(ix[:, 1, r], ed_i[:, at]).then_inc(s_ix[h], 1)

                    @block.gpsimd
                    def _(pool):
                        with pool.Fori(0, IT2) as i:
                            for h in range(2):
                                pool.wait_ge(s_ix[h], i + 1)
                                pool.sem_inc(s_begun, 1)
                                for k in range(h * HALF, (h + 1) * HALF):
                                    pool.indirect_dma_start(
                                        out=gs[:, k, :], out_offset=None, in_=srct_d,
                                        in_offset=bass.IndirectOffsetOnAxis(ap=ix[:, 0, k:k + 1], axis=0)).then_inc(ring_a[k], 16)
                                    pool.indirect_dma_start(
                                        out=gd[:, k, :], out_offset=None, in_=dstt_d,
                                        in_offset=bass.IndirectOffsetOnAxis(ap=ix[:, 1, k:k + 1], axis=0)).then_inc(ring_b[k], 16)

                    @block.vector
                    def _(dve):
                        V = nc.vector
                        V.memset(sums[:, :, :], 0.0).then_inc(s_z, 1)
                        with dve.Fori(0, IT2) as i:
                            for h in range(2):
                                r = slice(h * HALF, (h + 1) * HALF)
                                at = bass.ds(i * (2 * HALF) + h * HALF, HALF)
                                dve.wait_ge(s_mm[h], i + 1)
                                V.tensor_copy(lh[:, 0, r], lo_f[:, at])
                                V.tensor_copy(lh[:, 1, r], hi_f[:, at])
                                dve.drain()
                                for k in range(h * HALF, (h + 1) * HALF):
                                    V.tensor_scalar(hot[:, k, :], iota[:, :], lh[:, 0, k:k + 1], None, ALU.is_equal)
                                V.tensor_tensor(hih[:, r, :], iota[:, 0:NT].unsqueeze(1).to_broadcast([P, HALF, NT]),
                                                lh[:, 1, r].unsqueeze(2).to_broadcast([P, HALF, NT]), ALU.is_equal)
                                for k in range(h * HALF, (h + 1) * HALF):
                                    dve.wait_ge(ring_a[k], i * 16 + (base_a + 16))
                                    dve.wait_ge(ring_b[k], i * 16 + (base_b + 16))
                                V.tensor_tensor(ev[:, r, :], gs[:, r, 0:HEADS], gd[:, r, 0:HEADS], ALU.add)
                                dve.drain()
                                V.scalar_tensor_tensor(ev[:, r, :], ev[:, r, :], 0.2, ev[:, r, :], ALU.mult, ALU.max)
                                dve.drain()
                                V.tensor_tensor(ev[:, r, :], ev[:, r, :], gd[:, r, HEADS:DW], ALU.subtract).then_inc(s_ev[h], 1)
                                dve.wait_ge(s_ee[h], i + 1)
                                V.tensor_tensor(
                                    msg[:, r, 0:HK].rearrange("p t (h k) -> p t h k", k=NE),
                                    gs[:, r, HEADS:TW].rearrange("p t (h k) -> p t h k", k=NE),
                                    msg[:, r, HK:TW].unsqueeze(3).to_broadcast([P, HALF, HEADS, NE]), ALU.mult)
                                dve.drain()
                                for k in range(h * HALF, (h + 1) * HALF):
                                    last = V.tensor_tensor(
                                        mov[:, k, :].rearrange("p (t w) -> p t w", w=TW),
                                        msg[:, k, :].unsqueeze(1).to_broadcast([P, NT, TW]),
                                        hih[:, k, :].unsqueeze(2).to_broadcast([P, NT, TW]), ALU.mult)
                                last.then_inc(s_mv[h], 1)
                        dve.wait_ge(s_fin, 1)
                        V.tensor_copy(sums[:, :, :].rearrange("p t w -> p (t w)"), ps[:, :])

                    @block.tensor
                    def _(pe):
                        pe.sem_inc(s_mm[0], 1)
                        pe.sem_inc(s_mm[1], 1)
                        pe.wait_ge(s_z, 1)
                        nc.tensor.matmul(ps[:, :], ident[:, :], sums[:, :, :].rearrange("p t w -> p (t w)"),
                                         start=True, stop=False, skip_group_check=True)
                        with pe.Fori(0, IT2) as i:
                            for h in range(2):
                                pe.wait_ge(s_mv[h], i + 1)
                                for k in range(h * HALF, (h + 1) * HALF):
                                    last = nc.tensor.matmul(ps[:, :], hot[:, k, :], mov[:, k, :], start=False,
                                                            stop=False, skip_group_check=True)
                                last.then_inc(s_mm[h], 1)
                        nc.tensor.matmul(ps[:, :], ident[:, :], sums[:, :, :].rearrange("p t w -> p (t w)"),
                                         start=False, stop=True, skip_group_check=True).then_inc(s_fin, 1)

                agg = t("gat_agg", [P, NT, HK])
                den = t("gat_den", [P, NT, HEADS])
                s1 = t("gat_s1", [P, NT, 1])
                sc = t("gat_sc", [P, NT, NE])
                rank = t("gat_rank", [P, NT, NE])
                cmp_ = t("gat_cmp", [P, NT])
                gate = t("gat_gate", [P, NT, NE])
                b2row = t("gat_b2row", [P, NE, D])
                yst = t("gat_yst", [P, 2, GT * D])
                s_k, s_sq, s_q, s_ex2, s_b2 = sem("mix_step"), sem("mix_var"), sem("mix_std"), sem("mix_exp"), sem("mix_b2")
                s_e2, s_gate = sem("mix_score"), sem("mix_gate")
                s_y = [sem("mix_y_a"), sem("mix_y_b")]
                s_yu = sem("mix_y_used")
                with nc.Block() as block:
                    @block.vector
                    def _(dve):
                        dve.sem_inc(s_yu, 1)
                        V = nc.vector
                        step = Chain(dve, s_k)
                        b4 = lambda ap: ap.unsqueeze(3).to_broadcast([P, NT, HEADS, NE])
                        v4 = lambda ap: ap.rearrange("p t (h k) -> p t h k", k=NE)
                        rb = lambda k: rowv[:, k, :].unsqueeze(1).to_broadcast([P, NT, HK])
                        nb = lambda ap, w: ap.to_broadcast([P, NT, w])
                        step(V.tensor_tensor(v4(agg[:, :, :]), v4(TS[:, :, HEADS:TW]), b4(self_e[:, :, :]), ALU.mult))
                        step(V.tensor_tensor(agg[:, :, :], agg[:, :, :], sums[:, :, 0:HK], ALU.add))
                        step(V.tensor_tensor(den[:, :, :], sums[:, :, HK:TW], self_e[:, :, :], ALU.add))
                        step(V.tensor_scalar(den[:, :, :], den[:, :, :], 1e-16, None, ALU.add))
                        step(V.reciprocal(den[:, :, :], den[:, :, :]))
                        step(V.tensor_tensor(v4(agg[:, :, :]), v4(agg[:, :, :]), b4(den[:, :, :]), ALU.mult))
                        step(V.tensor_tensor(agg[:, :, :], agg[:, :, :], rb(2), ALU.add))
                        step(V.tensor_reduce(s1[:, :, 0], agg[:, :, :], AX.X, ALU.add))
                        step(V.tensor_scalar(s1[:, :, :], s1[:, :, :], 1.0 / HK, None, ALU.mult))
                        step(V.tensor_tensor(agg[:, :, :], agg[:, :, :], nb(s1[:, :, :], HK), ALU.subtract))
                        step(V.tensor_tensor(prod[:, :, :], agg[:, :, :], agg[:, :, :], ALU.mult))
                        step(V.tensor_reduce(s1[:, :, 0], prod[:, :, :], AX.X, ALU.add))
                        V.tensor_scalar(s1[:, :, :], s1[:, :, :], 1.0 / HK, EPS, ALU.mult, ALU.add).then_inc(s_sq, 1)
                        dve.wait_ge(s_q, 1)
                        step(V.reciprocal(s1[:, :, :], s1[:, :, :]))
                        step(V.tensor_tensor(agg[:, :, :], agg[:, :, :], nb(s1[:, :, :], HK), ALU.mult))
                        step(V.tensor_tensor(agg[:, :, :], agg[:, :, :], rb(3), ALU.mult))
                        step(V.tensor_tensor(agg[:, :, :], agg[:, :, :], rb(4), ALU.add))
                        step(V.tensor_reduce(sc[:, :, :], agg[:, :, :].rearrange("p t (h k) -> p t k h", k=NE), AX.X, ALU.add))
                        step(V.tensor_scalar(sc[:, :, :], sc[:, :, :], 1.0 / HEADS, None, ALU.mult))
                        step(V.memset(rank[:, :, :], 0.0))
                        for i in range(NE):
                            for j in range(NE):
                                if i != j:
                                    op = ALU.is_ge if j < i else ALU.is_gt
                                    step(V.tensor_tensor(cmp_[:, :], sc[:, :, j], sc[:, :, i], op))
                                    step(V.tensor_tensor(rank[:, :, i], rank[:, :, i], cmp_[:, :], ALU.add))
                        step(V.tensor_reduce(s1[:, :, 0], sc[:, :, :], AX.X, ALU.max))
                        V.tensor_tensor(sc[:, :, :], sc[:, :, :], nb(s1[:, :, :], NE), ALU.subtract).then_inc(s_e2, 1)
                        step(V.tensor_scalar(rank[:, :, :], rank[:, :, :], 1.5, None, ALU.is_lt))
                        dve.wait_ge(s_ex2, 1)
                        step(V.tensor_tensor(gate[:, :, :], gate[:, :, :], rank[:, :, :], ALU.mult))
                        step(V.tensor_reduce(s1[:, :, 0], gate[:, :, :], AX.X, ALU.add))
                        step(V.reciprocal(s1[:, :, :], s1[:, :, :]))
                        step(V.tensor_tensor(gate[:, :, :], gate[:, :, :], nb(s1[:, :, :], NE), ALU.mult))
                        dve.drain()
                        for e in range(NE):
                            with dve.Fori(0, NG) as g:
                                b = 0
                                dve.wait_ge(s_y[b], g * 16 + (e * NG + 1) * 16)
                                for k in range(GT):
                                    i = g * GT + k
                                    xs = X[:, bass.ds(i, 1), :].rearrange("p a b -> p (a b)")
                                    last = V.scalar_tensor_tensor(
                                        xs, yst[:, b, k * D:(k + 1) * D],
                                        gate[:, bass.ds(i, 1), e], xs, ALU.mult, ALU.add)
                                last.then_inc(s_yu, 1)
                                dve.drain()

                    @block.scalar
                    def _(act):
                        act.wait_ge(s_sq, 1)
                        nc.scalar.activation(s1[:, :, :], s1[:, :, :], ACT.Sqrt).then_inc(s_q, 1)
                        act.wait_ge(s_e2, 1)
                        nc.scalar.activation(gate[:, :, :], sc[:, :, :], ACT.Exp).then_inc(s_ex2, 1)

                    @block.sync
                    def _(sp):
                        for e in range(NE):
                            with sp.Fori(0, NG) as g:
                                sp.wait_ge(s_yu, g + (e * NG + 1))
                                sp.dma_start(yst[:, 0, :], y_d[e, :, bass.ds(g * (GT * D), GT * D)]).then_inc(s_y[0], 16)

        def experts0(HT):
            tmp = ExitStack()

            def t(name, shape, dt=f32):
                return tmp.enter_context(nc.sbuf_tensor(name, shape, dt))

            with tmp:
                w1 = t("ex_w1", [P, KD, NE, F])
                w2 = t("ex_w2", [P, KF, NE, D])
                b1 = t("ex_b1", [P, NE, KF])
                b2 = t("ex_b2", [P, NE, D])
                hh = t("ex_hh", [P, KF, GN])
                yo = t("ex_yo", [P, 2, GT * D])
                HN = GN // 2
                s_w, s_a, s_g, s_y = sem("ex_weights"), sem("ex_hidden"), sem("ex_gelu"), sem("ex_out")
                s_ye, s_u, s_free = sem("ex_out_copied"), sem("ex_stored"), sem("ex_out_free")
                s_hu = sem("ex_hidden_used")
                with nc.psum_tensor("ex_ps1", [P, 2, 2, 512], f32) as p1, nc.psum_tensor("ex_ps2", [P, 4, 512], f32) as p2, \
                        nc.Block() as block:
                    @block.sync
                    def _(sp):
                        sp.sem_inc(s_free, 2)
                        for e in range(NE):
                            sp.dma_start(w1[:, :, e, :], a["L0_ffn_W1"][e].rearrange("(c p) f -> p c f", p=P)).then_inc(s_w, 16)
                            sp.dma_start(w2[:, :, e, :], a["L0_ffn_W2"][e].rearrange("(c p) f -> p c f", p=P)).then_inc(s_w, 16)
                            with nc.allow_non_contiguous_dma(reason="bias by feature"):
                                sp.dma_start(b1[:, e, :], a["L0_ffn_b1"][e].rearrange("(c p) -> p c", p=P)).then_inc(s_w, 16)
                            sp.dma_start(b2[:, e, :], a["L0_ffn_b2"][e].partition_broadcast(P)).then_inc(s_w, 16)
                        with sp.Fori(0, NG) as g:
                            for e in range(NE):
                                sp.wait_ge(s_ye, g * (NE * GT) + (e + 1) * GT + 1)
                                sp.dma_start(y_d[e, :, bass.ds(g * (GT * D), GT * D)], yo[:, e % 2, :]).then_inc(s_u, 16)
                                sp.wait_ge(s_u, g * (16 * NE) + 16 * (e + 1))
                                sp.sem_inc(s_free, 1)

                    @block.tensor
                    def _(pe):
                        pe.sem_inc(s_y, 1)
                        pe.wait_ge(s_w, 16 * 4 * NE)
                        with pe.Fori(0, NG) as g:
                            for e in range(NE):
                                for m in range(KF):
                                    u = e * KF + m
                                    if u >= 2:
                                        pe.wait_ge(s_g, g * (NE * KF) + (u - 1) + 1)
                                    else:
                                        pe.wait_ge(s_g, g * (NE * KF) + 1)
                                    for n in range(2):
                                        for c in range(KD):
                                            last = nc.tensor.matmul(p1[:, u % 2, n, 0:HN], w1[:, c, e, m * P:(m + 1) * P],
                                                                    HT[:, c, bass.ds(g * GN + n * HN, HN)],
                                                                    start=(c == 0), stop=(c == KD - 1))
                                    last.then_inc(s_a, 1)
                                pe.wait_ge(s_g, g * (NE * KF) + (e + 1) * KF + 1)
                                for k in range(GT):
                                    v = e * GT + k
                                    if v >= 4:
                                        pe.wait_ge(s_ye, g * (NE * GT) + (v - 3) + 1)
                                    else:
                                        pe.wait_ge(s_ye, g * (NE * GT) + 1)
                                    for c in range(KF):
                                        last = nc.tensor.matmul(p2[:, v % 4, 0:D], hh[:, c, k * P:(k + 1) * P], w2[:, c, e, :],
                                                                start=(c == 0), stop=(c == KF - 1))
                                    last.then_inc(s_y, 1)

                    @block.scalar
                    def _(act):
                        act.sem_inc(s_g, 1)
                        with act.Fori(0, NG) as g:
                            for e in range(NE):
                                act.wait_ge(s_y, g * (NE * GT) + e * GT + 1)
                                for m in range(KF):
                                    u = e * KF + m
                                    act.wait_ge(s_a, g * (NE * KF) + (u + 1))
                                    nc.scalar.activation(hh[:, m, :].rearrange("p (n k) -> p n k", n=2), p1[:, u % 2, :, 0:HN], ACT.Gelu,
                                                         bias=b1[:, e, m:m + 1]).then_inc(s_g, 1)

                    @block.vector
                    def _(dve):
                        dve.sem_inc(s_ye, 1)
                        dve.wait_ge(s_w, 16 * 4 * NE)
                        with dve.Fori(0, NG) as g:
                            for e in range(NE):
                                dve.wait_ge(s_free, g * NE + (e + 1))
                                for k in range(GT):
                                    v = e * GT + k
                                    dve.wait_ge(s_y, g * (NE * GT) + (v + 1) + 1)
                                    nc.vector.tensor_tensor(yo[:, e % 2, k * D:(k + 1) * D], p2[:, v % 4, 0:D], b2[:, e, :],
                                                            ALU.add).then_inc(s_ye, 1)

        def stage_lin():
            tmp = ExitStack()

            def t(name, shape, dt=f32):
                return tmp.enter_context(nc.sbuf_tensor(name, shape, dt))

            with tmp:
                wt = t("lin_wt", [P, KD, D])
                br = t("lin_b", [P, D])
                sth = t("lin_sth", [P, GT, D])
                stt = t("lin_stt", [P, KD, GN])
                to = t("lin_out", [P, NT, D])
                s_w, s_h, s_t, s_c, s_y, s_o, s_d, s_o2 = (sem("lin_" + v) for v in ("w", "rows", "transposed", "staged", "made", "scaled", "stored", "biased"))
                with nc.psum_tensor("lin_pt", [P, KD, GN], f32) as pt, nc.psum_tensor("lin_py", [P, GT, D], f32) as py, \
                        nc.Block() as block:
                    @block.sync
                    def _(sp):
                        sp.dma_start(wt[:, :, :], a["L1_gnn_Wt"].rearrange("(c p) f -> p c f", p=P)).then_inc(s_w, 16)
                        sp.dma_start(br[:, :], a["L1_gnn_b"].partition_broadcast(P)).then_inc(s_w, 16)
                        sp.wait_ge(s_o, NT)
                        sp.dma_start(rows_d.rearrange("(t p) d -> p t d", p=P), to[:, :, :]).then_inc(s_d, 16)
                        sp.wait_ge(s_d, 16)

                    @block.vector
                    def _(dve):
                        dve.sem_inc(s_o2, 1)
                        dve.wait_ge(s_w, 32)
                        with dve.Fori(0, NG) as g:
                            dve.wait_ge(s_t, g + 1)
                            nc.vector.tensor_copy(sth[:, :, :], H[:, bass.ds(g * GT, GT), :]).then_inc(s_h, 1)
                            dve.wait_ge(s_y, g + 1 + 1)
                            nc.vector.tensor_tensor(to[:, bass.ds(g * GT, GT), :], py[:, :, :],
                                                    br[:, :].unsqueeze(1).to_broadcast([P, GT, D]), ALU.add).then_inc(s_o2, 1)
                            dve.drain()
                            for k in range(GT):
                                i = g * GT + k
                                o = to[:, bass.ds(i, 1), :].rearrange("p a b -> p (a b)")
                                nc.vector.tensor_scalar(o, o, norm[:, bass.ds(i, 1)], None, ALU.mult).then_inc(s_o, 1)

                    @block.scalar
                    def _(act):
                        with act.Fori(0, NG) as g:
                            act.wait_ge(s_t, g + 1 + 1)
                            act.wait_ge(s_y, g + 1)
                            nc.scalar.copy(stt[:, :, :], pt[:, :, :]).then_inc(s_c, 1)

                    @block.tensor
                    def _(pe):
                        pe.sem_inc(s_t, 1)
                        pe.sem_inc(s_y, 1)
                        pe.wait_ge(s_w, 32)
                        with pe.Fori(0, NG) as g:
                            pe.wait_ge(s_h, g + 1)
                            for k in range(GT):
                                for c in range(KD):
                                    last = nc.tensor.transpose(pt[:, c, k * P:(k + 1) * P], sth[:, k, c * P:(c + 1) * P], ident[:, :])
                            last.then_inc(s_t, 1)
                            pe.wait_ge(s_c, g + 1)
                            pe.wait_ge(s_o2, g + 1)
                            for k in range(GT):
                                for c in range(KD):
                                    last = nc.tensor.matmul(py[:, k, :], stt[:, c, k * P:(k + 1) * P], wt[:, c, :],
                                                            start=(c == 0), stop=(c == KD - 1))
                            last.then_inc(s_y, 1)

        def stage_add(acc):
            accv = acc[:, :].rearrange("p (t d) -> p t d", d=RW)
            with nc.Block() as block:
                @block.vector
                def _(dve):
                    with dve.Fori(0, NG) as g:
                        for k in range(GT):
                            i = g * GT + k
                            xs = X[:, bass.ds(i, 1), :].rearrange("p a b -> p (a b)")
                            nc.vector.scalar_tensor_tensor(xs, accv[:, bass.ds(i, 1), 0:D].rearrange("p a b -> p (a b)"),
                                                           norm[:, bass.ds(i, 1)], xs, ALU.mult, ALU.add)

        def stage_moe():
            tmp = ExitStack()

            def t(name, shape, dt=f32):
                return tmp.enter_context(nc.sbuf_tensor(name, shape, dt))

            with tmp:
                HT = t("moe_ht", [P, KD, NP])
                sth = t("moe_sth", [P, GT, D])
                wr = t("moe_wr", [P, KD, NE1])
                rw = t("moe_row", [1, 10, NE1])
                top = t("moe_top", [1, 8])
                topi = t("moe_topi", [1, 8], mybir.dt.uint32)
                wts = t("moe_wts", [1, 2])
                wcol = t("moe_wcol", [P, 2])
                mean = t("moe_mean", [P, KD])
                w1 = t("moe_w1", [P, 2, KD, F])
                w2 = t("moe_w2", [P, 2, KF, D])
                b1 = t("moe_b1", [P, 2, KF])
                b2 = t("moe_b2", [P, 2, D])
                bs = t("moe_bs", [P, D])
                gb = t("moe_gb", [P, 2, D])
                s_w, s_h, s_t, s_c = sem("moe_small"), sem("moe_rows"), sem("moe_transposed"), sem("moe_ht_copied")
                s_mn, s_mc, s_lg, s_rt = sem("moe_mean_made"), sem("moe_mean_copied"), sem("moe_logits"), sem("moe_routed")
                s_st, s_x, s_xd = sem("moe_step"), sem("moe_exp_in"), sem("moe_exp")
                s_wc, s_wcd, s_ld = sem("moe_weight_col"), sem("moe_pad2"), sem("moe_experts_loaded")
                with nc.psum_tensor("moe_pt", [P, KD, GN], f32) as pt, nc.psum_tensor("moe_pm", [P, 512], f32) as pm, \
                        nc.psum_tensor("moe_pw", [P, 512], f32) as pw, nc.Block() as block:
                    @block.sync
                    def _(sp):
                        sp.dma_start(wr[:, :, :], a["L1_ffn_Wr"].rearrange("(c p) e -> p c e", p=P)).then_inc(s_w, 16)
                        sp.dma_start(rw[:, 0, :], a["L1_ffn_br"].unsqueeze(0)).then_inc(s_w, 16)
                        sp.dma_start(gb[:, 0, :], a["L1_ffn_gamma"].partition_broadcast(P)).then_inc(s_w, 16)
                        sp.dma_start(gb[:, 1, :], a["L1_ffn_beta"].partition_broadcast(P)).then_inc(s_w, 16)
                        sp.wait_ge(s_rt, 1)
                        for j in range(2):
                            e = sp.value_load(topi[0:1, j:j + 1], min_val=0, max_val=NE1 - 1)
                            sp.dma_start(w1[:, j, :, :], a["L1_ffn_W1"][bass.ds(e, 1)].rearrange("o (c p) f -> p (o c) f", p=P)).then_inc(s_ld, 16)
                            sp.dma_start(w2[:, j, :, :], a["L1_ffn_W2"][bass.ds(e, 1)].rearrange("o (c p) f -> p (o c) f", p=P)).then_inc(s_ld, 16)
                            with nc.allow_non_contiguous_dma(reason="bias by feature"):
                                sp.dma_start(b1[:, j, :], a["L1_ffn_b1"][bass.ds(e, 1)].rearrange("o (c p) -> p (o c)", p=P)).then_inc(s_ld, 16)
                            sp.dma_start(b2[:, j, :], a["L1_ffn_b2"][bass.ds(e, 1)].to_broadcast([P, D])).then_inc(s_ld, 16)
                        sp.wait_ge(s_ld, 16 * 8)

                    @block.tensor
                    def _(pe):
                        pe.sem_inc(s_t, 1)
                        for c in range(KD):
                            for k in range(NT):
                                last = nc.tensor.matmul(pm[:, c:c + 1], H[:, k, c * P:(c + 1) * P],
                                                        valid[:, 1:2] if k == FULL else valid[:, 0:1],
                                                        start=(k == 0), stop=(k == NT - 1))
                        last.then_inc(s_mn, 1)
                        with pe.Fori(0, NG) as g:
                            pe.wait_ge(s_h, g + 1)
                            pe.wait_ge(s_c, g + 1)
                            for k in range(GT):
                                for c in range(KD):
                                    last = nc.tensor.transpose(pt[:, c, k * P:(k + 1) * P], sth[:, k, c * P:(c + 1) * P], ident[:, :])
                            last.then_inc(s_t, 1)
                        pe.wait_ge(s_w, 64)
                        pe.wait_ge(s_mc, 1)
                        for c in range(KD):
                            last = nc.tensor.matmul(pw[0:1, 0:NE1], mean[:, c:c + 1], wr[:, c, :], start=(c == 0), stop=(c == KD - 1))
                        last.then_inc(s_lg, 1)
                        pe.wait_ge(s_wc, 1)
                        nc.tensor.matmul(pm[:, 0:2], ones[0:1, :], wts[0:1, :], start=True, stop=True).then_inc(s_wcd, 1)

                    @block.vector
                    def _(dve):
                        dve.sem_inc(s_c, 1)
                        V = nc.vector
                        dve.wait_ge(s_mn, 1)
                        V.tensor_scalar(mean[:, :], pm[:, 0:KD], 1.0 / N, None, ALU.mult).then_inc(s_mc, 1)
                        with dve.Fori(0, NG) as g:
                            dve.wait_ge(s_t, g + 1)
                            V.tensor_copy(sth[:, :, :], H[:, bass.ds(g * GT, GT), :]).then_inc(s_h, 1)
                            dve.wait_ge(s_t, g + 1 + 1)
                            V.tensor_copy(HT[:, :, bass.ds(g * GN, GN)], pt[:, :, :]).then_inc(s_c, 1)
                        step = Chain(dve, s_st)

                        def softmax(src, dst, n, count):
                            step(V.tensor_reduce(rw[:, 9, 0:1], src, AX.X, ALU.max))
                            V.tensor_scalar(dst, src, rw[0:1, 9, 0:1], None, ALU.subtract).then_inc(s_x, 1)
                            dve.wait_ge(s_xd, count)
                            step(V.tensor_reduce(rw[:, 9, 0:1], dst, AX.X, ALU.add))
                            step(V.reciprocal(rw[:, 9, 1:2], rw[:, 9, 0:1]))
                            step(V.tensor_scalar(dst, dst, rw[0:1, 9, 1:2], None, ALU.mult))

                        dve.wait_ge(s_lg, 1)
                        step(V.tensor_tensor(rw[:, 1, :], rw[:, 0, :], pw[0:1, 0:NE1], ALU.add))
                        softmax(rw[:, 1, :], rw[:, 2, :], NE1, 1)
                        step(V.tensor_scalar(rw[:, 3, :], rw[:, 2, :], float(N), None, ALU.mult))
                        step(V.tensor_scalar(rw[:, 4, :], rw[:, 3, :], CAPACITY, None, ALU.is_gt))
                        step(V.tensor_scalar(rw[:, 3, :], rw[:, 3, :], CAPACITY, None, ALU.max))
                        step(V.reciprocal(rw[:, 5, :], rw[:, 3, :]))
                        step(V.tensor_scalar(rw[:, 5, :], rw[:, 5, :], CAPACITY, -1.0, ALU.mult, ALU.add))
                        step(V.tensor_tensor(rw[:, 5, :], rw[:, 5, :], rw[:, 4, :], ALU.mult))
                        step(V.tensor_scalar(rw[:, 5, :], rw[:, 5, :], 1.0, None, ALU.add))
                        step(V.tensor_tensor(rw[:, 6, :], rw[:, 2, :], rw[:, 5, :], ALU.mult))
                        softmax(rw[:, 6, :], rw[:, 7, :], NE1, 2)
                        step(V.max(top[:, :], rw[:, 7, :]))
                        V.max_index(topi[:, :], top[:, :], rw[:, 7, :]).then_inc(s_rt, 1)
                        softmax(top[:, 0:2], wts[:, :], 2, 3)
                        step(V.tensor_copy(wts[:, :], wts[:, :]))
                        V.tensor_copy(rw[:, 8, 0:2], wts[:, :]).then_inc(s_wc, 1)
                        dve.wait_ge(s_wcd, 1)
                        step(V.tensor_copy(wcol[:, :], pm[:, 0:2]))
                        dve.wait_ge(s_ld, 16 * 8)
                        for j in range(2):
                            V.tensor_scalar(w2[:, j, :, :].rearrange("p c f -> p (c f)"), w2[:, j, :, :].rearrange("p c f -> p (c f)"),
                                            wcol[:, j:j + 1], None, ALU.mult)
                        step(V.tensor_scalar(bs[:, :], b2[:, 0, :], wcol[:, 0:1], None, ALU.mult))
                        step(V.scalar_tensor_tensor(bs[:, :], b2[:, 1, :], wcol[:, 1:2], bs[:, :], ALU.mult, ALU.add))

                    @block.scalar
                    def _(act):
                        for k, v in enumerate((rw[:, 2, :], rw[:, 7, :], wts[:, :])):
                            act.wait_ge(s_x, k + 1)
                            nc.scalar.activation(v, v, ACT.Exp).then_inc(s_xd, 1)

                hh = t("moe_hh", [P, 2, KF, GN])
                os_ = t("moe_os", [P, 2, GT, D])
                HN = GN // 2
                mst = t("moe_st", [P, GT, 6])
                mmv = t("moe_mv", [P, GT, 2])
                msd = t("moe_sd", [P, GT])
                s_a, s_g, s_y, s_ye, s_sq, s_sr, s_o = (sem("moe_" + v) for v in (
                    "hidden", "gelu", "out", "out_added", "var", "std", "finished"))
                s_u, s_free = sem("moe_stored"), sem("moe_out_free")
                with nc.psum_tensor("moe_ps1", [P, 2, 2, 512], f32) as p1, nc.psum_tensor("moe_ps2", [P, 4, 512], f32) as p2, \
                        nc.Block() as block:
                    @block.tensor
                    def _(pe):
                        pe.sem_inc(s_y, 1)
                        with pe.Fori(0, NG) as g:
                            for e in range(2):
                                for m in range(KF):
                                    u = e * KF + m
                                    if u >= 2:
                                        pe.wait_ge(s_g, g * (2 * KF) + (u - 1) + 1)
                                    else:
                                        pe.wait_ge(s_g, g * (2 * KF) + 1)
                                    for n in range(2):
                                        for c in range(KD):
                                            last = nc.tensor.matmul(p1[:, u % 2, n, 0:HN], w1[:, e, c, m * P:(m + 1) * P],
                                                                    HT[:, c, bass.ds(g * GN + n * HN, HN)],
                                                                    start=(c == 0), stop=(c == KD - 1))
                                    last.then_inc(s_a, 1)
                            pe.wait_ge(s_g, (g + 1) * (2 * KF) + 1)
                            for k in range(GT):
                                if k >= 4:
                                    pe.wait_ge(s_ye, g * GT + (k - 3) + 1)
                                else:
                                    pe.wait_ge(s_ye, g * GT + 1)
                                for e in range(2):
                                    for c in range(KF):
                                        last = nc.tensor.matmul(p2[:, k % 4, 0:D], hh[:, e, c, k * P:(k + 1) * P], w2[:, e, c, :],
                                                                start=(e == 0 and c == 0), stop=(e == 1 and c == KF - 1))
                                last.then_inc(s_y, 1)

                    @block.scalar
                    def _(act):
                        act.sem_inc(s_g, 1)
                        with act.Fori(0, NG) as g:
                            act.wait_ge(s_y, g * GT + 1)
                            for e in range(2):
                                for m in range(KF):
                                    u = e * KF + m
                                    act.wait_ge(s_a, g * (2 * KF) + (u + 1))
                                    nc.scalar.activation(hh[:, e, m, :].rearrange("p (n k) -> p n k", n=2), p1[:, u % 2, :, 0:HN], ACT.Gelu,
                                                         bias=b1[:, e, m:m + 1]).then_inc(s_g, 1)
                            act.wait_ge(s_sq, g + 1)
                            nc.scalar.activation(msd[:, :], mmv[:, :, 1], ACT.Sqrt).then_inc(s_sr, 1)

                    @block.vector
                    def _(dve):
                        dve.sem_inc(s_ye, 1)
                        V = nc.vector
                        with dve.Fori(0, NG) as g:
                            ot = os_[:, 0, :, :]
                            dve.wait_ge(s_free, g + 1)
                            tl = bass.ds(g * GT, GT)
                            V.tensor_tensor(os_[:, 1, :, :], H[:, tl, :], bs[:, :].unsqueeze(1).to_broadcast([P, GT, D]), ALU.add)
                            dve.drain()
                            for k in range(GT):
                                dve.wait_ge(s_y, g * GT + (k + 1) + 1)
                                V.tensor_tensor(ot[:, k, :], p2[:, k % 4, 0:D], os_[:, 1, k, :], ALU.add).then_inc(s_ye, 1)
                            dve.drain()
                            for k in range(GT):
                                V.bn_stats(mst[:, k, :], ot[:, k, :])
                            dve.drain()
                            for k in range(GT):
                                V.bn_aggr(mmv[:, k, :], mst[:, k, :])
                            dve.drain()
                            V.tensor_scalar(mmv[:, :, 1], mmv[:, :, 1], EPS, None, ALU.add).then_inc(s_sq, 1)
                            dve.wait_ge(s_sr, g + 1)
                            V.reciprocal(msd[:, :], msd[:, :])
                            dve.drain()
                            for k in range(GT):
                                V.tensor_scalar(ot[:, k, :], ot[:, k, :], mmv[:, k, 0:1], msd[:, k:k + 1], ALU.subtract, ALU.mult)
                            dve.drain()
                            V.tensor_tensor(ot, ot, gb[:, 0, :].unsqueeze(1).to_broadcast([P, GT, D]), ALU.mult)
                            dve.drain()
                            V.tensor_tensor(ot, ot, gb[:, 1, :].unsqueeze(1).to_broadcast([P, GT, D]), ALU.add)
                            dve.drain()
                            V.tensor_tensor(ot, ot, X[:, tl, :], ALU.add).then_inc(s_o, 1)

                    @block.sync
                    def _(sp):
                        sp.sem_inc(s_free, 1)
                        of = out[0:FULL * P, :].rearrange("(t p) d -> p t d", p=P)
                        with sp.Fori(0, NG - 1) as g:
                            sp.wait_ge(s_o, g + 1)
                            sp.dma_start(of[:, bass.ds(g * GT, GT), :], os_[:, 0, :, :]).then_inc(s_u, 32)
                            sp.wait_ge(s_u, (g + 1) * 32)
                            sp.sem_inc(s_free, 1)
                        g = NG - 1
                        sp.wait_ge(s_o, NG)
                        sp.dma_start(of[:, g * GT:FULL, :], os_[:, 0, 0:GT - 1, :]).then_inc(s_u, 16)
                        sp.dma_start(out[FULL * P:N, :], os_[0:TAIL, 0, GT - 1, :]).then_inc(s_u, 16)
                        sp.wait_ge(s_u, 32 * NG)

        stage_consts()
        end_stage()
        stage_sort()
        end_stage()
        rows_norm("ln0", load=True, table=True)
        with nc.sbuf_tensor("acc0", [P, NT * RW], f32) as acc:
            message_pass("mp0", acc)
            stage_gin(acc)
        end_stage()
        rows_norm("ln1")
        stage_gat()
        end_stage()
        rows_norm("ln2")
        stage_lin()
        with nc.sbuf_tensor("acc1", [P, NT * RW], f32) as acc:
            message_pass("mp1", acc)
            stage_add(acc)
        end_stage()
        rows_norm("ln3")
        stage_moe()


_INS = ['x', 'src', 'dst', 'L0_gnn_W1', 'L0_gnn_b1', 'L0_gnn_g1', 'L0_gnn_bt1', 'L0_gnn_W2', 'L0_gnn_b2',
        'L0_gnn_g2', 'L0_gnn_bt2', 'L0_gnn_eps_gin', 'L0_ffn_W_gat', 'L0_ffn_att_src', 'L0_ffn_att_dst',
        'L0_ffn_b_gat', 'L0_ffn_ln_gamma', 'L0_ffn_ln_beta', 'L0_ffn_W1', 'L0_ffn_b1', 'L0_ffn_W2', 'L0_ffn_b2',
        'L0_ffn_edge_index', 'L1_gnn_W', 'L1_gnn_b', 'L1_ffn_Wr', 'L1_ffn_br', 'L1_ffn_W1', 'L1_ffn_b1',
        'L1_ffn_W2', 'L1_ffn_b2', 'L1_ffn_gamma', 'L1_ffn_beta']


def kernel(**inputs):
    import numpy as _np
    import concourse.bacc as _bacc
    from concourse import mybir as _mybir
    from concourse.bass_utils import run_bass_kernel_spmd as _run

    nc = _bacc.Bacc("TRN2", target_bir_lowering=False, num_devices=1)
    arrays, aps = {}, {}
    for name in _INS:
        v = _np.asarray(inputs[name])
        if name == "L1_gnn_W":
            name, v = "L1_gnn_Wt", v.T
        if name == "L0_gnn_eps_gin":
            v = v.reshape(1)
        v = _np.ascontiguousarray(v)
        arrays["in_" + name] = v
        aps[name] = nc.dram_tensor("in_" + name, v.shape, _mybir.dt.from_np(v.dtype), kind="ExternalInput").ap()
    out = nc.dram_tensor("out_0", (N, D), _mybir.dt.float32, kind="ExternalOutput").ap()
    build(nc, aps, out)
    r = _run(nc, [arrays], core_ids=[0])
    return r.results[0]["out_0"]
```

```python
import numpy as np
import concourse.bass as bass
from concourse import mybir
from contextlib import ExitStack

f32 = mybir.dt.float32
bf16 = mybir.dt.bfloat16
i32 = mybir.dt.int32
ALU = mybir.AluOpType
ACT = mybir.ActivationFunctionType
AX = mybir.AxisListType

P = 128
N = 3125
D = 256
KD = D // P
F = 512
KF = F // P
NT = -(-N // P)
NP = NT * P
FULL = N // P
TAIL = N - FULL * P
GT = 5
NG = NT // GT
GN = GT * P
CH = 512
NCH = N // CH
CTAIL = N - NCH * CH

E1 = 50000
ET = 400
EROWS = E1 // ET
NB = NT + 1
PAD_DST = NT * P
HIST = NB * ET
HCH = 512
HCHUNKS = 3 * (-(-HIST // (3 * HCH)))
HISTP = HCHUNKS * HCH
TILES = P * ET // P
TCH = -(-TILES // P)
TLAST = TILES - (TCH - 1) * P
HALF = 8
UNIT = 4
RING = 8
AHEAD = 4
MAXSLOTS = -(-E1 // P) + NT - 1
ITERS = -(-MAXSLOTS // (UNIT * RING))
SLOTS = ITERS * UNIT * RING
SLOTSP = SLOTS + AHEAD * UNIT
RW = D + 1

E2 = 32768
ET2 = E2 // P
NE = 4
STEPS = NG * NE
STEP = -(-ET2 // STEPS)
ET2P = (STEPS + 2) * STEP
HEADS = 4
HK = HEADS * NE
TW = HK + HEADS
DW = 2 * HEADS
NE1 = 8
CAPACITY = float(-(-N * 5 // (4 * NE1)))
EPS = 1e-5


class Chain:

    def __init__(self, eng, sem):
        self.eng, self.sem, self.n = eng, sem, 0

    def __call__(self, ins):
        self.n += 1
        ins.then_inc(self.sem, 1)
        self.eng.wait_ge(self.sem, self.n)


def build(nc, a, out):
    ctx = ExitStack()
    names = set()
    stage_sems = []

    def sb(name, shape, dt=f32):
        return ctx.enter_context(nc.sbuf_tensor(name, shape, dt))

    def sem(name):
        assert name not in names
        names.add(name)
        stage_sems.append(nc.alloc_semaphore(name))
        return stage_sems[-1]

    def end_stage():
        nc.clear_and_free_semaphores(stage_sems)
        nc.all_engine_barrier()
        del stage_sems[:]

    def dram(name, shape, dt=f32):
        return nc.dram_tensor(name, shape, dt, kind="Internal").ap()

    with ctx:
        scattered = [ctx.enter_context(nc.semaphore(f"scattered_{k}")) for k in range(2 * HALF)]
        gathered = [ctx.enter_context(nc.semaphore(f"gathered_{k}")) for k in range(4 * STEP)]
        done = [0] * len(gathered)
        x_d = a["x"]
        edges_d = dram("edges_sorted", [P * ET, 2], i32)
        rows_d = dram("rows_table", [NP, D])
        srct_d = dram("gat_src_table", [NP, TW])
        dstt_d = dram("gat_dst_table", [NP, DW])
        y_d = dram("expert_outputs", [NE, P, NT * D])

        iota = sb("iota", [P, P])
        pidx = sb("pidx", [P, 1])
        ident = sb("ident", [P, P])
        tri = sb("tri", [P, P], bf16)
        ones_bf = sb("ones_bf", [P, P], bf16)
        ones = sb("ones", [P, P])
        valid = sb("valid", [P, 2])
        X = sb("X", [P, NT, D])
        HROOM = max(NT * D, STEP * NT * TW)
        h_room = sb("H", [P, HROOM])
        H = h_room[:, 0:NT * D].rearrange("p (t d) -> p t d", d=D)
        stats = sb("stats", [P, NT, 6])
        mv = sb("mv", [P, NT, 2])
        rstd = sb("rstd", [P, NT])
        eps_col = sb("eps_col", [P, 1])
        norm = sb("norm", [P, NT])
        slot_src = sb("slot_src", [P, SLOTS], i32)
        slot_dst = sb("slot_dst", [P, SLOTSP])
        slot_bkt = sb("slot_bkt", [1, SLOTS // UNIT], i32)

        def stage_consts():
            s_iota, s_c = sem("iota_made"), sem("const_step")
            with nc.sbuf_tensor("iota_i", [P, P], i32) as iota_i, nc.sbuf_tensor("pidx_i", [P, 1], i32) as pidx_i, \
                    nc.Block() as block:
                @block.gpsimd
                def _(pool):
                    nc.gpsimd.iota(iota_i[:, :], [[1, P]], base=0, channel_multiplier=0).then_inc(s_iota, 1)
                    nc.gpsimd.iota(pidx_i[:, :], [[1, 1]], base=0, channel_multiplier=1).then_inc(s_iota, 1)

                @block.vector
                def _(dve):
                    step = Chain(dve, s_c)
                    nc.vector.memset(ones[:, :], 1.0)
                    nc.vector.memset(ones_bf[:, :], 1.0)
                    nc.vector.memset(eps_col[:, :], EPS)
                    nc.vector.memset(valid[:, :], 1.0)
                    dve.wait_ge(s_iota, 2)
                    nc.vector.tensor_copy(iota[:, :], iota_i[:, :])
                    step(nc.vector.tensor_copy(pidx[:, :], pidx_i[:, :]))
                    nc.vector.tensor_scalar(ident[:, :], iota[:, :], pidx[:, 0:1], None, ALU.is_equal)
                    nc.vector.tensor_scalar(tri[:, :], iota[:, :], pidx[:, 0:1], None, ALU.is_gt)
                    nc.vector.tensor_scalar(valid[:, 1:2], pidx[:, :], float(TAIL), None, ALU.is_lt)

        def stage_sort():
            tmp = ExitStack()

            def t(name, shape, dt=f32):
                return tmp.enter_context(nc.sbuf_tensor(name, shape, dt))

            with tmp:
                dst_i = t("dst_i", [P, ET], i32)
                nxt_i = t("nxt_i", [P, ET], i32)
                src_i = t("src_i", [P, ET], i32)
                hi_f = t("hi_f", [P, ET])
                falls = t("falls", [P, 1 + NB])
                pair = t("pair", [P, ET, 2], i32)
                onehot = t("onehot", [P, HISTP], bf16)
                bkt0 = t("bkt0", [1, NB + 1])
                falls_i = t("falls_i", [1, 1], i32)
                ps = tmp.enter_context(nc.psum_tensor("ps_sort", [P, 8, 512], f32))

                s_pad, s_ld, s_st = sem("sort_pad"), sem("sort_loaded"), sem("sort_step")
                s_cnt, s_sum, s_pair, s_id = sem("counted"), sem("counts_summed"), sem("pairs_made"), sem("identity_stored")
                with nc.Block() as block:
                    @block.sync
                    def _(sp):
                        sp.wait_ge(s_pad, 3)
                        sp.dma_start(dst_i[0:EROWS, :], a["dst"].rearrange("(p t) -> p t", t=ET)).then_inc(s_ld, 16)
                        sp.dma_start(nxt_i[0:EROWS - 1, :],
                                     a["dst"][1:E1 - ET + 1].rearrange("(p t) -> p t", t=ET)).then_inc(s_ld, 16)
                        sp.dma_start(nxt_i[EROWS - 1:EROWS, 0:ET - 1], a["dst"][E1 - ET + 1:E1].unsqueeze(0)).then_inc(s_ld, 16)
                        sp.dma_start(src_i[0:EROWS, :], a["src"].rearrange("(p t) -> p t", t=ET)).then_inc(s_ld, 16)
                        sp.wait_ge(s_pair, 1)
                        sp.dma_start(edges_d.rearrange("(p t) k -> p t k", t=ET), pair[:, :, :]).then_inc(s_id, 16)
                        sp.wait_ge(s_id, 16)

                    @block.vector
                    def _(dve):
                        step = Chain(dve, s_st)
                        V = nc.vector
                        V.memset(dst_i[:, :], PAD_DST).then_inc(s_pad, 1)
                        V.memset(nxt_i[:, :], PAD_DST).then_inc(s_pad, 1)
                        V.memset(src_i[:, :], 0).then_inc(s_pad, 1)
                        V.memset(onehot[:, HIST:HISTP], 0.0)
                        dve.wait_ge(s_ld, 64)
                        V.tensor_copy(pair[:, :, 0], src_i[:, :])
                        V.tensor_copy(pair[:, :, 1], dst_i[:, :]).then_inc(s_pair, 1)
                        V.tensor_scalar(nxt_i[:, :], nxt_i[:, :], 7, None, ALU.logical_shift_right)
                        step(V.tensor_scalar(dst_i[:, :], dst_i[:, :], 7, None, ALU.logical_shift_right))
                        step(V.tensor_copy(hi_f[:, :], dst_i[:, :]))
                        V.tensor_tensor(src_i[:, :], nxt_i[:, :], dst_i[:, :], ALU.is_lt)
                        step(V.tensor_tensor(
                            onehot[:, 0:HIST].rearrange("p (b t) -> p b t", t=ET),
                            hi_f[:, :].unsqueeze(1).to_broadcast([P, NB, ET]),
                            iota[:, 0:NB].unsqueeze(2).to_broadcast([P, NB, ET]), ALU.is_equal))
                        V.tensor_reduce(falls[:, 0:1], src_i[:, :], AX.X, ALU.add)
                        V.tensor_reduce(falls[:, 1:1 + NB], onehot[:, 0:HIST].rearrange("p (b t) -> p b t", t=ET),
                                        AX.X, ALU.add).then_inc(s_cnt, 1)
                        V.memset(bkt0[:, 0:1], 0.0)
                        dve.wait_ge(s_sum, 1)
                        V.tensor_copy(falls_i[:, :], ps[0:1, 0, 0:1])
                        V.tensor_tensor_scan(bkt0[:, 1:1 + NB], ones[0:1, 0:1].to_broadcast([1, NB]),
                                             ps[0:1, 0, 1:1 + NB], 0.0, ALU.mult, ALU.add)

                    @block.tensor
                    def _(pe):
                        pe.wait_ge(s_cnt, 1)
                        nc.tensor.matmul(ps[:, 0, 0:1 + NB], ones[:, :], falls[:, :], start=True, stop=True).then_inc(s_sum, 1)

                with ExitStack() as big:
                    before = big.enter_context(nc.sbuf_tensor("before", [P, HISTP], bf16))
                    total = big.enter_context(nc.sbuf_tensor("total", [P, HISTP], bf16))
                    start = big.enter_context(nc.sbuf_tensor("start", [P, 1 + HISTP], f32))
                    pos_f = big.enter_context(nc.sbuf_tensor("pos_f", [P, ET], f32))
                    pos_i = big.enter_context(nc.sbuf_tensor("pos_i", [P, ET], i32))
                    st_pos = big.enter_context(nc.sbuf_tensor("st_pos", [P, 2 * HALF], i32))
                    st_pair = big.enter_context(nc.sbuf_tensor("st_pair", [P, 2 * HALF, 2], i32))
                    s_ct, s_pst = sem("counts_made"), sem("position_step")
                    s_be, s_to = sem("before_copied"), sem("total_copied")
                    s_pos, s_begun = sem("positions_made"), sem("scatter_begun")
                    s_stg = [sem("scatter_staged_a"), sem("scatter_staged_b")]
                    flat = lambda ap: ap.rearrange("p b t -> p (b t)")
                    with nc.Block() as block:
                        def unsorted(eng):
                            return eng.If(eng.value_load(falls_i[0:1, 0:1], min_val=0, max_val=P * ET) > 0)

                        @block.vector
                        def _(dve):
                            with unsorted(dve):
                                step = Chain(dve, s_pst)
                                dve.sem_inc(s_to, 1)
                                nc.vector.memset(start[:, 0:1], 0.0)
                                with dve.Fori(0, HCHUNKS // 3) as i:
                                    dve.wait_ge(s_ct, 3 * i + 3)
                                    nc.vector.tensor_copy(total[:, bass.ds(i * (3 * HCH), 3 * HCH)],
                                                          flat(ps[:, 3:6, :])).then_inc(s_to, 1)
                                dve.wait_ge(s_to, HCHUNKS // 3 + 1)
                                step(nc.vector.tensor_tensor_scan(
                                    start[:, 1:1 + HIST], ones[:, 0:1].to_broadcast([P, HIST]), total[:, 0:HIST],
                                    0.0, ALU.mult, ALU.add))
                                dve.wait_ge(s_be, HCHUNKS // 3 + 1)
                                starts = start[:, 0:HIST]
                                step(nc.vector.tensor_tensor(starts, starts, before[:, 0:HIST], ALU.add))
                                step(nc.vector.tensor_tensor(starts, starts, onehot[:, 0:HIST], ALU.mult))
                                step(nc.vector.tensor_reduce(
                                    pos_f[:, :], starts.rearrange("p (b t) -> p t b", t=ET), AX.X, ALU.add))
                                nc.vector.tensor_copy(pos_i[:, :], pos_f[:, :]).then_inc(s_pos, 1)

                        @block.tensor
                        def _(pe):
                            with unsorted(pe):
                                with pe.Fori(0, HCHUNKS // 3) as i:
                                    pe.wait_ge(s_be, i + 1)
                                    pe.wait_ge(s_to, i + 1)
                                    for k in range(3):
                                        rhs = onehot[:, bass.ds(i * (3 * HCH) + k * HCH, HCH)]
                                        nc.tensor.matmul(ps[:, k, :], tri[:, :], rhs, start=True, stop=True)
                                        nc.tensor.matmul(ps[:, 3 + k, :], ones_bf[:, :], rhs, start=True,
                                                         stop=True).then_inc(s_ct, 1)

                        @block.scalar
                        def _(act):
                            with unsorted(act):
                                act.sem_inc(s_be, 1)
                                with act.Fori(0, HCHUNKS // 3) as i:
                                    act.wait_ge(s_ct, 3 * i + 3)
                                    nc.scalar.copy(before[:, bass.ds(i * (3 * HCH), 3 * HCH)],
                                                   flat(ps[:, 0:3, :])).then_inc(s_be, 1)
                                act.wait_ge(s_pos, 1)

                                def put(h, at):
                                    r = slice(h * HALF, (h + 1) * HALF)
                                    nc.scalar.copy(st_pos[:, r], pos_i[:, bass.ds(at, HALF)])
                                    nc.scalar.copy(st_pair[:, r, :], pair[:, bass.ds(at, HALF), :]).then_inc(s_stg[h], 1)

                                for h in range(2):
                                    put(h, h * HALF)
                                with act.Fori(0, ET // (2 * HALF) - 1) as i:
                                    for h in range(2):
                                        for k in range(h * HALF, (h + 1) * HALF):
                                            act.wait_ge(scattered[k], i * 16 + 16)
                                        put(h, (i + 1) * (2 * HALF) + h * HALF)

                        @block.gpsimd
                        def _(pool):
                            with unsorted(pool):
                                with pool.Fori(0, ET // (2 * HALF)) as i:
                                    for h in range(2):
                                        pool.wait_ge(s_stg[h], i + 1)
                                        pool.sem_inc(s_begun, 1)
                                        for k in range(h * HALF, (h + 1) * HALF):
                                            pool.indirect_dma_start(
                                                out=edges_d, out_offset=bass.IndirectOffsetOnAxis(ap=st_pos[:, k:k + 1], axis=0),
                                                in_=st_pair[:, k, :], in_offset=None).then_inc(scattered[k], 16)
                                for k in range(2 * HALF):
                                    pool.wait_ge(scattered[k], 16 * ET // (2 * HALF))

                row = t("row", [1, 6, NB])
                bnd = t("bnd", [1, 2, NB], i32)
                col3 = t("col3", [P, 3])
                wid = t("wid", [P, 2, P])
                iota_j = t("iota_j", [P, SLOTS])
                iota_ji = t("iota_ji", [P, SLOTS], i32)
                selb = t("selb", [P, SLOTS])
                tile_j = t("tile_j", [P, SLOTS])
                bkt_j = t("bkt_j", [P, SLOTS])
                val_j = t("val_j", [P, SLOTS])
                nat_i = t("nat_i", [P, TCH, 2 * P], i32)
                nat = t("nat", [P, TCH, 2 * P])
                tcol = t("tcol", [P, TCH])
                sel = t("sel", [P, TCH, SLOTS])
                pk = t("pk", [1, SLOTS])
                s_ij, s_nat, s_sl = sem("iota_j_made"), sem("sorted_loaded"), sem("slot_step")
                s_c3, s_row, s_sb = sem("cols_made"), sem("rows_made"), sem("bucket_sel")
                s_wid, s_npad = sem("wide_made"), sem("sorted_pad")
                s_sel, s_slot = sem("tile_sel"), sem("slots_made")
                with nc.Block() as block:
                    @block.gpsimd
                    def _(pool):
                        nc.gpsimd.iota(iota_ji[:, :], [[1, SLOTS]], base=0, channel_multiplier=0).then_inc(s_ij, 1)

                    @block.sync
                    def _(sp):
                        full = (TCH - 1) * P * P
                        sp.dma_start(nat_i[:, 0:TCH - 1, :],
                                     edges_d[0:full, :].rearrange("(c p e) k -> p c (e k)", p=P, e=P)).then_inc(s_nat, 16)
                        sp.wait_ge(s_npad, 1)
                        sp.dma_start(nat_i[0:TLAST, TCH - 1, :],
                                     edges_d[full:P * ET, :].rearrange("(p e) k -> p (e k)", e=P)).then_inc(s_nat, 16)

                    @block.vector
                    def _(dve):
                        step = Chain(dve, s_sl)
                        V = nc.vector
                        V.memset(nat_i[:, TCH - 1, :], PAD_DST).then_inc(s_npad, 1)
                        V.memset(col3[:, :], 0.0)
                        V.memset(slot_dst[:, SLOTS:SLOTSP], -1.0)
                        first, last, count, end, begin, off = (row[:, k, 0:NT] for k in range(6))
                        b0, b1 = bkt0[:, 0:NT], bkt0[:, 1:NT + 1]
                        step(V.tensor_copy(bnd[:, 0, 0:NT], b0))
                        step(V.tensor_scalar(last, b1, -1.0, None, ALU.add))
                        step(V.tensor_copy(bnd[:, 1, 0:NT], last))
                        V.tensor_scalar(bnd[:, 0, 0:NT], bnd[:, 0, 0:NT], 7, None, ALU.logical_shift_right)
                        step(V.tensor_scalar(bnd[:, 1, 0:NT], bnd[:, 1, 0:NT], 7, None, ALU.arith_shift_right))
                        V.tensor_copy(first, bnd[:, 0, 0:NT])
                        V.tensor_tensor(off, b1, b0, ALU.is_gt)
                        step(V.tensor_copy(last, bnd[:, 1, 0:NT]))
                        step(V.tensor_tensor(count, last, first, ALU.subtract))
                        step(V.scalar_tensor_tensor(count, count, 1.0, off, ALU.add, ALU.mult))
                        step(V.tensor_tensor_scan(end, ones[0:1, 0:1].to_broadcast([1, NT]), count, 0.0, ALU.mult, ALU.add))
                        step(V.tensor_tensor(begin, end, count, ALU.subtract))
                        V.tensor_tensor(off, first, begin, ALU.subtract).then_inc(s_row, 1)
                        dve.wait_ge(s_ij, 1)
                        step(V.tensor_copy(iota_j[:, :], iota_ji[:, :]))
                        dve.wait_ge(s_c3, 1)
                        step(V.tensor_copy(col3[0:NT, :], ps[0:NT, 0, 0:3]))
                        V.tensor_copy(wid[:, 0, :], col3[:, 2:3].to_broadcast([P, P]))
                        V.tensor_copy(wid[:, 1, :], pidx[:, 0:1].to_broadcast([P, P]))
                        step(V.tensor_scalar(tile_j[:, :], iota_j[:, :], col3[:, 0:1], None, ALU.is_lt))
                        V.scalar_tensor_tensor(selb[:, :], iota_j[:, :], col3[:, 1:2], tile_j[:, :], ALU.is_ge,
                                               ALU.mult).then_inc(s_wid, 1)
                        for c in range(TCH):
                            V.tensor_scalar(tcol[:, c:c + 1], pidx[:, :], float(c * P), None, ALU.add)
                        dve.wait_ge(s_nat, 32)
                        V.tensor_copy(nat[:, :, :], nat_i[:, :, :])
                        dve.wait_ge(s_sb, 1)
                        V.tensor_copy(bkt_j[:, :], ps[:, 2, 0:SLOTS])
                        V.tensor_scalar(val_j[:, :], ps[:, 3, 0:SLOTS], -1.0, 4096.0, ALU.add, ALU.mult)
                        step(V.tensor_tensor(tile_j[:, :], iota_j[:, :], ps[:, 1, 0:SLOTS], ALU.add))
                        step(V.tensor_tensor(tile_j[:, :], tile_j[:, :], val_j[:, :], ALU.add))
                        for c in range(TCH):
                            last_sel = V.tensor_scalar(sel[:, c, :], tile_j[:, :], tcol[:, c:c + 1], None, ALU.is_equal)
                        last_sel.then_inc(s_sel, 1)
                        pv = pk[:, :].rearrange("p (q k) -> p q k", k=UNIT)
                        bv = bkt_j[0:1, :].rearrange("p (q k) -> p q k", k=UNIT)
                        step(V.tensor_copy(pv[:, :, 0], bv[:, :, UNIT - 1]))
                        for k in range(UNIT - 2, -1, -1):
                            step(V.scalar_tensor_tensor(pv[:, :, 0], pv[:, :, 0], 32.0, bv[:, :, k], ALU.mult, ALU.add))
                        V.tensor_copy(slot_bkt[:, :], pv[:, :, 0])
                        step(V.scalar_tensor_tensor(bkt_j[:, :], bkt_j[:, :], -float(P), val_j[:, :], ALU.mult, ALU.add))
                        dve.wait_ge(s_slot, 1)
                        V.tensor_copy(slot_src[:, :], ps[:, 4, 0:SLOTS])
                        V.tensor_tensor(slot_dst[:, 0:SLOTS], ps[:, 5, 0:SLOTS], bkt_j[:, :], ALU.add)

                    @block.tensor
                    def _(pe):
                        pe.wait_ge(s_row, 1)
                        for k in range(3):
                            last = nc.tensor.matmul(ps[0:NT, 0, k:k + 1], row[0:1, 3 + k, 0:NT], ones[0:1, 0:1],
                                                    start=True, stop=True)
                        last.then_inc(s_c3, 1)
                        pe.wait_ge(s_wid, 1)
                        nc.tensor.matmul(ps[:, 1, 0:SLOTS], wid[0:NT, 0, :], selb[0:NT, :], start=True, stop=True)
                        nc.tensor.matmul(ps[:, 2, 0:SLOTS], wid[0:NT, 1, :], selb[0:NT, :], start=True, stop=True)
                        nc.tensor.matmul(ps[:, 3, 0:SLOTS], ones[0:NT, :], selb[0:NT, :], start=True,
                                         stop=True).then_inc(s_sb, 1)
                        pe.wait_ge(s_sel, 1)
                        for k in range(2):
                            for c in range(TCH):
                                lhs = nat[:, c, :].rearrange("p (e k) -> p e k", k=2)[:, :, k]
                                last = nc.tensor.matmul(ps[:, 4 + k, 0:SLOTS], lhs, sel[:, c, :],
                                                        start=(c == 0), stop=(c == TCH - 1))
                        last.then_inc(s_slot, 1)

        def rows_norm(tag, load=False, table=False):
            s_x, s_mv, s_std, s_h = sem(tag + "_x"), sem(tag + "_stats"), sem(tag + "_std"), sem(tag + "_h")
            s_t, s_ms = sem(tag + "_table"), sem(tag + "_moment_step")
            with nc.Block() as block:
                @block.sync
                def _(sp):
                    if load:
                        sp.wait_ge(s_h, 1)
                        sp.dma_start(X[:, 0:FULL, :], x_d[0:FULL * P, :].rearrange("(t p) d -> p t d", p=P)).then_inc(s_x, 16)
                        sp.dma_start(X[0:TAIL, FULL, :], x_d[FULL * P:N, :]).then_inc(s_x, 16)
                    if table:
                        sp.wait_ge(s_h, NT + 1)
                        sp.dma_start(rows_d.rearrange("(t p) d -> p t d", p=P), H[:, :, :]).then_inc(s_t, 16)
                        sp.wait_ge(s_t, 16)

                @block.vector
                def _(dve):
                    if load:
                        nc.vector.memset(X[:, FULL, :], 0.0).then_inc(s_h, 1)
                        dve.wait_ge(s_x, 32)
                    else:
                        nc.vector.memset(rstd[:, 0:1], 0.0).then_inc(s_h, 1)
                    with dve.Fori(0, NG) as g:
                        for k in range(GT):
                            nc.vector.bn_stats(stats[:, bass.ds(g * GT + k, 1), :].rearrange("p a b -> p (a b)"),
                                               X[:, bass.ds(g * GT + k, 1), :].rearrange("p a b -> p (a b)"))
                    dve.drain()
                    step = Chain(dve, s_ms)
                    mean_e, sq_e, mean_o, sq_o = (stats[:, :, k] for k in (1, 2, 4, 5))
                    nc.vector.tensor_tensor(sq_e, sq_e, sq_o, ALU.add)
                    nc.vector.tensor_tensor(mv[:, :, 0], mean_e, mean_o, ALU.add)
                    step(nc.vector.tensor_tensor(mean_e, mean_e, mean_o, ALU.subtract))
                    nc.vector.tensor_scalar(mv[:, :, 0], mv[:, :, 0], 0.5, None, ALU.mult)
                    nc.vector.tensor_scalar(sq_e, sq_e, 1.0 / D, EPS, ALU.mult, ALU.add)
                    step(nc.vector.tensor_tensor(mean_o, mean_e, mean_e, ALU.mult))
                    nc.vector.scalar_tensor_tensor(mv[:, :, 1], mean_o, 0.25, sq_e, ALU.mult, ALU.add).then_inc(s_mv, 1)
                    dve.wait_ge(s_std, 1)
                    nc.vector.reciprocal(rstd[:, :], rstd[:, :])
                    dve.drain()
                    with dve.Fori(0, NG) as g:
                        for k in range(GT):
                            i = g * GT + k
                            nc.vector.tensor_scalar(
                                H[:, bass.ds(i, 1), :].rearrange("p a b -> p (a b)"),
                                X[:, bass.ds(i, 1), :].rearrange("p a b -> p (a b)"),
                                mv[:, bass.ds(i, 1), 0], rstd[:, bass.ds(i, 1)],
                                ALU.subtract, ALU.mult).then_inc(s_h, 1)

                @block.scalar
                def _(act):
                    act.wait_ge(s_mv, 1)
                    nc.scalar.activation(rstd[:, :], mv[:, :, 1], ACT.Sqrt).then_inc(s_std, 1)

        def message_pass(tag, acc):
            tmp = ExitStack()
            with tmp:
                NR = UNIT * RING
                rows = tmp.enter_context(nc.sbuf_tensor(tag + "_rows", [P, NR, RW], f32))
                hot = tmp.enter_context(nc.sbuf_tensor(tag + "_hot", [P, NR, P], f32))
                idx = tmp.enter_context(nc.sbuf_tensor(tag + "_idx", [P, NR], i32))
                drel = tmp.enter_context(nc.sbuf_tensor(tag + "_drel", [P, NR], f32))
                ps = tmp.enter_context(nc.psum_tensor(tag + "_ps", [P, 2 * UNIT, 512], f32))
                s_idx, s_hot, s_mm, s_acc = (sem(tag + v) for v in ("_idx", "_hot", "_summed", "_added"))
                s_one, s_begun = sem(tag + "_ones"), sem(tag + "_begun")
                base = done[0]
                for k in range(NR):
                    assert done[k] == base
                    done[k] += 16 * ITERS
                places = lambda u: slice(u * UNIT, (u + 1) * UNIT)
                with nc.Block() as block:
                    @block.scalar
                    def _(act):
                        def put(u, at):
                            nc.scalar.copy(idx[:, places(u)], slot_src[:, bass.ds(at, UNIT)]).then_inc(s_idx, 1)

                        for u in range(RING):
                            put(u, u * UNIT)
                        with act.Fori(0, ITERS - 1) as i:
                            for u in range(RING):
                                act.wait_ge(s_mm, i * RING + (u + 1))
                                put(u, (i + 1) * NR + u * UNIT)

                    @block.gpsimd
                    def _(pool):
                        with pool.Fori(0, ITERS) as i:
                            for u in range(RING):
                                pool.wait_ge(s_idx, i * RING + (u + 1))
                                pool.sem_inc(s_begun, 1)
                                for k in range(u * UNIT, (u + 1) * UNIT):
                                    pool.indirect_dma_start(
                                        out=rows[:, k, 0:D], out_offset=None, in_=rows_d,
                                        in_offset=bass.IndirectOffsetOnAxis(ap=idx[:, k:k + 1], axis=0),
                                    ).then_inc(gathered[k], 16)

                    @block.vector
                    def _(dve):
                        nc.vector.memset(rows[:, :, D:RW], 1.0).then_inc(s_one, 1)
                        nc.vector.memset(acc[:, :], 0.0)

                        def one_hots(u, at):
                            nc.vector.tensor_copy(drel[:, places(u)], slot_dst[:, bass.ds(at, UNIT)])
                            dve.drain()
                            for k in range(u * UNIT, (u + 1) * UNIT):
                                last = nc.vector.tensor_scalar(hot[:, k, :], iota[:, :], drel[:, k:k + 1], None, ALU.is_equal)
                            last.then_inc(s_hot, 1)

                        for u in range(AHEAD):
                            one_hots(u, u * UNIT)
                        with dve.Fori(0, ITERS) as i:
                            for u in range(RING):
                                w = dve.value_load(slot_bkt[0:1, bass.ds(i * RING + u, 1)], min_val=0, max_val=(1 << 20) - 1)
                                one_hots((u + AHEAD) % RING, i * NR + (u + AHEAD) * UNIT)
                                bkt = [w % 32, (w // 32) % 32, (w // 1024) % 32, w // 32768]
                                for k in range(UNIT):
                                    b = nc.s_assert_within(bkt[k], 0, NT - 1, skip_runtime_bounds_check_because="a slot's bucket is one of NT")
                                    to = acc[:, bass.ds(b * RW, RW)]
                                    dve.drain()
                                    if k == 0:
                                        dve.wait_ge(s_mm, i * RING + (u + 1))
                                    last = nc.vector.tensor_tensor(to, to, ps[:, (u % 2) * UNIT + k, 0:RW], ALU.add)
                                last.then_inc(s_acc, 1)

                    @block.tensor
                    def _(pe):
                        def unit(u, i):
                            pe.wait_ge(s_hot, i * RING + (u + 1))
                            for k in range(UNIT):
                                pe.wait_ge(gathered[u * UNIT + k], i * 16 + (base + 16))
                                last = nc.tensor.matmul(ps[:, (u % 2) * UNIT + k, 0:RW], hot[:, u * UNIT + k, :],
                                                        rows[:, u * UNIT + k, :], start=True, stop=True)
                            last.then_inc(s_mm, 1)

                        pe.wait_ge(s_one, 1)
                        for u in range(2):
                            unit(u, 0)
                        for u in range(2, RING):
                            pe.wait_ge(s_acc, u - 1)
                            unit(u, 0)
                        with pe.Fori(1, ITERS) as i:
                            for u in range(RING):
                                pe.wait_ge(s_acc, i * RING + (u - 1))
                                unit(u, i)

        def stage_gin(acc):
            accv = acc[:, :].rearrange("p (t d) -> p t d", d=RW)
            tmp = ExitStack()

            def t(name, shape, dt=f32):
                return tmp.enter_context(nc.sbuf_tensor(name, shape, dt))

            with tmp:
                w1 = t("gin_w1", [P, KD, F])
                w2 = t("gin_w2", [P, KF, D])
                vec1 = t("gin_vec1", [P, 3, KF])
                vec2 = t("gin_vec2", [P, 3, KD])
                eps1 = t("gin_eps1", [P, 1])
                deg = t("deg", [P, NT])
                stage = t("gin_stage", [P, 2, GT * D])
                stz = stage[:, 0, :].rearrange("p (t d) -> p t d", d=D)
                sth = stage[:, 1, :].rearrange("p (t d) -> p t d", d=D)
                ZT = t("gin_zt", [P, KD, NP])
                HT = t("gin_ht", [P, KD, NP])
                s_w, s_deg, s_z = sem("gin_weights"), sem("gin_deg"), sem("gin_z")
                s_zt, s_zc, s_hc = sem("gin_transposed"), sem("gin_zt_copied"), sem("gin_ht_copied")
                s_step = sem("gin_step")
                with nc.psum_tensor("gin_pst", [P, KD, GN], f32) as pz, nc.psum_tensor("gin_psh", [P, KD, GN], f32) as ph, \
                        nc.Block() as block:
                    @block.sync
                    def _(sp):
                        with nc.allow_non_contiguous_dma(reason="small vectors by feature"):
                            sp.dma_start(eps1[:, :], a["L0_gnn_eps_gin"].partition_broadcast(P)).then_inc(s_w, 16)
                            for k, v in enumerate(("b1", "g1", "bt1")):
                                sp.dma_start(vec1[:, k, :], a["L0_gnn_" + v].rearrange("(c p) -> p c", p=P)).then_inc(s_w, 16)
                            for k, v in enumerate(("b2", "g2", "bt2")):
                                sp.dma_start(vec2[:, k, :], a["L0_gnn_" + v].rearrange("(c p) -> p c", p=P)).then_inc(s_w, 16)
                        sp.dma_start(w1[:, :, :], a["L0_gnn_W1"].rearrange("(c p) f -> p c f", p=P)).then_inc(s_w, 16)
                        sp.dma_start(w2[:, :, :], a["L0_gnn_W2"].rearrange("(c p) f -> p c f", p=P)).then_inc(s_w, 16)

                    @block.vector
                    def _(dve):
                        dve.sem_inc(s_zc, 1)
                        step = Chain(dve, s_step)
                        step(nc.vector.tensor_scalar(deg[:, :], accv[:, :, D], 1.0, None, ALU.max))
                        nc.vector.reciprocal(deg[:, :], deg[:, :]).then_inc(s_deg, 1)
                        dve.wait_ge(s_w, 16 * 9)
                        step(nc.vector.tensor_scalar(eps1[:, :], eps1[:, :], 1.0, None, ALU.add))
                        with dve.Fori(0, NG) as g:
                            dve.wait_ge(s_zt, g + 1)
                            tl = bass.ds(g * GT, GT)
                            nc.vector.tensor_copy(sth[:, :, :], H[:, tl, :])
                            nc.vector.scalar_tensor_tensor(stz, H[:, tl, :], eps1[:, 0:1], accv[:, tl, 0:D],
                                                           ALU.mult, ALU.add).then_inc(s_z, 1)
                            dve.wait_ge(s_zt, g + 1 + 1)
                            nc.vector.tensor_copy(ZT[:, :, bass.ds(g * GN, GN)], pz[:, :, :]).then_inc(s_zc, 1)

                    @block.tensor
                    def _(pe):
                        pe.sem_inc(s_zt, 1)
                        with pe.Fori(0, NG) as g:
                            pe.wait_ge(s_z, g + 1)
                            pe.wait_ge(s_zc, g + 1)
                            pe.wait_ge(s_hc, g + 1)
                            for k in range(GT):
                                for c in range(KD):
                                    nc.tensor.transpose(pz[:, c, k * P:(k + 1) * P], stz[:, k, c * P:(c + 1) * P], ident[:, :])
                                    last = nc.tensor.transpose(ph[:, c, k * P:(k + 1) * P], sth[:, k, c * P:(c + 1) * P], ident[:, :])
                            last.then_inc(s_zt, 1)

                    @block.scalar
                    def _(act):
                        act.sem_inc(s_hc, 1)
                        act.wait_ge(s_deg, 1)
                        nc.scalar.activation(norm[:, :], deg[:, :], ACT.Sqrt)
                        with act.Fori(0, NG) as g:
                            act.wait_ge(s_zt, g + 1 + 1)
                            nc.scalar.copy(HT[:, :, bass.ds(g * GN, GN)], ph[:, :, :]).then_inc(s_hc, 1)

                TT = t("gin_tt", [P, KF, N])
                st1 = t("gin_st1", [P, KF, NCH + 1, 6])
                st2 = t("gin_st2", [P, KD, NCH + 1, 6])
                mv1 = t("gin_mv1", [P, KF, 2])
                mv2 = t("gin_mv2", [P, KD, 2])
                sc1 = t("gin_sc1", [P, 2, KF])
                sc2 = t("gin_sc2", [P, 2, KD])

                def bn_coefficients(dve, st, mv, sc, vec, s_var, s_sd, s_ready):
                    for m in range(mv.shape[1]):
                        nc.vector.bn_aggr(mv[:, m, :], st[:, m, :, :].rearrange("p a b -> p (a b)"))
                    dve.drain()
                    nc.vector.tensor_scalar(mv[:, :, 1], mv[:, :, 1], EPS, None, ALU.add).then_inc(s_var, 1)
                    dve.wait_ge(s_sd, 1)
                    nc.vector.reciprocal(sc[:, 1, :], sc[:, 0, :])
                    dve.drain()
                    nc.vector.tensor_tensor(sc[:, 0, :], sc[:, 1, :], vec[:, 1, :], ALU.mult)
                    dve.drain()
                    nc.vector.tensor_tensor(sc[:, 1, :], mv[:, :, 0], sc[:, 0, :], ALU.mult)
                    dve.drain()
                    nc.vector.tensor_tensor(sc[:, 1, :], vec[:, 2, :], sc[:, 1, :], ALU.subtract).then_inc(s_ready, 1)

                s_mm, s_ev, s_st = sem("gin_t_made"), sem("gin_t_copied"), sem("gin_t_stats")
                s_va, s_sd, s_sc = sem("gin_var1"), sem("gin_sd1"), sem("gin_scale1")
                with nc.psum_tensor("gin_ps1", [P, 2, KF, CH], f32) as ps, nc.Block() as block:
                    @block.tensor
                    def _(pe):
                        def chunk(b, lo, n, count):
                            pe.wait_ge(s_ev, count + 1)
                            for m in range(KF):
                                for c in range(KD):
                                    last = nc.tensor.matmul(ps[:, b, m, 0:n], w1[:, c, m * P:(m + 1) * P],
                                                            ZT[:, c, bass.ds(lo, n)], start=(c == 0), stop=(c == KD - 1))
                            last.then_inc(s_mm, 1)
                        with pe.Fori(0, NCH // 2) as i:
                            for b in range(2):
                                chunk(b, i * (2 * CH) + b * CH, CH, i * (2 * KF))
                        chunk(0, NCH * CH, CTAIL, (NCH - 1) * KF)

                    @block.scalar
                    def _(act):
                        act.sem_inc(s_ev, 1)
                        def chunk(b, lo, n, count):
                            act.wait_ge(s_mm, count)
                            for m in range(KF):
                                nc.scalar.activation(TT[:, m, bass.ds(lo, n)], ps[:, b, m, 0:n], ACT.Identity,
                                                     bias=vec1[:, 0, m:m + 1]).then_inc(s_ev, 1)
                        with act.Fori(0, NCH // 2) as i:
                            for b in range(2):
                                chunk(b, i * (2 * CH) + b * CH, CH, i * 2 + b + 1)
                        chunk(0, NCH * CH, CTAIL, NCH + 1)
                        act.wait_ge(s_va, 1)
                        nc.scalar.activation(sc1[:, 0, :], mv1[:, :, 1], ACT.Sqrt).then_inc(s_sd, 1)

                    @block.vector
                    def _(dve):
                        def chunk(j, lo, n, count):
                            for m in range(KF):
                                dve.wait_ge(s_ev, count + m + 1 + 1)
                                o = st1[:, m, j, :] if isinstance(j, int) else st1[:, m, bass.ds(j, 1), :].rearrange("p a b -> p (a b)")
                                nc.vector.bn_stats(o, TT[:, m, bass.ds(lo, n)])
                        with dve.Fori(0, NCH) as i:
                            chunk(i, i * CH, CH, i * KF)
                        chunk(NCH, NCH * CH, CTAIL, NCH * KF)
                        dve.drain()
                        bn_coefficients(dve, st1, mv1, sc1, vec1, s_va, s_sd, s_sc)

                s_rl, s_cv, s_cc = sem("gin_relu"), sem("gin_c_made"), sem("gin_c_copied")
                s_va2, s_sd2, s_sc2 = sem("gin_var2"), sem("gin_sd2"), sem("gin_scale2")
                with nc.psum_tensor("gin_ps2", [P, 2, KD, CH], f32) as ps, nc.Block() as block:
                    @block.scalar
                    def _(act):
                        def chunk(lo, n):
                            for m in range(KF):
                                nc.scalar.activation(TT[:, m, bass.ds(lo, n)], TT[:, m, bass.ds(lo, n)], ACT.Relu,
                                                     bias=sc1[:, 1, m:m + 1], scale=sc1[:, 0, m:m + 1]).then_inc(s_rl, 1)
                        with act.Fori(0, NCH) as i:
                            chunk(i * CH, CH)
                        chunk(NCH * CH, CTAIL)
                        act.wait_ge(s_va2, 1)
                        nc.scalar.activation(sc2[:, 0, :], mv2[:, :, 1], ACT.Sqrt).then_inc(s_sd2, 1)

                    @block.tensor
                    def _(pe):
                        def chunk(b, lo, n, r, c0):
                            pe.wait_ge(s_rl, r)
                            pe.wait_ge(s_cc, c0 + 1)
                            for m in range(KD):
                                for c in range(KF):
                                    last = nc.tensor.matmul(ps[:, b, m, 0:n], w2[:, c, m * P:(m + 1) * P],
                                                            TT[:, c, bass.ds(lo, n)], start=(c == 0), stop=(c == KF - 1))
                            last.then_inc(s_cv, 1)
                        with pe.Fori(0, NCH // 2) as i:
                            for b in range(2):
                                chunk(b, i * (2 * CH) + b * CH, CH, i * (2 * KF) + (b + 1) * KF, i * (2 * KD))
                        chunk(0, NCH * CH, CTAIL, (NCH + 1) * KF, (NCH - 1) * KD)

                    @block.vector
                    def _(dve):
                        dve.sem_inc(s_cc, 1)
                        nc.vector.memset(ZT[:, :, N:NP], 0.0)

                        def chunk(b, j, lo, n, count):
                            dve.wait_ge(s_cv, count)
                            for m in range(KD):
                                nc.vector.scalar_tensor_tensor(
                                    ZT[:, m, bass.ds(lo, n)], ps[:, b, m, 0:n], vec2[:, 0, m:m + 1],
                                    HT[:, m, bass.ds(lo, n)], ALU.add, ALU.add).then_inc(s_cc, 1)
                            dve.drain()
                            for m in range(KD):
                                o = st2[:, m, j, :] if isinstance(j, int) else st2[:, m, bass.ds(j, 1), :].rearrange("p a b -> p (a b)")
                                nc.vector.bn_stats(o, ZT[:, m, bass.ds(lo, n)])
                        with dve.Fori(0, NCH // 2) as i:
                            for b in range(2):
                                chunk(b, i * 2 + b, i * (2 * CH) + b * CH, CH, i * 2 + b + 1)
                        chunk(0, NCH, NCH * CH, CTAIL, NCH + 1)
                        dve.drain()
                        bn_coefficients(dve, st2, mv2, sc2, vec2, s_va2, s_sd2, s_sc2)

                s_r2, s_xt, s_xa = sem("gin_relu2"), sem("gin_back"), sem("gin_x_added")
                stc = stage[:, :, :].rearrange("p b (c n) -> p b c n", n=GN)
                with nc.psum_tensor("gin_ps3", [P, GT, D], f32) as ps, nc.Block() as block:
                    @block.scalar
                    def _(act):
                        def group(b, g):
                            for m in range(KD):
                                last = nc.scalar.activation(stc[:, b, m, :], ZT[:, m, bass.ds(g * GN, GN)], ACT.Relu,
                                                            bias=sc2[:, 1, m:m + 1], scale=sc2[:, 0, m:m + 1])
                            last.then_inc(s_r2, 1)
                        group(0, 0)
                        group(1, 1)
                        with act.Fori(0, NG // 2) as i:
                            act.wait_ge(s_xt, 2 * i + 1)
                            group(0, 2 * i + 2)
                            act.wait_ge(s_xt, 2 * i + 2)
                            group(1, (2 * i + 3) % NG)

                    @block.tensor
                    def _(pe):
                        def group(b, g):
                            pe.wait_ge(s_r2, g + 1)
                            pe.wait_ge(s_xa, g + 1)
                            for k in range(GT):
                                for c in range(KD):
                                    last = nc.tensor.transpose(ps[:, k, c * P:(c + 1) * P], stc[:, b, c, k * P:(k + 1) * P], ident[:, :])
                            last.then_inc(s_xt, 1)
                        group(0, 0)
                        with pe.Fori(0, NG // 2) as i:
                            group(1, 2 * i + 1)
                            group(0, 2 * i + 2)

                    @block.vector
                    def _(dve):
                        dve.sem_inc(s_xa, 1)
                        with dve.Fori(0, NG) as g:
                            dve.wait_ge(s_xt, g + 1)
                            xs = X[:, bass.ds(g * GT, GT), :]
                            nc.vector.tensor_tensor(xs, xs, ps[:, :, :], ALU.add).then_inc(s_xa, 1)

        def stage_gat():
            tmp = ExitStack()

            def t(name, shape, dt=f32):
                return tmp.enter_context(nc.sbuf_tensor(name, shape, dt))

            with tmp:
                wg = t("gat_w", [P, KD, HK])
                rowv = t("gat_rows", [P, 5, HK])
                HT = t("gat_ht", [P, KD, NP])
                TS = t("gat_ts", [P, NT, TW])
                TD = t("gat_td", [P, NT, DW])
                prod = t("gat_prod", [P, NT, HK])
                gmax = t("gat_gmax", [P, HEADS])
                gall = t("gat_gall", [P, HEADS])
                e_s = t("gat_es", [P, NT, HEADS])
                self_e = t("gat_self", [P, NT, HEADS])
                es_i = t("gat_es_i", [P, ET2P], i32)
                ed_i = t("gat_ed_i", [P, ET2P], i32)
                lo_i = t("gat_lo_i", [P, ET2P], i32)
                lo_f = t("gat_lo_f", [P, ET2P])
                hi_f = t("gat_hi_f", [P, ET2P])
                hh = t("ex_hh", [P, KF, GN])
                stt = hh[:, 0:KD, :]
                sth = hh[:, KD:KF, :].rearrange("p c n -> p (c n)").rearrange("p (t d) -> p t d", d=D)
                s_w, s_e, s_pad = sem("gat_weights"), sem("gat_edges"), sem("gat_pad")
                s_h, s_t, s_c, s_c2 = sem("gat_h"), sem("gat_t"), sem("gat_ht_copied"), sem("gat_stage_copied")
                s_hh, s_hc = sem("gat_hh_made"), sem("gat_hh_copied")
                s_m, s_g, s_tab, s_st = sem("gat_max"), sem("gat_gmax"), sem("gat_tables"), sem("gat_step")
                s_out, s_ex = sem("gat_tables_out"), sem("gat_exp")
                with nc.psum_tensor("gat_pst", [P, KD, GN], f32) as pt, nc.psum_tensor("gat_psh", [P, GT, HK], f32) as ph, \
                        nc.Block() as block:
                    @block.sync
                    def _(sp):
                        sp.dma_start(wg[:, :, :], a["L0_ffn_W_gat"].rearrange("(c p) f -> p c f", p=P)).then_inc(s_w, 16)
                        for k, v in enumerate(("att_src", "att_dst")):
                            sp.dma_start(rowv[:, k, :], a["L0_ffn_" + v].rearrange("h k -> (h k)").partition_broadcast(P)).then_inc(s_w, 16)
                        for k, v in enumerate(("b_gat", "ln_gamma", "ln_beta")):
                            sp.dma_start(rowv[:, 2 + k, :], a["L0_ffn_" + v].partition_broadcast(P)).then_inc(s_w, 16)
                        sp.wait_ge(s_pad, 1)
                        for dst, k in ((es_i, 0), (ed_i, 1)):
                            sp.dma_start(dst[:, 0:ET2], a["L0_ffn_edge_index"][k, :].rearrange("(p t) -> p t", p=P)).then_inc(s_e, 16)
                        sp.wait_ge(s_tab, 1)
                        sp.dma_start(srct_d.rearrange("(t p) k -> p t k", p=P), TS[:, :, :]).then_inc(s_out, 16)
                        sp.dma_start(dstt_d.rearrange("(t p) k -> p t k", p=P), TD[:, :, :]).then_inc(s_out, 16)
                        sp.wait_ge(s_out, 32)

                    @block.vector
                    def _(dve):
                        dve.sem_inc(s_c, 1)
                        dve.sem_inc(s_hc, 1)
                        V = nc.vector
                        V.memset(es_i[:, ET2:ET2P], NP - 1)
                        V.memset(ed_i[:, ET2:ET2P], NP - 1).then_inc(s_pad, 1)
                        with dve.Fori(0, NG) as g:
                            dve.wait_ge(s_t, g + 1)
                            V.tensor_copy(sth[:, :, :], H[:, bass.ds(g * GT, GT), :]).then_inc(s_h, 1)
                            dve.wait_ge(s_c2, g + 1 + 1)
                            V.tensor_copy(HT[:, :, bass.ds(g * GN, GN)], stt[:, :, :]).then_inc(s_c, 1)
                            dve.wait_ge(s_hh, g + 1 + 1)
                            V.tensor_copy(TS[:, bass.ds(g * GT, GT), HEADS:TW], ph[:, :, :]).then_inc(s_hc, 1)
                        step = Chain(dve, s_st)
                        dve.wait_ge(s_w, 16 * 6)
                        hv = TS[:, :, HEADS:TW]
                        for k, to in ((0, TS[:, :, 0:HEADS]), (1, TD[:, :, 0:HEADS])):
                            dve.drain()
                            step(V.tensor_tensor(prod[:, :, :], hv, rowv[:, k, :].unsqueeze(1).to_broadcast([P, NT, HK]), ALU.mult))
                            step(V.tensor_reduce(to, prod[:, :, :].rearrange("p t (h k) -> p t h k", k=NE), AX.X, ALU.add))
                        a_s, a_d, shift = TS[:, :, 0:HEADS], TD[:, :, 0:HEADS], TD[:, :, HEADS:DW]
                        V.tensor_reduce(gmax[:, :], a_s.rearrange("p t h -> p h t"), AX.X, ALU.max).then_inc(s_m, 1)
                        step(V.tensor_tensor(e_s[:, :, :], a_s, a_d, ALU.add))
                        step(V.scalar_tensor_tensor(e_s[:, :, :], e_s[:, :, :], 0.2, e_s[:, :, :], ALU.mult, ALU.max))
                        dve.wait_ge(s_g, 1)
                        step(V.tensor_tensor(self_e[:, :, :], a_d, gall[:, :].unsqueeze(1).to_broadcast([P, NT, HEADS]), ALU.add))
                        step(V.scalar_tensor_tensor(self_e[:, :, :], self_e[:, :, :], 0.2, self_e[:, :, :], ALU.mult, ALU.max))
                        step(V.tensor_scalar(self_e[:, :, :], self_e[:, :, :], -60.0, None, ALU.add))
                        step(V.tensor_tensor(shift, self_e[:, :, :], e_s[:, :, :], ALU.max))
                        step(V.tensor_tensor(e_s[:, :, :], e_s[:, :, :], shift, ALU.subtract))
                        V.tensor_copy(gmax[:, :], gall[:, :]).then_inc(s_tab, 1)
                        dve.wait_ge(s_e, 32)
                        step(V.tensor_scalar(lo_i[:, :], ed_i[:, :], P - 1, None, ALU.bitwise_and))
                        step(V.tensor_copy(lo_f[:, :], lo_i[:, :]))
                        step(V.tensor_scalar(lo_i[:, :], ed_i[:, :], 7, None, ALU.logical_shift_right))
                        step(V.tensor_copy(hi_f[:, :], lo_i[:, :]))
                        V.memset(hi_f[:, ET2:ET2P], float(NT))

                    @block.gpsimd
                    def _(pool):
                        pool.wait_ge(s_m, 1)
                        nc.gpsimd.partition_all_reduce(gall[:, :], gmax[:, :], P, bass.bass_isa.ReduceOp.max).then_inc(s_g, 1)

                    @block.scalar
                    def _(act):
                        act.sem_inc(s_c2, 1)
                        with act.Fori(0, NG) as g:
                            act.wait_ge(s_t, g + 1 + 1)
                            act.wait_ge(s_hh, g + 1)
                            act.wait_ge(s_c, g + 1)
                            nc.scalar.copy(stt[:, :, :], pt[:, :, :]).then_inc(s_c2, 1)
                        act.wait_ge(s_tab, 1)
                        nc.scalar.activation(self_e[:, :, :], e_s[:, :, :], ACT.Exp).then_inc(s_ex, 1)

                    @block.tensor
                    def _(pe):
                        pe.sem_inc(s_t, 1)
                        pe.sem_inc(s_hh, 1)
                        pe.wait_ge(s_w, 16 * 6)
                        with pe.Fori(0, NG) as g:
                            pe.wait_ge(s_h, g + 1)
                            pe.wait_ge(s_c2, g + 1)
                            pe.wait_ge(s_hc, g + 1)
                            for k in range(GT):
                                for c in range(KD):
                                    last = nc.tensor.transpose(pt[:, c, k * P:(k + 1) * P], sth[:, k, c * P:(c + 1) * P], ident[:, :])
                            last.then_inc(s_t, 1)
                            pe.wait_ge(s_c2, g + 1 + 1)
                            for k in range(GT):
                                for c in range(KD):
                                    last = nc.tensor.matmul(ph[:, k, :], stt[:, c, k * P:(k + 1) * P], wg[:, c, :],
                                                            start=(c == 0), stop=(c == KD - 1))
                            last.then_inc(s_hh, 1)

                sums = t("gat_sums", [P, NT, TW])
                loop = ExitStack()
                u = lambda name, shape, dt=f32: loop.enter_context(nc.sbuf_tensor(name, shape, dt))
                w1 = u("ex_w1", [P, KD, NE, F])
                w2 = u("ex_w2", [P, KF, NE, D])
                b1 = u("ex_b1", [P, NE, KF])
                b2 = u("ex_b2", [P, NE, D])
                yo = u("ex_yo", [P, 2, GT * D])
                gs = u("gat_gs", [P, 2 * STEP, TW])
                gd = u("gat_gd", [P, 2 * STEP, DW])
                ix = u("gat_ix", [P, 2, 2 * STEP], i32)
                lh = u("gat_lh", [P, 2, 2 * STEP])
                ev = u("gat_ev", [P, 2 * STEP, HEADS])
                msg = u("gat_msg", [P, 2 * STEP, TW])
                hot = u("gat_hot", [P, 2 * STEP, P])
                hih = u("gat_hih", [P, 2 * STEP, NT])
                mov_b = u("gat_mov", [P, STEP, NT * TW])
                mov = [h_room[:, 0:STEP * NT * TW].rearrange("p (k w) -> p k w", k=STEP), mov_b]
                HN = GN // 2
                src_sem, dst_sem = gathered[0:2 * STEP], gathered[2 * STEP:4 * STEP]
                base_of = done[:]
                for k in range(4 * STEP):
                    done[k] += 16 * (STEPS // 2)
                s_ix, s_begun = sem("gat_ix"), sem("gat_begun")
                s_ev, s_ee, s_mv, s_mm = sem("gat_score"), sem("gat_weight"), sem("gat_moving"), sem("gat_summed")
                s_z, s_fin = sem("gat_zero"), sem("gat_all_summed")
                s_w, s_a, s_g, s_y = sem("ex_weights"), sem("ex_hidden"), sem("ex_gelu"), sem("ex_out")
                s_ye, s_u, s_free = sem("ex_out_copied"), sem("ex_stored"), sem("ex_out_free")
                WLOADS = 16 * 4 * NE
                with nc.psum_tensor("gat_acc", [P, 512], f32) as ps, \
                        nc.psum_tensor("ex_ps1", [P, 2, 2, 512], f32) as p1, nc.psum_tensor("ex_ps2", [P, 3, 512], f32) as p2, \
                        nc.Block() as block:
                    acc = ps[:, 0:NT * TW]
                    half = lambda e: slice((e % 2) * STEP, (e % 2 + 1) * STEP)

                    @block.sync
                    def _(sp):
                        sp.sem_inc(s_free, 2)
                        for e in range(NE):
                            sp.dma_start(w1[:, :, e, :], a["L0_ffn_W1"][e].rearrange("(c p) f -> p c f", p=P)).then_inc(s_w, 16)
                            sp.dma_start(w2[:, :, e, :], a["L0_ffn_W2"][e].rearrange("(c p) f -> p c f", p=P)).then_inc(s_w, 16)
                            with nc.allow_non_contiguous_dma(reason="bias by feature"):
                                sp.dma_start(b1[:, e, :], a["L0_ffn_b1"][e].rearrange("(c p) -> p c", p=P)).then_inc(s_w, 16)
                            sp.dma_start(b2[:, e, :], a["L0_ffn_b2"][e].partition_broadcast(P)).then_inc(s_w, 16)
                        with sp.Fori(0, NG) as g:
                            for e in range(NE):
                                sp.wait_ge(s_ye, g * (NE * GT) + ((e + 1) * GT + 1))
                                sp.dma_start(y_d[e, :, bass.ds(g * (GT * D), GT * D)], yo[:, e % 2, :]).then_inc(s_u, 16)
                                sp.wait_ge(s_u, g * (16 * NE) + 16 * (e + 1))
                                sp.sem_inc(s_free, 1)

                    @block.gpsimd
                    def _(pool):
                        with pool.Fori(0, NG) as g:
                            for e in range(NE):
                                pool.wait_ge(s_ix, g * NE + (e + 1))
                                pool.sem_inc(s_begun, 1)
                                for k in range((e % 2) * STEP, (e % 2 + 1) * STEP):
                                    pool.indirect_dma_start(
                                        out=gs[:, k, :], out_offset=None, in_=srct_d,
                                        in_offset=bass.IndirectOffsetOnAxis(ap=ix[:, 0, k:k + 1], axis=0)).then_inc(src_sem[k], 16)
                                    pool.indirect_dma_start(
                                        out=gd[:, k, :], out_offset=None, in_=dstt_d,
                                        in_offset=bass.IndirectOffsetOnAxis(ap=ix[:, 1, k:k + 1], axis=0)).then_inc(dst_sem[k], 16)

                    @block.scalar
                    def _(act):
                        def put(e, at):
                            nc.scalar.copy(ix[:, 0, half(e)], es_i[:, bass.ds(at, STEP)])
                            nc.scalar.copy(ix[:, 1, half(e)], ed_i[:, bass.ds(at, STEP)]).then_inc(s_ix, 1)

                        act.sem_inc(s_g, 1)
                        for e in range(2):
                            put(e, e * STEP)
                        with act.Fori(0, NG) as g:
                            for e in range(NE):
                                w = g * NE + e
                                act.wait_ge(s_y, g * (NE * GT) + (e * GT + 1))
                                for m in range(KF):
                                    act.wait_ge(s_a, g * (NE * KF) + (e * KF + m + 1))
                                    nc.scalar.activation(hh[:, m, :].rearrange("p (n k) -> p n k", n=2), p1[:, m % 2, :, 0:HN],
                                                         ACT.Gelu, bias=b1[:, e, m:m + 1]).then_inc(s_g, 1)
                                act.wait_ge(s_ev, g * NE + (e + 1))
                                nc.scalar.activation(msg[:, half(e), HK:TW], ev[:, half(e), :], ACT.Exp).then_inc(s_ee, 1)
                                act.wait_ge(s_mm, g * NE + (e + 3))
                                put(e, (g * NE + (e + 2)) * STEP)

                    @block.vector
                    def _(dve):
                        V = nc.vector
                        dve.sem_inc(s_ye, 1)
                        V.memset(sums[:, :, :], 0.0).then_inc(s_z, 1)
                        dve.wait_ge(s_w, WLOADS)
                        with dve.Fori(0, NG) as g:
                            for e in range(NE):
                                r = half(e)
                                ks = range((e % 2) * STEP, (e % 2 + 1) * STEP)
                                at = bass.ds((g * NE + e) * STEP, STEP)
                                dve.wait_ge(s_mm, g * NE + (e + 1))
                                V.tensor_copy(lh[:, 0, r], lo_f[:, at])
                                V.tensor_copy(lh[:, 1, r], hi_f[:, at])
                                dve.drain()
                                for k in ks:
                                    V.tensor_scalar(hot[:, k, :], iota[:, :], lh[:, 0, k:k + 1], None, ALU.is_equal)
                                V.tensor_tensor(hih[:, r, :], iota[:, 0:NT].unsqueeze(1).to_broadcast([P, STEP, NT]),
                                                lh[:, 1, r].unsqueeze(2).to_broadcast([P, STEP, NT]), ALU.is_equal)
                                for k in ks:
                                    dve.wait_ge(src_sem[k], g * 32 + (16 * (e // 2 + 1) + base_of[k]))
                                    dve.wait_ge(dst_sem[k], g * 32 + (16 * (e // 2 + 1) + base_of[2 * STEP + k]))
                                V.tensor_tensor(ev[:, r, :], gs[:, r, 0:HEADS], gd[:, r, 0:HEADS], ALU.add)
                                dve.drain()
                                V.scalar_tensor_tensor(ev[:, r, :], ev[:, r, :], 0.2, ev[:, r, :], ALU.mult, ALU.max)
                                dve.drain()
                                V.tensor_tensor(ev[:, r, :], ev[:, r, :], gd[:, r, HEADS:DW], ALU.subtract).then_inc(s_ev, 1)
                                dve.wait_ge(s_ee, g * NE + (e + 1))
                                V.tensor_tensor(
                                    msg[:, r, 0:HK].rearrange("p t (h k) -> p t h k", k=NE),
                                    gs[:, r, HEADS:TW].rearrange("p t (h k) -> p t h k", k=NE),
                                    msg[:, r, HK:TW].unsqueeze(3).to_broadcast([P, STEP, HEADS, NE]), ALU.mult)
                                dve.drain()
                                for k in ks:
                                    V.tensor_tensor(
                                        mov[e % 2][:, k % STEP, :].rearrange("p (t w) -> p t w", w=TW),
                                        msg[:, k, :].unsqueeze(1).to_broadcast([P, NT, TW]),
                                        hih[:, k, :].unsqueeze(2).to_broadcast([P, NT, TW]), ALU.mult).then_inc(s_mv, 1)
                                dve.wait_ge(s_free, g * NE + (e + 1))
                                for k in range(GT):
                                    dve.wait_ge(s_y, g * (NE * GT) + (e * GT + k + 2))
                                    V.tensor_tensor(yo[:, e % 2, k * D:(k + 1) * D], p2[:, (e * GT + k) % 2, 0:D], b2[:, e, :],
                                                    ALU.add).then_inc(s_ye, 1)
                        dve.wait_ge(s_fin, 1)
                        V.tensor_copy(sums[:, :, :].rearrange("p t w -> p (t w)"), acc)

                    @block.tensor
                    def _(pe):
                        pe.sem_inc(s_y, 1)
                        pe.sem_inc(s_mm, 2)
                        pe.wait_ge(s_z, 1)
                        zeros = sums[:, :, :].rearrange("p t w -> p (t w)")
                        nc.tensor.matmul(acc, ident[:, :], zeros, start=True, stop=False, skip_group_check=True)
                        pe.wait_ge(s_w, WLOADS)
                        with pe.Fori(0, NG) as g:
                            for e in range(NE):
                                for m in range(KF):
                                    pe.wait_ge(s_g, g * (NE * KF) + max(e * KF + m, 1))
                                    for n in range(2):
                                        for c in range(KD):
                                            last = nc.tensor.matmul(p1[:, m % 2, n, 0:HN], w1[:, c, e, m * P:(m + 1) * P],
                                                                    HT[:, c, bass.ds(g * GN + n * HN, HN)],
                                                                    start=(c == 0), stop=(c == KD - 1))
                                    last.then_inc(s_a, 1)
                                for k in range(STEP):
                                    q = (e % 2) * STEP + k
                                    pe.wait_ge(s_mv, (g * NE + e) * STEP + (k + 1))
                                    last = nc.tensor.matmul(acc, hot[:, q, :], mov[e % 2][:, k, :], start=False,
                                                            stop=False, skip_group_check=True)
                                last.then_inc(s_mm, 1)
                                pe.wait_ge(s_g, g * (NE * KF) + ((e + 1) * KF + 1))
                                for k in range(GT):
                                    v = e * GT + k
                                    pe.wait_ge(s_ye, g * (NE * GT) + max(v, 1))
                                    for c in range(KF):
                                        last = nc.tensor.matmul(p2[:, v % 2, 0:D], hh[:, c, k * P:(k + 1) * P], w2[:, c, e, :],
                                                                start=(c == 0), stop=(c == KF - 1))
                                    last.then_inc(s_y, 1)
                        nc.tensor.matmul(acc, ident[:, :], zeros, start=False, stop=True, skip_group_check=True).then_inc(s_fin, 1)
                loop.close()

                agg = t("gat_agg", [P, NT, HK])
                den = t("gat_den", [P, NT, HEADS])
                s1 = t("gat_s1", [P, NT, 1])
                sc = t("gat_sc", [P, NT, NE])
                rank = t("gat_rank", [P, NT, NE])
                cmp_ = t("gat_cmp", [P, NT])
                gate = t("gat_gate", [P, NT, NE])
                yst = t("gat_yst", [P, 2, GT * D])
                s_k, s_sq, s_q, s_ex2, s_b2 = sem("mix_step"), sem("mix_var"), sem("mix_std"), sem("mix_exp"), sem("mix_b2")
                s_e2, s_gate = sem("mix_score"), sem("mix_gate")
                s_y = [sem("mix_y_a"), sem("mix_y_b")]
                s_yu = sem("mix_y_used")
                with nc.Block() as block:
                    @block.vector
                    def _(dve):
                        dve.sem_inc(s_yu, 1)
                        V = nc.vector
                        step = Chain(dve, s_k)
                        b4 = lambda ap: ap.unsqueeze(3).to_broadcast([P, NT, HEADS, NE])
                        v4 = lambda ap: ap.rearrange("p t (h k) -> p t h k", k=NE)
                        rb = lambda k: rowv[:, k, :].unsqueeze(1).to_broadcast([P, NT, HK])
                        nb = lambda ap, w: ap.to_broadcast([P, NT, w])
                        step(V.tensor_tensor(v4(agg[:, :, :]), v4(TS[:, :, HEADS:TW]), b4(self_e[:, :, :]), ALU.mult))
                        step(V.tensor_tensor(agg[:, :, :], agg[:, :, :], sums[:, :, 0:HK], ALU.add))
                        step(V.tensor_tensor(den[:, :, :], sums[:, :, HK:TW], self_e[:, :, :], ALU.add))
                        step(V.tensor_scalar(den[:, :, :], den[:, :, :], 1e-16, None, ALU.add))
                        step(V.reciprocal(den[:, :, :], den[:, :, :]))
                        step(V.tensor_tensor(v4(agg[:, :, :]), v4(agg[:, :, :]), b4(den[:, :, :]), ALU.mult))
                        step(V.tensor_tensor(agg[:, :, :], agg[:, :, :], rb(2), ALU.add))
                        step(V.tensor_reduce(s1[:, :, 0], agg[:, :, :], AX.X, ALU.add))
                        step(V.tensor_scalar(s1[:, :, :], s1[:, :, :], 1.0 / HK, None, ALU.mult))
                        step(V.tensor_tensor(agg[:, :, :], agg[:, :, :], nb(s1[:, :, :], HK), ALU.subtract))
                        step(V.tensor_tensor(prod[:, :, :], agg[:, :, :], agg[:, :, :], ALU.mult))
                        step(V.tensor_reduce(s1[:, :, 0], prod[:, :, :], AX.X, ALU.add))
                        V.tensor_scalar(s1[:, :, :], s1[:, :, :], 1.0 / HK, EPS, ALU.mult, ALU.add).then_inc(s_sq, 1)
                        dve.wait_ge(s_q, 1)
                        step(V.reciprocal(s1[:, :, :], s1[:, :, :]))
                        step(V.tensor_tensor(agg[:, :, :], agg[:, :, :], nb(s1[:, :, :], HK), ALU.mult))
                        step(V.tensor_tensor(agg[:, :, :], agg[:, :, :], rb(3), ALU.mult))
                        step(V.tensor_tensor(agg[:, :, :], agg[:, :, :], rb(4), ALU.add))
                        step(V.tensor_reduce(sc[:, :, :], agg[:, :, :].rearrange("p t (h k) -> p t k h", k=NE), AX.X, ALU.add))
                        step(V.tensor_scalar(sc[:, :, :], sc[:, :, :], 1.0 / HEADS, None, ALU.mult))
                        step(V.memset(rank[:, :, :], 0.0))
                        for i in range(NE):
                            for j in range(NE):
                                if i != j:
                                    op = ALU.is_ge if j < i else ALU.is_gt
                                    step(V.tensor_tensor(cmp_[:, :], sc[:, :, j], sc[:, :, i], op))
                                    step(V.tensor_tensor(rank[:, :, i], rank[:, :, i], cmp_[:, :], ALU.add))
                        step(V.tensor_reduce(s1[:, :, 0], sc[:, :, :], AX.X, ALU.max))
                        V.tensor_tensor(sc[:, :, :], sc[:, :, :], nb(s1[:, :, :], NE), ALU.subtract).then_inc(s_e2, 1)
                        step(V.tensor_scalar(rank[:, :, :], rank[:, :, :], 1.5, None, ALU.is_lt))
                        dve.wait_ge(s_ex2, 1)
                        step(V.tensor_tensor(gate[:, :, :], gate[:, :, :], rank[:, :, :], ALU.mult))
                        step(V.tensor_reduce(s1[:, :, 0], gate[:, :, :], AX.X, ALU.add))
                        step(V.reciprocal(s1[:, :, :], s1[:, :, :]))
                        step(V.tensor_tensor(gate[:, :, :], gate[:, :, :], nb(s1[:, :, :], NE), ALU.mult))
                        dve.drain()
                        for e in range(NE):
                            with dve.Fori(0, NG) as g:
                                b = 0
                                dve.wait_ge(s_y[b], g * 16 + (e * NG + 1) * 16)
                                for k in range(GT):
                                    i = g * GT + k
                                    xs = X[:, bass.ds(i, 1), :].rearrange("p a b -> p (a b)")
                                    last = V.scalar_tensor_tensor(
                                        xs, yst[:, b, k * D:(k + 1) * D],
                                        gate[:, bass.ds(i, 1), e], xs, ALU.mult, ALU.add)
                                last.then_inc(s_yu, 1)
                                dve.drain()

                    @block.scalar
                    def _(act):
                        act.wait_ge(s_sq, 1)
                        nc.scalar.activation(s1[:, :, :], s1[:, :, :], ACT.Sqrt).then_inc(s_q, 1)
                        act.wait_ge(s_e2, 1)
                        nc.scalar.activation(gate[:, :, :], sc[:, :, :], ACT.Exp).then_inc(s_ex2, 1)

                    @block.sync
                    def _(sp):
                        for e in range(NE):
                            with sp.Fori(0, NG) as g:
                                sp.wait_ge(s_yu, g + (e * NG + 1))
                                sp.dma_start(yst[:, 0, :], y_d[e, :, bass.ds(g * (GT * D), GT * D)]).then_inc(s_y[0], 16)

        def stage_lin():
            tmp = ExitStack()

            def t(name, shape, dt=f32):
                return tmp.enter_context(nc.sbuf_tensor(name, shape, dt))

            with tmp:
                wt = t("lin_wt", [P, KD, D])
                br = t("lin_b", [P, D])
                sth = t("lin_sth", [P, GT, D])
                stt = t("lin_stt", [P, KD, GN])
                to = t("lin_out", [P, NT, D])
                s_w, s_h, s_t, s_c, s_y, s_o, s_d, s_o2 = (sem("lin_" + v) for v in ("w", "rows", "transposed", "staged", "made", "scaled", "stored", "biased"))
                with nc.psum_tensor("lin_pt", [P, KD, GN], f32) as pt, nc.psum_tensor("lin_py", [P, GT, D], f32) as py, \
                        nc.Block() as block:
                    @block.sync
                    def _(sp):
                        sp.dma_start(wt[:, :, :], a["L1_gnn_Wt"].rearrange("(c p) f -> p c f", p=P)).then_inc(s_w, 16)
                        sp.dma_start(br[:, :], a["L1_gnn_b"].partition_broadcast(P)).then_inc(s_w, 16)
                        sp.wait_ge(s_o, NT)
                        sp.dma_start(rows_d.rearrange("(t p) d -> p t d", p=P), to[:, :, :]).then_inc(s_d, 16)
                        sp.wait_ge(s_d, 16)

                    @block.vector
                    def _(dve):
                        dve.sem_inc(s_o2, 1)
                        dve.wait_ge(s_w, 32)
                        with dve.Fori(0, NG) as g:
                            dve.wait_ge(s_t, g + 1)
                            nc.vector.tensor_copy(sth[:, :, :], H[:, bass.ds(g * GT, GT), :]).then_inc(s_h, 1)
                            dve.wait_ge(s_y, g + 1 + 1)
                            nc.vector.tensor_tensor(to[:, bass.ds(g * GT, GT), :], py[:, :, :],
                                                    br[:, :].unsqueeze(1).to_broadcast([P, GT, D]), ALU.add).then_inc(s_o2, 1)
                            dve.drain()
                            for k in range(GT):
                                i = g * GT + k
                                o = to[:, bass.ds(i, 1), :].rearrange("p a b -> p (a b)")
                                nc.vector.tensor_scalar(o, o, norm[:, bass.ds(i, 1)], None, ALU.mult).then_inc(s_o, 1)

                    @block.scalar
                    def _(act):
                        with act.Fori(0, NG) as g:
                            act.wait_ge(s_t, g + 1 + 1)
                            act.wait_ge(s_y, g + 1)
                            nc.scalar.copy(stt[:, :, :], pt[:, :, :]).then_inc(s_c, 1)

                    @block.tensor
                    def _(pe):
                        pe.sem_inc(s_t, 1)
                        pe.sem_inc(s_y, 1)
                        pe.wait_ge(s_w, 32)
                        with pe.Fori(0, NG) as g:
                            pe.wait_ge(s_h, g + 1)
                            for k in range(GT):
                                for c in range(KD):
                                    last = nc.tensor.transpose(pt[:, c, k * P:(k + 1) * P], sth[:, k, c * P:(c + 1) * P], ident[:, :])
                            last.then_inc(s_t, 1)
                            pe.wait_ge(s_c, g + 1)
                            pe.wait_ge(s_o2, g + 1)
                            for k in range(GT):
                                for c in range(KD):
                                    last = nc.tensor.matmul(py[:, k, :], stt[:, c, k * P:(k + 1) * P], wt[:, c, :],
                                                            start=(c == 0), stop=(c == KD - 1))
                            last.then_inc(s_y, 1)

        def stage_add(acc):
            accv = acc[:, :].rearrange("p (t d) -> p t d", d=RW)
            with nc.Block() as block:
                @block.vector
                def _(dve):
                    with dve.Fori(0, NG) as g:
                        for k in range(GT):
                            i = g * GT + k
                            xs = X[:, bass.ds(i, 1), :].rearrange("p a b -> p (a b)")
                            nc.vector.scalar_tensor_tensor(xs, accv[:, bass.ds(i, 1), 0:D].rearrange("p a b -> p (a b)"),
                                                           norm[:, bass.ds(i, 1)], xs, ALU.mult, ALU.add)

        def stage_moe():
            tmp = ExitStack()

            def t(name, shape, dt=f32):
                return tmp.enter_context(nc.sbuf_tensor(name, shape, dt))

            with tmp:
                HT = t("moe_ht", [P, KD, NP])
                sth = t("moe_sth", [P, GT, D])
                wr = t("moe_wr", [P, KD, NE1])
                rw = t("moe_row", [1, 10, NE1])
                top = t("moe_top", [1, 8])
                topi = t("moe_topi", [1, 8], mybir.dt.uint32)
                wts = t("moe_wts", [1, 2])
                wcol = t("moe_wcol", [P, 2])
                mean = t("moe_mean", [P, KD])
                w1 = t("moe_w1", [P, 2, KD, F])
                w2 = t("moe_w2", [P, 2, KF, D])
                b1 = t("moe_b1", [P, 2, KF])
                b2 = t("moe_b2", [P, 2, D])
                bs = t("moe_bs", [P, D])
                gb = t("moe_gb", [P, 2, D])
                s_w, s_h, s_t, s_c = sem("moe_small"), sem("moe_rows"), sem("moe_transposed"), sem("moe_ht_copied")
                s_mn, s_mc, s_lg, s_rt = sem("moe_mean_made"), sem("moe_mean_copied"), sem("moe_logits"), sem("moe_routed")
                s_st, s_x, s_xd = sem("moe_step"), sem("moe_exp_in"), sem("moe_exp")
                s_wc, s_wcd, s_ld = sem("moe_weight_col"), sem("moe_pad2"), sem("moe_experts_loaded")
                with nc.psum_tensor("moe_pt", [P, KD, GN], f32) as pt, nc.psum_tensor("moe_pm", [P, 512], f32) as pm, \
                        nc.psum_tensor("moe_pw", [P, 512], f32) as pw, nc.Block() as block:
                    @block.sync
                    def _(sp):
                        sp.dma_start(wr[:, :, :], a["L1_ffn_Wr"].rearrange("(c p) e -> p c e", p=P)).then_inc(s_w, 16)
                        sp.dma_start(rw[:, 0, :], a["L1_ffn_br"].unsqueeze(0)).then_inc(s_w, 16)
                        sp.dma_start(gb[:, 0, :], a["L1_ffn_gamma"].partition_broadcast(P)).then_inc(s_w, 16)
                        sp.dma_start(gb[:, 1, :], a["L1_ffn_beta"].partition_broadcast(P)).then_inc(s_w, 16)
                        sp.wait_ge(s_rt, 1)
                        for j in range(2):
                            e = sp.value_load(topi[0:1, j:j + 1], min_val=0, max_val=NE1 - 1)
                            sp.dma_start(w1[:, j, :, :], a["L1_ffn_W1"][bass.ds(e, 1)].rearrange("o (c p) f -> p (o c) f", p=P)).then_inc(s_ld, 16)
                            sp.dma_start(w2[:, j, :, :], a["L1_ffn_W2"][bass.ds(e, 1)].rearrange("o (c p) f -> p (o c) f", p=P)).then_inc(s_ld, 16)
                            with nc.allow_non_contiguous_dma(reason="bias by feature"):
                                sp.dma_start(b1[:, j, :], a["L1_ffn_b1"][bass.ds(e, 1)].rearrange("o (c p) -> p (o c)", p=P)).then_inc(s_ld, 16)
                            sp.dma_start(b2[:, j, :], a["L1_ffn_b2"][bass.ds(e, 1)].to_broadcast([P, D])).then_inc(s_ld, 16)
                        sp.wait_ge(s_ld, 16 * 8)

                    @block.tensor
                    def _(pe):
                        pe.sem_inc(s_t, 1)
                        for c in range(KD):
                            for k in range(NT):
                                last = nc.tensor.matmul(pm[:, c:c + 1], H[:, k, c * P:(c + 1) * P],
                                                        valid[:, 1:2] if k == FULL else valid[:, 0:1],
                                                        start=(k == 0), stop=(k == NT - 1))
                        last.then_inc(s_mn, 1)
                        with pe.Fori(0, NG) as g:
                            pe.wait_ge(s_h, g + 1)
                            pe.wait_ge(s_c, g + 1)
                            for k in range(GT):
                                for c in range(KD):
                                    last = nc.tensor.transpose(pt[:, c, k * P:(k + 1) * P], sth[:, k, c * P:(c + 1) * P], ident[:, :])
                            last.then_inc(s_t, 1)
                        pe.wait_ge(s_w, 64)
                        pe.wait_ge(s_mc, 1)
                        for c in range(KD):
                            last = nc.tensor.matmul(pw[0:1, 0:NE1], mean[:, c:c + 1], wr[:, c, :], start=(c == 0), stop=(c == KD - 1))
                        last.then_inc(s_lg, 1)
                        pe.wait_ge(s_wc, 1)
                        nc.tensor.matmul(pm[:, 0:2], ones[0:1, :], wts[0:1, :], start=True, stop=True).then_inc(s_wcd, 1)

                    @block.vector
                    def _(dve):
                        dve.sem_inc(s_c, 1)
                        V = nc.vector
                        dve.wait_ge(s_mn, 1)
                        V.tensor_scalar(mean[:, :], pm[:, 0:KD], 1.0 / N, None, ALU.mult).then_inc(s_mc, 1)
                        with dve.Fori(0, NG) as g:
                            dve.wait_ge(s_t, g + 1)
                            V.tensor_copy(sth[:, :, :], H[:, bass.ds(g * GT, GT), :]).then_inc(s_h, 1)
                            dve.wait_ge(s_t, g + 1 + 1)
                            V.tensor_copy(HT[:, :, bass.ds(g * GN, GN)], pt[:, :, :]).then_inc(s_c, 1)
                        step = Chain(dve, s_st)

                        def softmax(src, dst, n, count):
                            step(V.tensor_reduce(rw[:, 9, 0:1], src, AX.X, ALU.max))
                            V.tensor_scalar(dst, src, rw[0:1, 9, 0:1], None, ALU.subtract).then_inc(s_x, 1)
                            dve.wait_ge(s_xd, count)
                            step(V.tensor_reduce(rw[:, 9, 0:1], dst, AX.X, ALU.add))
                            step(V.reciprocal(rw[:, 9, 1:2], rw[:, 9, 0:1]))
                            step(V.tensor_scalar(dst, dst, rw[0:1, 9, 1:2], None, ALU.mult))

                        dve.wait_ge(s_lg, 1)
                        step(V.tensor_tensor(rw[:, 1, :], rw[:, 0, :], pw[0:1, 0:NE1], ALU.add))
                        softmax(rw[:, 1, :], rw[:, 2, :], NE1, 1)
                        step(V.tensor_scalar(rw[:, 3, :], rw[:, 2, :], float(N), None, ALU.mult))
                        step(V.tensor_scalar(rw[:, 4, :], rw[:, 3, :], CAPACITY, None, ALU.is_gt))
                        step(V.tensor_scalar(rw[:, 3, :], rw[:, 3, :], CAPACITY, None, ALU.max))
                        step(V.reciprocal(rw[:, 5, :], rw[:, 3, :]))
                        step(V.tensor_scalar(rw[:, 5, :], rw[:, 5, :], CAPACITY, -1.0, ALU.mult, ALU.add))
                        step(V.tensor_tensor(rw[:, 5, :], rw[:, 5, :], rw[:, 4, :], ALU.mult))
                        step(V.tensor_scalar(rw[:, 5, :], rw[:, 5, :], 1.0, None, ALU.add))
                        step(V.tensor_tensor(rw[:, 6, :], rw[:, 2, :], rw[:, 5, :], ALU.mult))
                        softmax(rw[:, 6, :], rw[:, 7, :], NE1, 2)
                        step(V.max(top[:, :], rw[:, 7, :]))
                        V.max_index(topi[:, :], top[:, :], rw[:, 7, :]).then_inc(s_rt, 1)
                        softmax(top[:, 0:2], wts[:, :], 2, 3)
                        step(V.tensor_copy(wts[:, :], wts[:, :]))
                        V.tensor_copy(rw[:, 8, 0:2], wts[:, :]).then_inc(s_wc, 1)
                        dve.wait_ge(s_wcd, 1)
                        step(V.tensor_copy(wcol[:, :], pm[:, 0:2]))
                        dve.wait_ge(s_ld, 16 * 8)
                        for j in range(2):
                            V.tensor_scalar(w2[:, j, :, :].rearrange("p c f -> p (c f)"), w2[:, j, :, :].rearrange("p c f -> p (c f)"),
                                            wcol[:, j:j + 1], None, ALU.mult)
                        step(V.tensor_scalar(bs[:, :], b2[:, 0, :], wcol[:, 0:1], None, ALU.mult))
                        step(V.scalar_tensor_tensor(bs[:, :], b2[:, 1, :], wcol[:, 1:2], bs[:, :], ALU.mult, ALU.add))

                    @block.scalar
                    def _(act):
                        for k, v in enumerate((rw[:, 2, :], rw[:, 7, :], wts[:, :])):
                            act.wait_ge(s_x, k + 1)
                            nc.scalar.activation(v, v, ACT.Exp).then_inc(s_xd, 1)

                hh = t("moe_hh", [P, 2, KF, GN])
                os_ = t("moe_os", [P, 2, GT, D])
                HN = GN // 2
                mst = t("moe_st", [P, GT, 6])
                mmv = t("moe_mv", [P, GT, 2])
                msd = t("moe_sd", [P, GT])
                s_a, s_g, s_y, s_ye, s_sq, s_sr, s_o = (sem("moe_" + v) for v in (
                    "hidden", "gelu", "out", "out_added", "var", "std", "finished"))
                s_u, s_free = sem("moe_stored"), sem("moe_out_free")
                with nc.psum_tensor("moe_ps1", [P, 2, 2, 512], f32) as p1, nc.psum_tensor("moe_ps2", [P, 4, 512], f32) as p2, \
                        nc.Block() as block:
                    @block.tensor
                    def _(pe):
                        pe.sem_inc(s_y, 1)
                        with pe.Fori(0, NG) as g:
                            for e in range(2):
                                for m in range(KF):
                                    u = e * KF + m
                                    if u >= 2:
                                        pe.wait_ge(s_g, g * (2 * KF) + (u - 1) + 1)
                                    else:
                                        pe.wait_ge(s_g, g * (2 * KF) + 1)
                                    for n in range(2):
                                        for c in range(KD):
                                            last = nc.tensor.matmul(p1[:, u % 2, n, 0:HN], w1[:, e, c, m * P:(m + 1) * P],
                                                                    HT[:, c, bass.ds(g * GN + n * HN, HN)],
                                                                    start=(c == 0), stop=(c == KD - 1))
                                    last.then_inc(s_a, 1)
                            pe.wait_ge(s_g, (g + 1) * (2 * KF) + 1)
                            for k in range(GT):
                                if k >= 4:
                                    pe.wait_ge(s_ye, g * GT + (k - 3) + 1)
                                else:
                                    pe.wait_ge(s_ye, g * GT + 1)
                                for e in range(2):
                                    for c in range(KF):
                                        last = nc.tensor.matmul(p2[:, k % 4, 0:D], hh[:, e, c, k * P:(k + 1) * P], w2[:, e, c, :],
                                                                start=(e == 0 and c == 0), stop=(e == 1 and c == KF - 1))
                                last.then_inc(s_y, 1)

                    @block.scalar
                    def _(act):
                        act.sem_inc(s_g, 1)
                        with act.Fori(0, NG) as g:
                            act.wait_ge(s_y, g * GT + 1)
                            for e in range(2):
                                for m in range(KF):
                                    u = e * KF + m
                                    act.wait_ge(s_a, g * (2 * KF) + (u + 1))
                                    nc.scalar.activation(hh[:, e, m, :].rearrange("p (n k) -> p n k", n=2), p1[:, u % 2, :, 0:HN], ACT.Gelu,
                                                         bias=b1[:, e, m:m + 1]).then_inc(s_g, 1)
                            act.wait_ge(s_sq, g + 1)
                            nc.scalar.activation(msd[:, :], mmv[:, :, 1], ACT.Sqrt).then_inc(s_sr, 1)

                    @block.vector
                    def _(dve):
                        dve.sem_inc(s_ye, 1)
                        V = nc.vector
                        with dve.Fori(0, NG) as g:
                            ot = os_[:, 0, :, :]
                            dve.wait_ge(s_free, g + 1)
                            tl = bass.ds(g * GT, GT)
                            V.tensor_tensor(os_[:, 1, :, :], H[:, tl, :], bs[:, :].unsqueeze(1).to_broadcast([P, GT, D]), ALU.add)
                            dve.drain()
                            for k in range(GT):
                                dve.wait_ge(s_y, g * GT + (k + 1) + 1)
                                V.tensor_tensor(ot[:, k, :], p2[:, k % 4, 0:D], os_[:, 1, k, :], ALU.add).then_inc(s_ye, 1)
                            dve.drain()
                            for k in range(GT):
                                V.bn_stats(mst[:, k, :], ot[:, k, :])
                            dve.drain()
                            for k in range(GT):
                                V.bn_aggr(mmv[:, k, :], mst[:, k, :])
                            dve.drain()
                            V.tensor_scalar(mmv[:, :, 1], mmv[:, :, 1], EPS, None, ALU.add).then_inc(s_sq, 1)
                            dve.wait_ge(s_sr, g + 1)
                            V.reciprocal(msd[:, :], msd[:, :])
                            dve.drain()
                            for k in range(GT):
                                V.tensor_scalar(ot[:, k, :], ot[:, k, :], mmv[:, k, 0:1], msd[:, k:k + 1], ALU.subtract, ALU.mult)
                            dve.drain()
                            V.tensor_tensor(ot, ot, gb[:, 0, :].unsqueeze(1).to_broadcast([P, GT, D]), ALU.mult)
                            dve.drain()
                            V.tensor_tensor(ot, ot, gb[:, 1, :].unsqueeze(1).to_broadcast([P, GT, D]), ALU.add)
                            dve.drain()
                            V.tensor_tensor(ot, ot, X[:, tl, :], ALU.add).then_inc(s_o, 1)

                    @block.sync
                    def _(sp):
                        sp.sem_inc(s_free, 1)
                        of = out[0:FULL * P, :].rearrange("(t p) d -> p t d", p=P)
                        with sp.Fori(0, NG - 1) as g:
                            sp.wait_ge(s_o, g + 1)
                            sp.dma_start(of[:, bass.ds(g * GT, GT), :], os_[:, 0, :, :]).then_inc(s_u, 32)
                            sp.wait_ge(s_u, (g + 1) * 32)
                            sp.sem_inc(s_free, 1)
                        g = NG - 1
                        sp.wait_ge(s_o, NG)
                        sp.dma_start(of[:, g * GT:FULL, :], os_[:, 0, 0:GT - 1, :]).then_inc(s_u, 16)
                        sp.dma_start(out[FULL * P:N, :], os_[0:TAIL, 0, GT - 1, :]).then_inc(s_u, 16)
                        sp.wait_ge(s_u, 32 * NG)

        stage_consts()
        rows_norm("ln0", load=True, table=True)
        end_stage()
        stage_sort()
        end_stage()
        with nc.sbuf_tensor("acc0", [P, NT * RW], f32) as acc:
            message_pass("mp0", acc)
            stage_gin(acc)
        end_stage()
        rows_norm("ln1")
        stage_gat()
        end_stage()
        rows_norm("ln2")
        stage_lin()
        with nc.sbuf_tensor("acc1", [P, NT * RW], f32) as acc:
            message_pass("mp1", acc)
            stage_add(acc)
        end_stage()
        rows_norm("ln3")
        stage_moe()


_INS = ['x', 'src', 'dst', 'L0_gnn_W1', 'L0_gnn_b1', 'L0_gnn_g1', 'L0_gnn_bt1', 'L0_gnn_W2', 'L0_gnn_b2',
        'L0_gnn_g2', 'L0_gnn_bt2', 'L0_gnn_eps_gin', 'L0_ffn_W_gat', 'L0_ffn_att_src', 'L0_ffn_att_dst',
        'L0_ffn_b_gat', 'L0_ffn_ln_gamma', 'L0_ffn_ln_beta', 'L0_ffn_W1', 'L0_ffn_b1', 'L0_ffn_W2', 'L0_ffn_b2',
        'L0_ffn_edge_index', 'L1_gnn_W', 'L1_gnn_b', 'L1_ffn_Wr', 'L1_ffn_br', 'L1_ffn_W1', 'L1_ffn_b1',
        'L1_ffn_W2', 'L1_ffn_b2', 'L1_ffn_gamma', 'L1_ffn_beta']


def kernel(**inputs):
    import numpy as _np
    import concourse.bacc as _bacc
    from concourse import mybir as _mybir
    from concourse.bass_utils import run_bass_kernel_spmd as _run

    nc = _bacc.Bacc("TRN2", target_bir_lowering=False, num_devices=1)
    arrays, aps = {}, {}
    for name in _INS:
        v = _np.asarray(inputs[name])
        if name == "L1_gnn_W":
            name, v = "L1_gnn_Wt", v.T
        if name == "L0_gnn_eps_gin":
            v = v.reshape(1)
        v = _np.ascontiguousarray(v)
        arrays["in_" + name] = v
        aps[name] = nc.dram_tensor("in_" + name, v.shape, _mybir.dt.from_np(v.dtype), kind="ExternalInput").ap()
    out = nc.dram_tensor("out_0", (N, D), _mybir.dt.float32, kind="ExternalOutput").ap()
    build(nc, aps, out)
    r = _run(nc, [arrays], core_ids=[0])
    return r.results[0]["out_0"]
```

```python
import numpy as np
import concourse.bass as bass
from concourse import mybir
from contextlib import ExitStack

f32 = mybir.dt.float32
bf16 = mybir.dt.bfloat16
i32 = mybir.dt.int32
ALU = mybir.AluOpType
ACT = mybir.ActivationFunctionType
AX = mybir.AxisListType

P = 128
N = 3125
D = 256
KD = D // P
F = 512
KF = F // P
NT = -(-N // P)
NP = NT * P
FULL = N // P
TAIL = N - FULL * P
GT = 5
NG = NT // GT
GN = GT * P
CH = 512
NCH = N // CH
CTAIL = N - NCH * CH

E1 = 50000
ET = 400
EROWS = E1 // ET
NB = NT + 1
PAD_DST = NT * P
HIST = NB * ET
HCH = 512
HCHUNKS = 3 * (-(-HIST // (3 * HCH)))
HISTP = HCHUNKS * HCH
TILES = P * ET // P
TCH = -(-TILES // P)
TLAST = TILES - (TCH - 1) * P
HALF = 8
UNIT = 4
RING = 8
AHEAD = 4
MAXSLOTS = -(-E1 // P) + NT - 1
ITERS = -(-MAXSLOTS // (UNIT * RING))
SLOTS = ITERS * UNIT * RING
SLOTSP = SLOTS + AHEAD * UNIT
RW = D + 1

E2 = 32768
ET2 = E2 // P
NE = 4
STEPS = NG * NE
STEP = -(-ET2 // STEPS)
STEP_END = ET2 - (STEPS - 1) * STEP
ET2P = STEPS * STEP
PARTS = 3
HEADS = 4
HK = HEADS * NE
TW = HK + HEADS
DW = 2 * HEADS
NE1 = 8
CAPACITY = float(-(-N * 5 // (4 * NE1)))
EPS = 1e-5


class Chain:

    def __init__(self, eng, sem):
        self.eng, self.sem, self.n = eng, sem, 0

    def __call__(self, ins):
        self.n += 1
        ins.then_inc(self.sem, 1)
        self.eng.wait_ge(self.sem, self.n)


def build(nc, a, out):
    ctx = ExitStack()
    names = set()
    stage_sems = []

    def sb(name, shape, dt=f32):
        return ctx.enter_context(nc.sbuf_tensor(name, shape, dt))

    def sem(name):
        assert name not in names
        names.add(name)
        stage_sems.append(nc.alloc_semaphore(name))
        return stage_sems[-1]

    def end_stage():
        nc.clear_and_free_semaphores(stage_sems)
        nc.all_engine_barrier()
        del stage_sems[:]

    def dram(name, shape, dt=f32):
        return nc.dram_tensor(name, shape, dt, kind="Internal").ap()

    with ctx:
        scattered = [ctx.enter_context(nc.semaphore(f"scattered_{k}")) for k in range(2 * HALF)]
        gathered = [ctx.enter_context(nc.semaphore(f"gathered_{k}")) for k in range(4 * STEP)]
        done = [0] * len(gathered)
        x_d = a["x"]
        edges_d = dram("edges_sorted", [P * ET, 2], i32)
        rows_d = dram("rows_table", [NP, D])
        srct_d = dram("gat_src_table", [NP, TW])
        dstt_d = dram("gat_dst_table", [NP, DW])
        y_d = dram("expert_outputs", [NE, P, NT * D])

        iota = sb("iota", [P, P])
        pidx = sb("pidx", [P, 1])
        ident = sb("ident", [P, P])
        tri = sb("tri", [P, P], bf16)
        ones_bf = sb("ones_bf", [P, P], bf16)
        ones = sb("ones", [P, P])
        valid = sb("valid", [P, 2])
        X = sb("X", [P, NT, D])
        h_room = sb("H", [P, NT * D])
        H = h_room[:, :].rearrange("p (t d) -> p t d", d=D)
        stats = sb("stats", [P, NT, 6])
        mv = sb("mv", [P, NT, 2])
        rstd = sb("rstd", [P, NT])
        eps_col = sb("eps_col", [P, 1])
        norm = sb("norm", [P, NT])
        slot_src = sb("slot_src", [P, SLOTS], i32)
        slot_dst = sb("slot_dst", [P, SLOTSP])
        slot_bkt = sb("slot_bkt", [1, SLOTS // UNIT], i32)

        def stage_consts():
            s_iota, s_c = sem("iota_made"), sem("const_step")
            with nc.sbuf_tensor("iota_i", [P, P], i32) as iota_i, nc.sbuf_tensor("pidx_i", [P, 1], i32) as pidx_i, \
                    nc.Block() as block:
                @block.gpsimd
                def _(pool):
                    nc.gpsimd.iota(iota_i[:, :], [[1, P]], base=0, channel_multiplier=0).then_inc(s_iota, 1)
                    nc.gpsimd.iota(pidx_i[:, :], [[1, 1]], base=0, channel_multiplier=1).then_inc(s_iota, 1)

                @block.vector
                def _(dve):
                    step = Chain(dve, s_c)
                    nc.vector.memset(ones[:, :], 1.0)
                    nc.vector.memset(ones_bf[:, :], 1.0)
                    nc.vector.memset(eps_col[:, :], EPS)
                    nc.vector.memset(valid[:, :], 1.0)
                    dve.wait_ge(s_iota, 2)
                    nc.vector.tensor_copy(iota[:, :], iota_i[:, :])
                    step(nc.vector.tensor_copy(pidx[:, :], pidx_i[:, :]))
                    nc.vector.tensor_scalar(ident[:, :], iota[:, :], pidx[:, 0:1], None, ALU.is_equal)
                    nc.vector.tensor_scalar(tri[:, :], iota[:, :], pidx[:, 0:1], None, ALU.is_gt)
                    nc.vector.tensor_scalar(valid[:, 1:2], pidx[:, :], float(TAIL), None, ALU.is_lt)

        def row_stats(i):
            return nc.vector.bn_stats(tile_of(stats, i), tile_of(X, i))

        def row_moments(dve, tag, s_mv, s_std, have_stats=False):
            if not have_stats:
                with dve.Fori(0, NG) as g:
                    for k in range(GT):
                        row_stats(g * GT + k)
                dve.drain()
            step = Chain(dve, sem(tag + "_moment_step"))
            mean_e, sq_e, mean_o, sq_o = (stats[:, :, k] for k in (1, 2, 4, 5))
            nc.vector.tensor_tensor(sq_e, sq_e, sq_o, ALU.add)
            nc.vector.tensor_tensor(mv[:, :, 0], mean_e, mean_o, ALU.add)
            step(nc.vector.tensor_tensor(mean_e, mean_e, mean_o, ALU.subtract))
            nc.vector.tensor_scalar(mv[:, :, 0], mv[:, :, 0], 0.5, None, ALU.mult)
            nc.vector.tensor_scalar(sq_e, sq_e, 1.0 / D, EPS, ALU.mult, ALU.add)
            step(nc.vector.tensor_tensor(mean_o, mean_e, mean_e, ALU.mult))
            nc.vector.scalar_tensor_tensor(mv[:, :, 1], mean_o, 0.25, sq_e, ALU.mult, ALU.add).then_inc(s_mv, 1)
            dve.wait_ge(s_std, 1)
            nc.vector.reciprocal(rstd[:, :], rstd[:, :])
            dve.drain()

        def row_deviations(act, s_mv, s_std):
            act.wait_ge(s_mv, 1)
            nc.scalar.activation(rstd[:, :], mv[:, :, 1], ACT.Sqrt).then_inc(s_std, 1)

        def normalise(to, i):
            return nc.vector.tensor_scalar(to, X[:, bass.ds(i, 1), :].rearrange("p a b -> p (a b)"),
                                           mv[:, bass.ds(i, 1), 0], rstd[:, bass.ds(i, 1)], ALU.subtract, ALU.mult)

        def tile_of(buf, i):
            return buf[:, bass.ds(i, 1), :].rearrange("p a b -> p (a b)")

        def columns_of(buf, i):
            return buf[:, :, bass.ds(i * P, P)]

        def transpose_tile(to, rows):
            for c in range(KD):
                last = nc.tensor.transpose(to[:, c * P:(c + 1) * P], rows[:, c * P:(c + 1) * P], ident[:, :])
            return last

        by_chunk = lambda ap: ap.rearrange("p (c n) -> p c n", c=KD)
        BANK = [k % 3 for k in range(GT)]

        def stage_start(acc):
            tmp = ExitStack()

            def t(name, shape, dt=f32):
                return tmp.enter_context(nc.sbuf_tensor(name, shape, dt))

            with tmp:
                dst_i = t("dst_i", [P, ET], i32)
                nxt_i = t("nxt_i", [P, ET], i32)
                src_i = t("src_i", [P, ET], i32)
                hi = t("hi", [P, ET], bf16)
                falls = t("falls", [P, 1 + NB])
                pair = t("pair", [P, ET, 2], i32)
                onehot = t("onehot", [P, HISTP], bf16)
                bkt0 = t("bkt0", [1, NB + 1])
                falls_i = t("falls_i", [1, 1], i32)
                ps = tmp.enter_context(nc.psum_tensor("ps_sort", [P, 8, 512], f32))

                s_pad, s_ld, s_st = sem("sort_pad"), sem("sort_loaded"), sem("sort_step")
                s_x, s_mv, s_std, s_h, s_t = (sem("ln0_" + v) for v in ("x", "stats", "std", "h", "table"))
                s_cnt, s_sum, s_pair, s_id = sem("counted"), sem("counts_summed"), sem("pairs_made"), sem("identity_stored")
                with nc.sbuf_tensor("half", [P, NB, ET // 2], bf16) as half, nc.Block() as block:
                    @block.sync
                    def _(sp):
                        sp.wait_ge(s_pad, 4)
                        sp.dma_start(dst_i[0:EROWS, :], a["dst"].rearrange("(p t) -> p t", t=ET)).then_inc(s_ld, 16)
                        sp.dma_start(nxt_i[0:EROWS - 1, :],
                                     a["dst"][1:E1 - ET + 1].rearrange("(p t) -> p t", t=ET)).then_inc(s_ld, 16)
                        sp.dma_start(nxt_i[EROWS - 1:EROWS, 0:ET - 1], a["dst"][E1 - ET + 1:E1].unsqueeze(0)).then_inc(s_ld, 16)
                        sp.dma_start(src_i[0:EROWS, :], a["src"].rearrange("(p t) -> p t", t=ET)).then_inc(s_ld, 16)
                        sp.dma_start(X[:, 0:FULL, :], x_d[0:FULL * P, :].rearrange("(t p) d -> p t d", p=P)).then_inc(s_x, 16)
                        sp.dma_start(X[0:TAIL, FULL, :], x_d[FULL * P:N, :]).then_inc(s_x, 16)
                        sp.wait_ge(s_pair, 1)
                        sp.dma_start(edges_d.rearrange("(p t) k -> p t k", t=ET), pair[:, :, :]).then_inc(s_id, 16)
                        with sp.Fori(0, NG) as g:
                            sp.wait_ge(s_h, g * GT + GT)
                            tl = bass.ds(g * GT, GT)
                            sp.dma_start(rows_d.rearrange("(t p) d -> p t d", p=P)[:, tl, :], H[:, tl, :]).then_inc(s_t, 16)
                        sp.wait_ge(s_id, 16)

                    @block.gpsimd
                    def _(pool):
                        nc.gpsimd.memset(acc[:, :], 0.0)

                    @block.vector
                    def _(dve):
                        step = Chain(dve, s_st)
                        V = nc.vector
                        V.memset(dst_i[:, :], PAD_DST).then_inc(s_pad, 1)
                        V.memset(nxt_i[:, :], PAD_DST).then_inc(s_pad, 1)
                        V.memset(src_i[:, :], 0).then_inc(s_pad, 1)
                        V.memset(X[:, FULL, :], 0.0).then_inc(s_pad, 1)
                        V.memset(onehot[:, HIST:HISTP], 0.0)
                        dve.wait_ge(s_ld, 64)
                        V.tensor_copy(pair[:, :, 0], src_i[:, :])
                        V.tensor_copy(pair[:, :, 1], dst_i[:, :]).then_inc(s_pair, 1)
                        V.tensor_scalar(nxt_i[:, :], nxt_i[:, :], 7, None, ALU.logical_shift_right)
                        step(V.tensor_scalar(dst_i[:, :], dst_i[:, :], 7, None, ALU.logical_shift_right))
                        step(V.tensor_copy(hi[:, :], dst_i[:, :]))
                        V.tensor_tensor(src_i[:, :], nxt_i[:, :], dst_i[:, :], ALU.is_lt)
                        for b in range(NB):
                            V.tensor_scalar(onehot[:, b * ET:(b + 1) * ET], hi[:, :], float(b), None, ALU.is_equal)
                        dve.drain()
                        w = ET // 2
                        src = onehot[:, 0:HIST].rearrange("p (b t) -> p b t", t=ET)
                        for level in range(3):
                            step(V.tensor_tensor(half[:, :, 0:w], src[:, :, 0:w], src[:, :, w:2 * w], ALU.add))
                            src, w = half, w // 2
                        V.tensor_reduce(falls[:, 0:1], src_i[:, :], AX.X, ALU.add)
                        V.tensor_reduce(falls[:, 1:1 + NB], half[:, :, 0:2 * w], AX.X, ALU.add).then_inc(s_cnt, 1)
                        V.memset(bkt0[:, 0:1], 0.0)
                        dve.wait_ge(s_sum, 1)
                        V.tensor_copy(falls_i[:, :], ps[0:1, 0, 0:1])
                        V.tensor_tensor_scan(bkt0[:, 1:1 + NB], ones[0:1, 0:1].to_broadcast([1, NB]),
                                             ps[0:1, 0, 1:1 + NB], 0.0, ALU.mult, ALU.add)
                        dve.wait_ge(s_x, 32)
                        row_moments(dve, "ln0", s_mv, s_std)
                        with dve.Fori(0, NG) as g:
                            for k in range(GT):
                                normalise(tile_of(H, g * GT + k), g * GT + k).then_inc(s_h, 1)

                    @block.scalar
                    def _(act):
                        row_deviations(act, s_mv, s_std)

                    @block.tensor
                    def _(pe):
                        pe.wait_ge(s_cnt, 1)
                        nc.tensor.matmul(ps[:, 0, 0:1 + NB], ones[:, :], falls[:, :], start=True, stop=True).then_inc(s_sum, 1)

                with ExitStack() as big:
                    before = big.enter_context(nc.sbuf_tensor("before", [P, HISTP], bf16))
                    total = big.enter_context(nc.sbuf_tensor("total", [P, HISTP], bf16))
                    start = big.enter_context(nc.sbuf_tensor("start", [P, 1 + HISTP], f32))
                    pos_f = big.enter_context(nc.sbuf_tensor("pos_f", [P, ET], f32))
                    pos_i = big.enter_context(nc.sbuf_tensor("pos_i", [P, ET], i32))
                    st_pos = big.enter_context(nc.sbuf_tensor("st_pos", [P, 2 * HALF], i32))
                    st_pair = big.enter_context(nc.sbuf_tensor("st_pair", [P, 2 * HALF, 2], i32))
                    s_ct, s_pst = sem("counts_made"), sem("position_step")
                    s_be, s_to = sem("before_copied"), sem("total_copied")
                    s_pos, s_begun = sem("positions_made"), sem("scatter_begun")
                    s_stg = [sem("scatter_staged_a"), sem("scatter_staged_b")]
                    flat = lambda ap: ap.rearrange("p b t -> p (b t)")
                    with nc.Block() as block:
                        def unsorted(eng):
                            return eng.If(eng.value_load(falls_i[0:1, 0:1], min_val=0, max_val=P * ET) > 0)

                        @block.vector
                        def _(dve):
                            with unsorted(dve):
                                step = Chain(dve, s_pst)
                                dve.sem_inc(s_to, 1)
                                nc.vector.memset(start[:, 0:1], 0.0)
                                with dve.Fori(0, HCHUNKS // 3) as i:
                                    dve.wait_ge(s_ct, 3 * i + 3)
                                    nc.vector.tensor_copy(total[:, bass.ds(i * (3 * HCH), 3 * HCH)],
                                                          flat(ps[:, 3:6, :])).then_inc(s_to, 1)
                                dve.wait_ge(s_to, HCHUNKS // 3 + 1)
                                step(nc.vector.tensor_tensor_scan(
                                    start[:, 1:1 + HIST], ones[:, 0:1].to_broadcast([P, HIST]), total[:, 0:HIST],
                                    0.0, ALU.mult, ALU.add))
                                dve.wait_ge(s_be, HCHUNKS // 3 + 1)
                                starts = start[:, 0:HIST]
                                step(nc.vector.tensor_tensor(starts, starts, before[:, 0:HIST], ALU.add))
                                step(nc.vector.tensor_tensor(starts, starts, onehot[:, 0:HIST], ALU.mult))
                                step(nc.vector.tensor_reduce(
                                    pos_f[:, :], starts.rearrange("p (b t) -> p t b", t=ET), AX.X, ALU.add))
                                nc.vector.tensor_copy(pos_i[:, :], pos_f[:, :]).then_inc(s_pos, 1)

                        @block.tensor
                        def _(pe):
                            with unsorted(pe):
                                with pe.Fori(0, HCHUNKS // 3) as i:
                                    pe.wait_ge(s_be, i + 1)
                                    pe.wait_ge(s_to, i + 1)
                                    for k in range(3):
                                        rhs = onehot[:, bass.ds(i * (3 * HCH) + k * HCH, HCH)]
                                        nc.tensor.matmul(ps[:, k, :], tri[:, :], rhs, start=True, stop=True)
                                        nc.tensor.matmul(ps[:, 3 + k, :], ones_bf[:, :], rhs, start=True,
                                                         stop=True).then_inc(s_ct, 1)

                        @block.scalar
                        def _(act):
                            with unsorted(act):
                                act.sem_inc(s_be, 1)
                                with act.Fori(0, HCHUNKS // 3) as i:
                                    act.wait_ge(s_ct, 3 * i + 3)
                                    nc.scalar.copy(before[:, bass.ds(i * (3 * HCH), 3 * HCH)],
                                                   flat(ps[:, 0:3, :])).then_inc(s_be, 1)
                                act.wait_ge(s_pos, 1)

                                def put(h, at):
                                    r = slice(h * HALF, (h + 1) * HALF)
                                    nc.scalar.copy(st_pos[:, r], pos_i[:, bass.ds(at, HALF)])
                                    nc.scalar.copy(st_pair[:, r, :], pair[:, bass.ds(at, HALF), :]).then_inc(s_stg[h], 1)

                                for h in range(2):
                                    put(h, h * HALF)
                                with act.Fori(0, ET // (2 * HALF) - 1) as i:
                                    for h in range(2):
                                        for k in range(h * HALF, (h + 1) * HALF):
                                            act.wait_ge(scattered[k], i * 16 + 16)
                                        put(h, (i + 1) * (2 * HALF) + h * HALF)

                        @block.gpsimd
                        def _(pool):
                            with unsorted(pool):
                                with pool.Fori(0, ET // (2 * HALF)) as i:
                                    for h in range(2):
                                        pool.wait_ge(s_stg[h], i + 1)
                                        pool.sem_inc(s_begun, 1)
                                        for k in range(h * HALF, (h + 1) * HALF):
                                            pool.indirect_dma_start(
                                                out=edges_d, out_offset=bass.IndirectOffsetOnAxis(ap=st_pos[:, k:k + 1], axis=0),
                                                in_=st_pair[:, k, :], in_offset=None).then_inc(scattered[k], 16)
                                for k in range(2 * HALF):
                                    pool.wait_ge(scattered[k], 16 * ET // (2 * HALF))

                row = t("row", [1, 6, NB])
                bnd = t("bnd", [1, 2, NB], i32)
                col3 = t("col3", [P, 3])
                wid = t("wid", [P, 2, P])
                iota_j = t("iota_j", [P, SLOTS])
                iota_ji = t("iota_ji", [P, SLOTS], i32)
                selb = t("selb", [P, SLOTS])
                tile_j = t("tile_j", [P, SLOTS])
                bkt_j = t("bkt_j", [P, SLOTS])
                val_j = t("val_j", [P, SLOTS])
                nat_i = t("nat_i", [P, TCH, 2 * P], i32)
                nat = t("nat", [P, TCH, 2 * P])
                tcol = t("tcol", [P, TCH])
                sel = t("sel", [P, TCH, SLOTS])
                pk = t("pk", [1, SLOTS])
                s_ij, s_nat, s_sl = sem("iota_j_made"), sem("sorted_loaded"), sem("slot_step")
                s_c3, s_row, s_sb = sem("cols_made"), sem("rows_made"), sem("bucket_sel")
                s_wid, s_npad = sem("wide_made"), sem("sorted_pad")
                s_sel, s_slot = sem("tile_sel"), sem("slots_made")
                with nc.Block() as block:
                    @block.gpsimd
                    def _(pool):
                        nc.gpsimd.iota(iota_ji[:, :], [[1, SLOTS]], base=0, channel_multiplier=0).then_inc(s_ij, 1)

                    @block.sync
                    def _(sp):
                        sp.wait_ge(s_t, 16 * NG)
                        full = (TCH - 1) * P * P
                        sp.dma_start(nat_i[:, 0:TCH - 1, :],
                                     edges_d[0:full, :].rearrange("(c p e) k -> p c (e k)", p=P, e=P)).then_inc(s_nat, 16)
                        sp.wait_ge(s_npad, 1)
                        sp.dma_start(nat_i[0:TLAST, TCH - 1, :],
                                     edges_d[full:P * ET, :].rearrange("(p e) k -> p (e k)", e=P)).then_inc(s_nat, 16)

                    @block.vector
                    def _(dve):
                        step = Chain(dve, s_sl)
                        V = nc.vector
                        V.memset(nat_i[:, TCH - 1, :], PAD_DST).then_inc(s_npad, 1)
                        V.memset(col3[:, :], 0.0)
                        V.memset(slot_dst[:, SLOTS:SLOTSP], -1.0)
                        first, last, count, end, begin, off = (row[:, k, 0:NT] for k in range(6))
                        b0, b1 = bkt0[:, 0:NT], bkt0[:, 1:NT + 1]
                        step(V.tensor_copy(bnd[:, 0, 0:NT], b0))
                        step(V.tensor_scalar(last, b1, -1.0, None, ALU.add))
                        step(V.tensor_copy(bnd[:, 1, 0:NT], last))
                        V.tensor_scalar(bnd[:, 0, 0:NT], bnd[:, 0, 0:NT], 7, None, ALU.logical_shift_right)
                        step(V.tensor_scalar(bnd[:, 1, 0:NT], bnd[:, 1, 0:NT], 7, None, ALU.arith_shift_right))
                        V.tensor_copy(first, bnd[:, 0, 0:NT])
                        V.tensor_tensor(off, b1, b0, ALU.is_gt)
                        step(V.tensor_copy(last, bnd[:, 1, 0:NT]))
                        step(V.tensor_tensor(count, last, first, ALU.subtract))
                        step(V.scalar_tensor_tensor(count, count, 1.0, off, ALU.add, ALU.mult))
                        step(V.tensor_tensor_scan(end, ones[0:1, 0:1].to_broadcast([1, NT]), count, 0.0, ALU.mult, ALU.add))
                        step(V.tensor_tensor(begin, end, count, ALU.subtract))
                        V.tensor_tensor(off, first, begin, ALU.subtract).then_inc(s_row, 1)
                        dve.wait_ge(s_ij, 1)
                        step(V.tensor_copy(iota_j[:, :], iota_ji[:, :]))
                        dve.wait_ge(s_c3, 1)
                        step(V.tensor_copy(col3[0:NT, :], ps[0:NT, 0, 0:3]))
                        V.tensor_copy(wid[:, 0, :], col3[:, 2:3].to_broadcast([P, P]))
                        V.tensor_copy(wid[:, 1, :], pidx[:, 0:1].to_broadcast([P, P]))
                        step(V.tensor_scalar(tile_j[:, :], iota_j[:, :], col3[:, 0:1], None, ALU.is_lt))
                        V.scalar_tensor_tensor(selb[:, :], iota_j[:, :], col3[:, 1:2], tile_j[:, :], ALU.is_ge,
                                               ALU.mult).then_inc(s_wid, 1)
                        for c in range(TCH):
                            V.tensor_scalar(tcol[:, c:c + 1], pidx[:, :], float(c * P), None, ALU.add)
                        dve.wait_ge(s_nat, 32)
                        V.tensor_copy(nat[:, :, :], nat_i[:, :, :])
                        dve.wait_ge(s_sb, 1)
                        V.tensor_copy(bkt_j[:, :], ps[:, 2, 0:SLOTS])
                        V.tensor_scalar(val_j[:, :], ps[:, 3, 0:SLOTS], -1.0, 4096.0, ALU.add, ALU.mult)
                        step(V.tensor_tensor(tile_j[:, :], iota_j[:, :], ps[:, 1, 0:SLOTS], ALU.add))
                        step(V.tensor_tensor(tile_j[:, :], tile_j[:, :], val_j[:, :], ALU.add))
                        for c in range(TCH):
                            last_sel = V.tensor_scalar(sel[:, c, :], tile_j[:, :], tcol[:, c:c + 1], None, ALU.is_equal)
                        last_sel.then_inc(s_sel, 1)
                        pv = pk[:, :].rearrange("p (q k) -> p q k", k=UNIT)
                        bv = bkt_j[0:1, :].rearrange("p (q k) -> p q k", k=UNIT)
                        step(V.tensor_copy(pv[:, :, 0], bv[:, :, UNIT - 1]))
                        for k in range(UNIT - 2, -1, -1):
                            step(V.scalar_tensor_tensor(pv[:, :, 0], pv[:, :, 0], 32.0, bv[:, :, k], ALU.mult, ALU.add))
                        V.tensor_copy(slot_bkt[:, :], pv[:, :, 0])
                        step(V.scalar_tensor_tensor(bkt_j[:, :], bkt_j[:, :], -float(P), val_j[:, :], ALU.mult, ALU.add))
                        dve.wait_ge(s_slot, 1)
                        V.tensor_copy(slot_src[:, :], ps[:, 4, 0:SLOTS])
                        V.tensor_tensor(slot_dst[:, 0:SLOTS], ps[:, 5, 0:SLOTS], bkt_j[:, :], ALU.add)

                    @block.tensor
                    def _(pe):
                        pe.wait_ge(s_row, 1)
                        for k in range(3):
                            last = nc.tensor.matmul(ps[0:NT, 0, k:k + 1], row[0:1, 3 + k, 0:NT], ones[0:1, 0:1],
                                                    start=True, stop=True)
                        last.then_inc(s_c3, 1)
                        pe.wait_ge(s_wid, 1)
                        nc.tensor.matmul(ps[:, 1, 0:SLOTS], wid[0:NT, 0, :], selb[0:NT, :], start=True, stop=True)
                        nc.tensor.matmul(ps[:, 2, 0:SLOTS], wid[0:NT, 1, :], selb[0:NT, :], start=True, stop=True)
                        nc.tensor.matmul(ps[:, 3, 0:SLOTS], ones[0:NT, :], selb[0:NT, :], start=True,
                                         stop=True).then_inc(s_sb, 1)
                        pe.wait_ge(s_sel, 1)
                        for k in range(2):
                            for c in range(TCH):
                                lhs = nat[:, c, :].rearrange("p (e k) -> p e k", k=2)[:, :, k]
                                last = nc.tensor.matmul(ps[:, 4 + k, 0:SLOTS], lhs, sel[:, c, :],
                                                        start=(c == 0), stop=(c == TCH - 1))
                        last.then_inc(s_slot, 1)

        def message_pass(tag, acc):
            tmp = ExitStack()
            with tmp:
                NR = UNIT * RING
                rows = tmp.enter_context(nc.sbuf_tensor(tag + "_rows", [P, NR, RW], f32))
                hot = tmp.enter_context(nc.sbuf_tensor(tag + "_hot", [P, NR, P], f32))
                idx = tmp.enter_context(nc.sbuf_tensor(tag + "_idx", [P, NR], i32))
                drel = tmp.enter_context(nc.sbuf_tensor(tag + "_drel", [P, NR], f32))
                ps = tmp.enter_context(nc.psum_tensor(tag + "_ps", [P, 2 * UNIT, 512], f32))
                s_idx, s_hot, s_mm, s_acc = (sem(tag + v) for v in ("_idx", "_hot", "_summed", "_added"))
                s_one, s_begun = sem(tag + "_ones"), sem(tag + "_begun")
                base_of = done[:]
                for k in range(NR):
                    done[k] += 16 * ITERS
                places = lambda u: slice(u * UNIT, (u + 1) * UNIT)
                with nc.Block() as block:
                    @block.scalar
                    def _(act):
                        def put(u, at):
                            nc.scalar.copy(drel[:, places(u)], slot_dst[:, bass.ds(at, UNIT)])
                            nc.scalar.copy(idx[:, places(u)], slot_src[:, bass.ds(at, UNIT)]).then_inc(s_idx, 1)

                        for u in range(RING):
                            put(u, u * UNIT)
                        with act.Fori(0, ITERS - 1) as i:
                            for u in range(RING):
                                act.wait_ge(s_mm, i * RING + (u + 1))
                                put(u, (i + 1) * NR + u * UNIT)
                        for u in range(AHEAD):
                            act.wait_ge(s_mm, (ITERS - 1) * RING + (u + 1))
                            nc.scalar.copy(drel[:, places(u)], slot_dst[:, SLOTS + u * UNIT:SLOTS + (u + 1) * UNIT]).then_inc(s_idx, 1)

                    @block.gpsimd
                    def _(pool):
                        with pool.Fori(0, ITERS) as i:
                            for u in range(RING):
                                pool.wait_ge(s_idx, i * RING + (u + 1))
                                pool.sem_inc(s_begun, 1)
                                for k in range(u * UNIT, (u + 1) * UNIT):
                                    pool.indirect_dma_start(
                                        out=rows[:, k, 0:D], out_offset=None, in_=rows_d,
                                        in_offset=bass.IndirectOffsetOnAxis(ap=idx[:, k:k + 1], axis=0),
                                    ).then_inc(gathered[k], 16)

                    @block.vector
                    def _(dve):
                        nc.vector.memset(rows[:, :, D:RW], 1.0).then_inc(s_one, 1)

                        def one_hots(u, count):
                            dve.wait_ge(s_idx, count)
                            for k in range(u * UNIT, (u + 1) * UNIT):
                                last = nc.vector.tensor_scalar(hot[:, k, :], iota[:, :], drel[:, k:k + 1], None, ALU.is_equal)
                            last.then_inc(s_hot, 1)

                        for u in range(AHEAD):
                            one_hots(u, u + 1)
                        with dve.Fori(0, ITERS) as i:
                            for u in range(RING):
                                w = dve.value_load(slot_bkt[0:1, bass.ds(i * RING + u, 1)], min_val=0, max_val=(1 << 20) - 1)
                                one_hots((u + AHEAD) % RING, i * RING + (u + AHEAD + 1))
                                bkt = [w % 32, (w // 32) % 32, (w // 1024) % 32, w // 32768]
                                for k in range(UNIT):
                                    b = nc.s_assert_within(bkt[k], 0, NT - 1, skip_runtime_bounds_check_because="a slot's bucket is one of NT")
                                    to = acc[:, bass.ds(b * RW, RW)]
                                    dve.drain()
                                    if k == 0:
                                        dve.wait_ge(s_mm, i * RING + (u + 1))
                                    last = nc.vector.tensor_tensor(to, to, ps[:, (u % 2) * UNIT + k, 0:RW], ALU.add)
                                last.then_inc(s_acc, 1)

                    @block.tensor
                    def _(pe):
                        def unit(u, i):
                            pe.wait_ge(s_hot, i * RING + (u + 1))
                            for k in range(UNIT):
                                pe.wait_ge(gathered[u * UNIT + k], i * 16 + (base_of[u * UNIT + k] + 16))
                                last = nc.tensor.matmul(ps[:, (u % 2) * UNIT + k, 0:RW], hot[:, u * UNIT + k, :],
                                                        rows[:, u * UNIT + k, :], start=True, stop=True)
                            last.then_inc(s_mm, 1)

                        pe.wait_ge(s_one, 1)
                        for u in range(2):
                            unit(u, 0)
                        for u in range(2, RING):
                            pe.wait_ge(s_acc, u - 1)
                            unit(u, 0)
                        with pe.Fori(1, ITERS) as i:
                            for u in range(RING):
                                pe.wait_ge(s_acc, i * RING + (u - 1))
                                unit(u, i)

        def stage_gin(acc):
            accv = acc[:, :].rearrange("p (t d) -> p t d", d=RW)
            tmp = ExitStack()

            def t(name, shape, dt=f32):
                return tmp.enter_context(nc.sbuf_tensor(name, shape, dt))

            with tmp:
                w1 = t("gin_w1", [P, KD, F])
                w2 = t("gin_w2", [P, KF, D])
                vec1 = t("gin_vec1", [P, 3, KF])
                vec2 = t("gin_vec2", [P, 3, KD])
                eps1 = t("gin_eps1", [P, 1])
                deg = t("deg", [P, NT])
                stage = t("gin_stage", [P, 2, GT * D])
                stz, sth = (stage[:, b, :].rearrange("p (t d) -> p t d", d=D) for b in range(2))
                ZT = t("gin_zt", [P, KD, NP])
                HT = t("gin_ht", [P, KD, NP])
                s_w, s_deg, s_z, s_h = sem("gin_weights"), sem("gin_deg"), sem("gin_z"), sem("gin_h")
                s_zt, s_zc, s_hc = sem("gin_transposed"), sem("gin_zt_copied"), sem("gin_ht_copied")
                s_step = sem("gin_step")
                with nc.psum_tensor("gin_pst", [P, 3, 512], f32) as pz, nc.psum_tensor("gin_psh", [P, 3, 512], f32) as ph, \
                        nc.Block() as block:
                    @block.sync
                    def _(sp):
                        with nc.allow_non_contiguous_dma(reason="small vectors by feature"):
                            sp.dma_start(eps1[:, :], a["L0_gnn_eps_gin"].partition_broadcast(P)).then_inc(s_w, 16)
                            for k, v in enumerate(("b1", "g1", "bt1")):
                                sp.dma_start(vec1[:, k, :], a["L0_gnn_" + v].rearrange("(c p) -> p c", p=P)).then_inc(s_w, 16)
                            for k, v in enumerate(("b2", "g2", "bt2")):
                                sp.dma_start(vec2[:, k, :], a["L0_gnn_" + v].rearrange("(c p) -> p c", p=P)).then_inc(s_w, 16)
                        sp.dma_start(w1[:, :, :], a["L0_gnn_W1"].rearrange("(c p) f -> p c f", p=P)).then_inc(s_w, 16)
                        sp.dma_start(w2[:, :, :], a["L0_gnn_W2"].rearrange("(c p) f -> p c f", p=P)).then_inc(s_w, 16)

                    @block.vector
                    def _(dve):
                        dve.sem_inc(s_zc, 2)
                        step = Chain(dve, s_step)
                        step(nc.vector.tensor_scalar(deg[:, :], accv[:, :, D], 1.0, None, ALU.max))
                        nc.vector.reciprocal(deg[:, :], deg[:, :]).then_inc(s_deg, 1)
                        dve.wait_ge(s_w, 16 * 9)
                        step(nc.vector.tensor_scalar(eps1[:, :], eps1[:, :], 1.0, None, ALU.add))

                        def z(k, i):
                            nc.vector.scalar_tensor_tensor(stz[:, k, :], tile_of(H, i), eps1[:, 0:1],
                                                           accv[:, bass.ds(i, 1), 0:D].rearrange("p a b -> p (a b)"),
                                                           ALU.mult, ALU.add).then_inc(s_z, 1)

                        for k in range(GT):
                            z(k, k)
                        with dve.Fori(0, NG) as g:
                            for k in range(GT):
                                i = g * GT + k
                                dve.wait_ge(s_zt, i + 1)
                                nc.vector.tensor_copy(columns_of(ZT, i), by_chunk(pz[:, BANK[k], 0:D])).then_inc(s_zc, 1)
                                z(k, ((g + 1) % NG) * GT + k)

                    @block.tensor
                    def _(pe):
                        with pe.Fori(0, NG) as g:
                            for k in range(GT):
                                i = g * GT + k
                                pe.wait_ge(s_zc, i + 1)
                                pe.wait_ge(s_hc, i + 1)
                                pe.wait_ge(s_z, i + 1)
                                pe.wait_ge(s_h, i + 1)
                                transpose_tile(pz[:, BANK[k], :], stz[:, k, :])
                                transpose_tile(ph[:, BANK[k], :], sth[:, k, :]).then_inc(s_zt, 1)

                    @block.scalar
                    def _(act):
                        act.sem_inc(s_hc, 2)
                        act.wait_ge(s_deg, 1)
                        nc.scalar.activation(norm[:, :], deg[:, :], ACT.Sqrt)

                        def h(k, i):
                            nc.scalar.copy(sth[:, k, :], tile_of(H, i)).then_inc(s_h, 1)

                        for k in range(GT):
                            h(k, k)
                        with act.Fori(0, NG) as g:
                            for k in range(GT):
                                i = g * GT + k
                                act.wait_ge(s_zt, i + 1)
                                nc.scalar.copy(columns_of(HT, i), by_chunk(ph[:, BANK[k], 0:D])).then_inc(s_hc, 1)
                                h(k, ((g + 1) % NG) * GT + k)

                TT = t("gin_tt", [P, KF, N])
                st1 = t("gin_st1", [P, KF, NCH + 1, 6])
                st2 = t("gin_st2", [P, KD, NCH + 1, 6])
                mv1 = t("gin_mv1", [P, KF, 2])
                mv2 = t("gin_mv2", [P, KD, 2])
                sc1 = t("gin_sc1", [P, 2, KF])
                sc2 = t("gin_sc2", [P, 2, KD])

                def bn_coefficients(dve, st, mv, sc, vec, s_var, s_sd, s_ready):
                    for m in range(mv.shape[1]):
                        nc.vector.bn_aggr(mv[:, m, :], st[:, m, :, :].rearrange("p a b -> p (a b)"))
                    dve.drain()
                    nc.vector.tensor_scalar(mv[:, :, 1], mv[:, :, 1], EPS, None, ALU.add).then_inc(s_var, 1)
                    dve.wait_ge(s_sd, 1)
                    nc.vector.reciprocal(sc[:, 1, :], sc[:, 0, :])
                    dve.drain()
                    nc.vector.tensor_tensor(sc[:, 0, :], sc[:, 1, :], vec[:, 1, :], ALU.mult)
                    dve.drain()
                    nc.vector.tensor_tensor(sc[:, 1, :], mv[:, :, 0], sc[:, 0, :], ALU.mult)
                    dve.drain()
                    nc.vector.tensor_tensor(sc[:, 1, :], vec[:, 2, :], sc[:, 1, :], ALU.subtract).then_inc(s_ready, 1)

                s_mm, s_ev, s_st = sem("gin_t_made"), sem("gin_t_copied"), sem("gin_t_stats")
                s_va, s_sd, s_sc = sem("gin_var1"), sem("gin_sd1"), sem("gin_scale1")
                with nc.psum_tensor("gin_ps1", [P, 2, KF, CH], f32) as ps, nc.Block() as block:
                    @block.tensor
                    def _(pe):
                        def chunk(b, lo, n, count):
                            pe.wait_ge(s_ev, count)
                            for m in range(KF):
                                for c in range(KD):
                                    last = nc.tensor.matmul(ps[:, b, m, 0:n], w1[:, c, m * P:(m + 1) * P],
                                                            ZT[:, c, bass.ds(lo, n)], start=(c == 0), stop=(c == KD - 1))
                            last.then_inc(s_mm, 1)
                        with pe.Fori(0, NCH // 2) as i:
                            for b in range(2):
                                chunk(b, i * (2 * CH) + b * CH, CH, i * (2 * KF) + (b + 1) * KF)
                        chunk(0, NCH * CH, CTAIL, (NCH + 1) * KF)

                    @block.scalar
                    def _(act):
                        act.sem_inc(s_ev, 2 * KF)
                        def chunk(b, lo, n, count):
                            act.wait_ge(s_mm, count)
                            for m in range(KF):
                                nc.scalar.activation(TT[:, m, bass.ds(lo, n)], ps[:, b, m, 0:n], ACT.Identity,
                                                     bias=vec1[:, 0, m:m + 1]).then_inc(s_ev, 1)
                        with act.Fori(0, NCH // 2) as i:
                            for b in range(2):
                                chunk(b, i * (2 * CH) + b * CH, CH, i * 2 + b + 1)
                        chunk(0, NCH * CH, CTAIL, NCH + 1)
                        act.wait_ge(s_va, 1)
                        nc.scalar.activation(sc1[:, 0, :], mv1[:, :, 1], ACT.Sqrt).then_inc(s_sd, 1)

                    @block.vector
                    def _(dve):
                        def chunk(j, lo, n, count):
                            for m in range(KF):
                                dve.wait_ge(s_ev, count + (m + 1 + 2 * KF))
                                o = st1[:, m, j, :] if isinstance(j, int) else st1[:, m, bass.ds(j, 1), :].rearrange("p a b -> p (a b)")
                                nc.vector.bn_stats(o, TT[:, m, bass.ds(lo, n)])
                        with dve.Fori(0, NCH) as i:
                            chunk(i, i * CH, CH, i * KF)
                        chunk(NCH, NCH * CH, CTAIL, NCH * KF)
                        dve.drain()
                        bn_coefficients(dve, st1, mv1, sc1, vec1, s_va, s_sd, s_sc)

                s_rl, s_cv, s_cc = sem("gin_relu"), sem("gin_c_made"), sem("gin_c_copied")
                s_va2, s_sd2, s_sc2 = sem("gin_var2"), sem("gin_sd2"), sem("gin_scale2")
                with nc.psum_tensor("gin_ps2", [P, 2, KD, CH], f32) as ps, nc.Block() as block:
                    @block.scalar
                    def _(act):
                        def chunk(lo, n):
                            for m in range(KF):
                                nc.scalar.activation(TT[:, m, bass.ds(lo, n)], TT[:, m, bass.ds(lo, n)], ACT.Relu,
                                                     bias=sc1[:, 1, m:m + 1], scale=sc1[:, 0, m:m + 1]).then_inc(s_rl, 1)
                        with act.Fori(0, NCH) as i:
                            chunk(i * CH, CH)
                        chunk(NCH * CH, CTAIL)
                        act.wait_ge(s_va2, 1)
                        nc.scalar.activation(sc2[:, 0, :], mv2[:, :, 1], ACT.Sqrt).then_inc(s_sd2, 1)

                    @block.tensor
                    def _(pe):
                        def chunk(b, lo, n, r, c0):
                            pe.wait_ge(s_rl, r)
                            pe.wait_ge(s_cc, c0)
                            for m in range(KD):
                                for c in range(KF):
                                    last = nc.tensor.matmul(ps[:, b, m, 0:n], w2[:, c, m * P:(m + 1) * P],
                                                            TT[:, c, bass.ds(lo, n)], start=(c == 0), stop=(c == KF - 1))
                            last.then_inc(s_cv, 1)
                        with pe.Fori(0, NCH // 2) as i:
                            for b in range(2):
                                chunk(b, i * (2 * CH) + b * CH, CH, i * (2 * KF) + (b + 1) * KF, i * (2 * KD) + (b + 1) * KD)
                        chunk(0, NCH * CH, CTAIL, (NCH + 1) * KF, (NCH + 1) * KD)

                    @block.vector
                    def _(dve):
                        dve.sem_inc(s_cc, 2 * KD)
                        nc.vector.memset(ZT[:, :, N:NP], 0.0)

                        def chunk(b, j, lo, n, count):
                            dve.wait_ge(s_cv, count)
                            for m in range(KD):
                                nc.vector.scalar_tensor_tensor(
                                    ZT[:, m, bass.ds(lo, n)], ps[:, b, m, 0:n], vec2[:, 0, m:m + 1],
                                    HT[:, m, bass.ds(lo, n)], ALU.add, ALU.add).then_inc(s_cc, 1)
                            dve.drain()
                            for m in range(KD):
                                o = st2[:, m, j, :] if isinstance(j, int) else st2[:, m, bass.ds(j, 1), :].rearrange("p a b -> p (a b)")
                                nc.vector.bn_stats(o, ZT[:, m, bass.ds(lo, n)])
                        with dve.Fori(0, NCH // 2) as i:
                            for b in range(2):
                                chunk(b, i * 2 + b, i * (2 * CH) + b * CH, CH, i * 2 + b + 1)
                        chunk(0, NCH, NCH * CH, CTAIL, NCH + 1)
                        dve.drain()
                        bn_coefficients(dve, st2, mv2, sc2, vec2, s_va2, s_sd2, s_sc2)

                s_r2, s_xt, s_xa = sem("gin_relu2"), sem("gin_back"), sem("gin_x_added")
                with nc.psum_tensor("gin_ps3", [P, 3, 512], f32) as ps, nc.Block() as block:
                    @block.scalar
                    def _(act):
                        def tile(k, i):
                            for m in range(KD):
                                last = nc.scalar.activation(sth[:, k, m * P:(m + 1) * P], ZT[:, m, bass.ds(i * P, P)], ACT.Relu,
                                                            bias=sc2[:, 1, m:m + 1], scale=sc2[:, 0, m:m + 1])
                            last.then_inc(s_r2, 1)

                        for k in range(GT):
                            tile(k, k)
                        with act.Fori(0, NG) as g:
                            for k in range(GT):
                                act.wait_ge(s_xt, g * GT + (k + 1))
                                tile(k, ((g + 1) % NG) * GT + k)

                    @block.tensor
                    def _(pe):
                        with pe.Fori(0, NG) as g:
                            for k in range(GT):
                                i = g * GT + k
                                pe.wait_ge(s_r2, i + 1)
                                pe.wait_ge(s_xa, i + 1)
                                transpose_tile(ps[:, BANK[k], :], sth[:, k, :]).then_inc(s_xt, 1)

                    @block.vector
                    def _(dve):
                        dve.sem_inc(s_xa, 2)
                        with dve.Fori(0, NG) as g:
                            for k in range(GT):
                                i = g * GT + k
                                dve.wait_ge(s_xt, i + 1)
                                nc.vector.tensor_tensor(tile_of(X, i), tile_of(X, i), ps[:, BANK[k], 0:D], ALU.add).then_inc(s_xa, 1)
                                dve.drain()
                                row_stats(i)

        def stage_gat():
            tmp = ExitStack()

            def t(name, shape, dt=f32):
                return tmp.enter_context(nc.sbuf_tensor(name, shape, dt))

            with tmp:
                wg = t("gat_w", [P, KD, HK])
                rowv = t("gat_rows", [P, 5, HK])
                HT = t("gat_ht", [P, KD, NP])
                TS = t("gat_ts", [P, NT, TW])
                TD = t("gat_td", [P, NT, DW])
                prod = t("gat_prod", [P, NT, HK])
                gmax = t("gat_gmax", [P, HEADS])
                gall = t("gat_gall", [P, HEADS])
                e_s = t("gat_es", [P, NT, HEADS])
                self_e = t("gat_self", [P, NT, HEADS])
                es_i = t("gat_es_i", [P, ET2P], i32)
                ed_i = t("gat_ed_i", [P, ET2P], i32)
                lo_i = t("gat_lo_i", [P, ET2P], i32)
                lo_f = t("gat_lo_f", [P, ET2P])
                hi_f = t("gat_hi_f", [P, ET2P])
                hh = t("ex_hh", [P, KF, GN])
                stages = hh[:, :, :].rearrange("p c n -> p (c n)").rearrange("p (b t d) -> p b t d", b=2, d=D)
                sth, stt = stages[:, 0], stages[:, 1]
                s_w, s_e, s_pad = sem("gat_weights"), sem("gat_edges"), sem("gat_pad")
                s_mv, s_std = sem("gat_row_stats"), sem("gat_row_std")
                s_h, s_t, s_c = sem("gat_h"), sem("gat_t"), sem("gat_copied")
                s_hh, s_hc = sem("gat_hh_made"), sem("gat_hh_copied")
                s_m, s_g, s_tab, s_st = sem("gat_max"), sem("gat_gmax"), sem("gat_tables"), sem("gat_step")
                s_out, s_ex = sem("gat_tables_out"), sem("gat_exp")
                with nc.psum_tensor("gat_pst", [P, 3, 512], f32) as pt, nc.psum_tensor("gat_psh", [P, GT, 512], f32) as ph, \
                        nc.Block() as block:
                    @block.sync
                    def _(sp):
                        sp.dma_start(wg[:, :, :], a["L0_ffn_W_gat"].rearrange("(c p) f -> p c f", p=P)).then_inc(s_w, 16)
                        for k, v in enumerate(("att_src", "att_dst")):
                            sp.dma_start(rowv[:, k, :], a["L0_ffn_" + v].rearrange("h k -> (h k)").partition_broadcast(P)).then_inc(s_w, 16)
                        for k, v in enumerate(("b_gat", "ln_gamma", "ln_beta")):
                            sp.dma_start(rowv[:, 2 + k, :], a["L0_ffn_" + v].partition_broadcast(P)).then_inc(s_w, 16)
                        sp.wait_ge(s_pad, 1)
                        for dst, k in ((es_i, 0), (ed_i, 1)):
                            sp.dma_start(dst[:, 0:ET2], a["L0_ffn_edge_index"][k, :].rearrange("(p t) -> p t", p=P)).then_inc(s_e, 16)
                        sp.wait_ge(s_tab, 1)
                        sp.dma_start(srct_d.rearrange("(t p) k -> p t k", p=P), TS[:, :, :]).then_inc(s_out, 16)
                        sp.dma_start(dstt_d.rearrange("(t p) k -> p t k", p=P), TD[:, :, :]).then_inc(s_out, 16)
                        sp.wait_ge(s_out, 32)

                    @block.vector
                    def _(dve):
                        dve.sem_inc(s_hc, 1)
                        V = nc.vector
                        V.memset(es_i[:, ET2:ET2P], NP - 1)
                        V.memset(ed_i[:, ET2:ET2P], NP - 1).then_inc(s_pad, 1)
                        row_moments(dve, "gat", s_mv, s_std, have_stats=True)
                        for k in range(GT):
                            normalise(sth[:, k, :], k).then_inc(s_h, 1)
                        with dve.Fori(0, NG) as g:
                            for k in range(GT):
                                i = g * GT + k
                                dve.wait_ge(s_t, i + 1)
                                normalise(sth[:, k, :], ((g + 1) % NG) * GT + k).then_inc(s_h, 1)
                                dve.wait_ge(s_hh, i + GT + 1)
                                V.tensor_copy(TS[:, bass.ds(i, 1), HEADS:TW].rearrange("p a b -> p (a b)"),
                                              ph[:, k, 0:HK]).then_inc(s_hc, 1)
                        step = Chain(dve, s_st)
                        dve.wait_ge(s_w, 16 * 6)
                        hv = TS[:, :, HEADS:TW]
                        for k, to in ((0, TS[:, :, 0:HEADS]), (1, TD[:, :, 0:HEADS])):
                            dve.drain()
                            step(V.tensor_tensor(prod[:, :, :], hv, rowv[:, k, :].unsqueeze(1).to_broadcast([P, NT, HK]), ALU.mult))
                            step(V.tensor_reduce(to, prod[:, :, :].rearrange("p t (h k) -> p t h k", k=NE), AX.X, ALU.add))
                        a_s, a_d, shift = TS[:, :, 0:HEADS], TD[:, :, 0:HEADS], TD[:, :, HEADS:DW]
                        V.tensor_reduce(gmax[:, :], a_s.rearrange("p t h -> p h t"), AX.X, ALU.max).then_inc(s_m, 1)
                        step(V.tensor_tensor(e_s[:, :, :], a_s, a_d, ALU.add))
                        step(V.scalar_tensor_tensor(e_s[:, :, :], e_s[:, :, :], 0.2, e_s[:, :, :], ALU.mult, ALU.max))
                        dve.wait_ge(s_g, 1)
                        step(V.tensor_tensor(self_e[:, :, :], a_d, gall[:, :].unsqueeze(1).to_broadcast([P, NT, HEADS]), ALU.add))
                        step(V.scalar_tensor_tensor(self_e[:, :, :], self_e[:, :, :], 0.2, self_e[:, :, :], ALU.mult, ALU.max))
                        step(V.tensor_scalar(self_e[:, :, :], self_e[:, :, :], -60.0, None, ALU.add))
                        step(V.tensor_tensor(shift, self_e[:, :, :], e_s[:, :, :], ALU.max))
                        step(V.tensor_tensor(e_s[:, :, :], e_s[:, :, :], shift, ALU.subtract))
                        V.tensor_copy(gmax[:, :], gall[:, :]).then_inc(s_tab, 1)
                        dve.wait_ge(s_e, 32)
                        step(V.tensor_scalar(lo_i[:, :], ed_i[:, :], P - 1, None, ALU.bitwise_and))
                        step(V.tensor_copy(lo_f[:, :], lo_i[:, :]))
                        step(V.tensor_scalar(lo_i[:, :], ed_i[:, :], 7, None, ALU.logical_shift_right))
                        step(V.tensor_copy(hi_f[:, :], lo_i[:, :]))
                        V.memset(hi_f[:, ET2:ET2P], float(NT))

                    @block.gpsimd
                    def _(pool):
                        pool.wait_ge(s_m, 1)
                        nc.gpsimd.partition_all_reduce(gall[:, :], gmax[:, :], P, bass.bass_isa.ReduceOp.max).then_inc(s_g, 1)

                    @block.scalar
                    def _(act):
                        act.sem_inc(s_c, 2)
                        row_deviations(act, s_mv, s_std)
                        with act.Fori(0, NG) as g:
                            for k in range(GT):
                                i = g * GT + k
                                act.wait_ge(s_hh, i + 1)
                                act.wait_ge(s_t, i + 1)
                                nc.scalar.copy(stt[:, k, :], pt[:, BANK[k], 0:D])
                                nc.scalar.copy(columns_of(HT, i), by_chunk(pt[:, BANK[k], 0:D])).then_inc(s_c, 1)
                        act.wait_ge(s_tab, 1)
                        nc.scalar.activation(self_e[:, :, :], e_s[:, :, :], ACT.Exp).then_inc(s_ex, 1)

                    @block.tensor
                    def _(pe):
                        pe.sem_inc(s_hh, GT)
                        pe.wait_ge(s_w, 16 * 6)

                        def turn(k, i):
                            pe.wait_ge(s_h, i + 1)
                            transpose_tile(pt[:, BANK[k], :], sth[:, k, :]).then_inc(s_t, 1)

                        turn(0, 0)
                        with pe.Fori(0, NG) as g:
                            pe.wait_ge(s_hc, g * GT + 1)
                            for k in range(GT):
                                i = g * GT + k
                                turn((k + 1) % GT, i + 1)
                                pe.wait_ge(s_c, i + 3)
                                for c in range(KD):
                                    last = nc.tensor.matmul(ph[:, k, 0:HK], stt[:, k, c * P:(c + 1) * P], wg[:, c, :],
                                                            start=(c == 0), stop=(c == KD - 1))
                                last.then_inc(s_hh, 1)

                sums = t("gat_sums", [P, NT, TW])
                loop = ExitStack()

                def u(name, shape, dt=f32):
                    return loop.enter_context(nc.sbuf_tensor(name, shape, dt))

                w1 = h_room[:, 0:KD * NE * F].rearrange("p (c e f) -> p c e f", c=KD, e=NE)
                w2 = u("ex_w2", [P, KF, NE, D])
                b1 = u("ex_b1", [P, NE, KF])
                b2 = u("ex_b2", [P, NE, D])
                yo = u("ex_yo", [P, 2, GT * D])
                gs = u("gat_gs", [P, 2 * STEP, TW])
                gd = u("gat_gd", [P, 2 * STEP, DW])
                ix = u("gat_ix", [P, 2, 2 * STEP], i32)
                lh = u("gat_lh", [P, 2, 2 * STEP])
                ev = u("gat_ev", [P, 2 * STEP, HEADS])
                ee = u("gat_ee", [P, 2 * STEP, HEADS])
                msg = u("gat_msg", [P, STEP, TW])
                parts = u("gat_parts", [P, STEP, PARTS, TW], bf16)
                colt = u("gat_colt", [P, NT, TW], bf16)
                mask = u("gat_mask", [P, STEP, NT * TW], bf16)
                hot = u("gat_hot", [P, 2 * STEP, P], bf16)
                mov = u("gat_mov", [P, STEP, PARTS, NT * TW], bf16)
                HN = GN // 2
                count_of = lambda final, e: STEP_END if final and e == NE - 1 else STEP

                def outs_at(n):
                    return [max(n - 2 * (GT - k), k) for k in range(GT)]

                src_sem, dst_sem = gathered[0:2 * STEP], gathered[2 * STEP:4 * STEP]
                base_of = done[:]
                for k in range(4 * STEP):
                    done[k] += 16 * (STEPS // 2 - (k % (2 * STEP) >= STEP + STEP_END))
                s_ix, s_begun, s_msg = sem("gat_ix"), sem("gat_begun"), sem("gat_messages")
                s_ev, s_ee, s_mv, s_mm = sem("gat_score"), sem("gat_weight"), sem("gat_moving"), sem("gat_summed")
                s_z, s_fin = sem("gat_zero"), sem("gat_all_summed")
                s_w, s_a, s_g, s_y = sem("ex_weights"), sem("ex_hidden"), sem("ex_gelu"), sem("ex_out")
                s_ye, s_u, s_free = sem("ex_out_copied"), sem("ex_stored"), sem("ex_out_free")
                WLOADS = 16 * 4 * NE

                def gather_rows(pool, k):
                    pool.indirect_dma_start(
                        out=gs[:, k, :], out_offset=None, in_=srct_d,
                        in_offset=bass.IndirectOffsetOnAxis(ap=ix[:, 0, k:k + 1], axis=0)).then_inc(src_sem[k], 16)
                    pool.indirect_dma_start(
                        out=gd[:, k, :], out_offset=None, in_=dstt_d,
                        in_offset=bass.IndirectOffsetOnAxis(ap=ix[:, 1, k:k + 1], axis=0)).then_inc(dst_sem[k], 16)

                with nc.psum_tensor("gat_acc", [P, 512], f32) as ps, \
                        nc.psum_tensor("ex_ps1", [P, 2, 2, 512], f32) as p1, nc.psum_tensor("ex_ps2", [P, 2, 512], f32) as p2, \
                        nc.Block() as block:
                    acc = ps[:, 0:NT * TW]
                    half = lambda e: slice((e % 2) * STEP, (e % 2 + 1) * STEP)
                    tiles = lambda e: range((e % 2) * STEP, (e % 2 + 1) * STEP)

                    @block.sync
                    def _(sp):
                        sp.sem_inc(s_free, 2)
                        for e in range(NE):
                            sp.dma_start(w1[:, :, e, :], a["L0_ffn_W1"][e].rearrange("(c p) f -> p c f", p=P)).then_inc(s_w, 16)
                            sp.dma_start(w2[:, :, e, :], a["L0_ffn_W2"][e].rearrange("(c p) f -> p c f", p=P)).then_inc(s_w, 16)
                            with nc.allow_non_contiguous_dma(reason="bias by feature"):
                                sp.dma_start(b1[:, e, :], a["L0_ffn_b1"][e].rearrange("(c p) -> p c", p=P)).then_inc(s_w, 16)
                            sp.dma_start(b2[:, e, :], a["L0_ffn_b2"][e].partition_broadcast(P)).then_inc(s_w, 16)
                        with sp.Fori(0, NG) as g:
                            for e in range(NE):
                                sp.wait_ge(s_ye, g * (NE * GT) + ((e + 1) * GT + 1))
                                sp.dma_start(y_d[e, :, bass.ds(g * (GT * D), GT * D)], yo[:, e % 2, :]).then_inc(s_u, 16)
                                sp.wait_ge(s_u, g * (16 * NE) + 16 * (e + 1))
                                sp.sem_inc(s_free, 1)

                    @block.gpsimd
                    def _(pool):
                        def group(g, final):
                            for e in range(NE):
                                pool.wait_ge(s_ix, g * NE + (e + 1))
                                pool.sem_inc(s_begun, 1)
                                for k in tiles(e)[:count_of(final, e)]:
                                    gather_rows(pool, k)

                        with pool.Fori(0, NG - 1) as g:
                            group(g, False)
                        group(NG - 1, True)

                    @block.scalar
                    def _(act):
                        def put(e, at):
                            nc.scalar.copy(ix[:, 0, half(e)], es_i[:, bass.ds(at, STEP)])
                            nc.scalar.copy(ix[:, 1, half(e)], ed_i[:, bass.ds(at, STEP)]).then_inc(s_ix, 1)

                        act.sem_inc(s_g, 1)
                        for e in range(2):
                            put(e, e * STEP)

                        def exps(e, at):
                            act.wait_ge(s_ev, at)
                            nc.scalar.activation(ee[:, half(e), :], ev[:, half(e), :], ACT.Exp).then_inc(s_ee, 1)

                        def group(g, final):
                            for e in range(NE):
                                if not (final and e >= NE - 2):
                                    act.wait_ge(s_msg, g * NE + (e + 1))
                                    put(e, (g * NE + (e + 2)) * STEP)
                                act.wait_ge(s_y, g * (NE * GT) + (e * GT + 1))
                                for m in range(KF):
                                    act.wait_ge(s_a, g * (NE * KF) + (e * KF + m + 1))
                                    nc.scalar.activation(hh[:, m, :].rearrange("p (n k) -> p n k", n=2), p1[:, m % 2, :, 0:HN],
                                                         ACT.Gelu, bias=b1[:, e, m:m + 1]).then_inc(s_g, 1)
                                if not (final and e == NE - 1):
                                    exps(e + 1, g * NE + (e + 2))

                        exps(0, 1)
                        with act.Fori(0, NG - 1) as g:
                            group(g, False)
                        group(NG - 1, True)

                    @block.vector
                    def _(dve):
                        V = nc.vector
                        dve.sem_inc(s_ye, 1)
                        V.memset(sums[:, :, :], 0.0).then_inc(s_z, 1)
                        V.tensor_copy(colt[:, :, :], iota[:, 0:NT].unsqueeze(2).to_broadcast([P, NT, TW]))

                        def scores(e, at, n, rows_in):
                            r = half(e)
                            V.tensor_copy(lh[:, 0, r], lo_f[:, at])
                            V.tensor_copy(lh[:, 1, r], hi_f[:, at])
                            dve.drain()
                            for k in tiles(e):
                                V.tensor_scalar(hot[:, k, :], iota[:, :], lh[:, 0, k:k + 1], None, ALU.is_equal)
                            for k in tiles(e)[:n]:
                                rows_in(k)
                            V.tensor_tensor(ev[:, r, :], gs[:, r, 0:HEADS], gd[:, r, 0:HEADS], ALU.add)
                            dve.drain()
                            V.scalar_tensor_tensor(ev[:, r, :], ev[:, r, :], 0.2, ev[:, r, :], ALU.mult, ALU.max)
                            dve.drain()
                            V.tensor_tensor(ev[:, r, :], ev[:, r, :], gd[:, r, HEADS:DW], ALU.subtract).then_inc(s_ev, 1)

                        def first_rows(k):
                            dve.wait_ge(src_sem[k], base_of[k] + 16)
                            dve.wait_ge(dst_sem[k], base_of[2 * STEP + k] + 16)

                        scores(0, slice(0, STEP), STEP, first_rows)
                        dve.wait_ge(s_w, WLOADS)

                        def group(g, final):
                            for e in range(NE):
                                r = half(e)
                                dve.wait_ge(s_ee, g * NE + (e + 1))
                                V.tensor_tensor(
                                    msg[:, :, 0:HK].rearrange("p t (h k) -> p t h k", k=NE),
                                    gs[:, r, HEADS:TW].rearrange("p t (h k) -> p t h k", k=NE),
                                    ee[:, r, :].unsqueeze(3).to_broadcast([P, STEP, HEADS, NE]), ALU.mult).then_inc(s_msg, 1)
                                V.tensor_copy(msg[:, :, HK:TW], ee[:, r, :])
                                for k in range(STEP):
                                    V.tensor_scalar(mask[:, k, :], colt[:, :, :].rearrange("p t w -> p (t w)"),
                                                    lh[:, 1, (e % 2) * STEP + k:(e % 2) * STEP + k + 1], None, ALU.is_equal)
                                dve.drain()
                                for q in range(PARTS):
                                    V.tensor_copy(parts[:, :, q, :], msg[:, :, :])
                                    dve.drain()
                                    if q + 1 < PARTS:
                                        V.tensor_tensor(msg[:, :, :], msg[:, :, :], parts[:, :, q, :], ALU.subtract)
                                        dve.drain()
                                dve.wait_ge(s_mm, g * NE + (e + 2))
                                dve.wait_ge(s_free, g * NE + (e + 1))
                                n = count_of(final, e)
                                for k in range(n):
                                    V.tensor_tensor(
                                        mov[:, k, :, :].rearrange("p q (t w) -> p q t w", w=TW),
                                        parts[:, k, :, :].unsqueeze(2).to_broadcast([P, PARTS, NT, TW]),
                                        mask[:, k, :].rearrange("p (t w) -> p t w", w=TW).unsqueeze(1).to_broadcast([P, PARTS, NT, TW]),
                                        ALU.mult).then_inc(s_mv, 1)
                                    if k in outs_at(n):
                                        o = outs_at(n).index(k)
                                        dve.wait_ge(s_y, g * (NE * GT) + (e * GT + o + 2))
                                        V.tensor_tensor(yo[:, e % 2, o * D:(o + 1) * D], p2[:, (e * GT + o) % 2, 0:D], b2[:, e, :],
                                                        ALU.add).then_inc(s_ye, 1)

                                def rows_in(k):
                                    dve.wait_ge(src_sem[k], g * 32 + (16 * ((e + 1) // 2 + 1) + base_of[k]))
                                    dve.wait_ge(dst_sem[k], g * 32 + (16 * ((e + 1) // 2 + 1) + base_of[2 * STEP + k]))

                                if not (final and e == NE - 1):
                                    scores(e + 1, bass.ds((g * NE + (e + 1)) * STEP, STEP), count_of(final, e + 1), rows_in)

                        with dve.Fori(0, NG - 1) as g:
                            group(g, False)
                        group(NG - 1, True)
                        dve.wait_ge(s_fin, 1)
                        V.tensor_copy(sums[:, :, :].rearrange("p t w -> p (t w)"), acc)

                    @block.tensor
                    def _(pe):
                        pe.sem_inc(s_y, 1)
                        pe.sem_inc(s_mm, 2)
                        pe.wait_ge(s_z, 1)
                        zeros = sums[:, :, :].rearrange("p t w -> p (t w)")
                        nc.tensor.matmul(acc, ident[:, :], zeros, start=True, stop=False, skip_group_check=True)
                        pe.wait_ge(s_w, WLOADS)

                        def group(g, final):
                            for e in range(NE):
                                for m in range(KF):
                                    pe.wait_ge(s_g, g * (NE * KF) + max(e * KF + m, 1))
                                    for n in range(2):
                                        for c in range(KD):
                                            last = nc.tensor.matmul(p1[:, m % 2, n, 0:HN], w1[:, c, e, m * P:(m + 1) * P],
                                                                    HT[:, c, bass.ds(g * GN + n * HN, HN)],
                                                                    start=(c == 0), stop=(c == KD - 1))
                                    last.then_inc(s_a, 1)
                                pe.wait_ge(s_g, g * (NE * KF) + ((e + 1) * KF + 1))
                                for k in range(GT):
                                    v = e * GT + k
                                    pe.wait_ge(s_ye, g * (NE * GT) + max(v, 1))
                                    for c in range(KF):
                                        last = nc.tensor.matmul(p2[:, v % 2, 0:D], hh[:, c, k * P:(k + 1) * P], w2[:, c, e, :],
                                                                start=(c == 0), stop=(c == KF - 1))
                                    last.then_inc(s_y, 1)
                                for k in range(count_of(final, e)):
                                    q = (e % 2) * STEP + k
                                    pe.wait_ge(s_mv, (g * NE + e) * STEP + (k + 1))
                                    for part in range(PARTS):
                                        last = nc.tensor.matmul(acc, hot[:, q, :], mov[:, k, part, :], start=False,
                                                                stop=False, skip_group_check=True)
                                last.then_inc(s_mm, 1)

                        with pe.Fori(0, NG - 1) as g:
                            group(g, False)
                        group(NG - 1, True)
                        nc.tensor.matmul(acc, ident[:, :], zeros, start=False, stop=True, skip_group_check=True).then_inc(s_fin, 1)
                loop.close()

                agg = t("gat_agg", [P, NT, HK])
                den = t("gat_den", [P, NT, HEADS])
                s1 = t("gat_s1", [P, NT, 1])
                sc = t("gat_sc", [P, NT, NE])
                rank = t("gat_rank", [P, NT, NE])
                over = t("gat_over", [P, 2, NT, NE, NE])
                before = t("gat_before", [P, NE, NE])
                gate = t("gat_gate", [P, NT, NE])
                y_rest = t("gat_yst", [P, NG - 1, NE, GT * D])
                yst = [h_room[:, 0:NE * GT * D].rearrange("p (e n) -> p e n", e=NE)] + [y_rest[:, g, :, :] for g in range(NG - 1)]
                s_k, s_sq, s_q, s_ex2 = sem("mix_step"), sem("mix_var"), sem("mix_std"), sem("mix_exp")
                s_e2 = sem("mix_score")
                s_y = [sem(f"mix_y_{g}") for g in range(NG)]
                s_pg, s_gy, s_xg = sem("mix_gate_ready"), sem("mix_gated"), sem("mix_added")
                DG = 3

                with nc.Block() as block:
                    @block.vector
                    def _(dve):
                        V = nc.vector
                        step = Chain(dve, s_k)
                        b4 = lambda ap: ap.unsqueeze(3).to_broadcast([P, NT, HEADS, NE])
                        v4 = lambda ap: ap.rearrange("p t (h k) -> p t h k", k=NE)
                        rb = lambda k: rowv[:, k, :].unsqueeze(1).to_broadcast([P, NT, HK])
                        nb = lambda ap, w: ap.to_broadcast([P, NT, w])
                        step(V.tensor_tensor(v4(agg[:, :, :]), v4(TS[:, :, HEADS:TW]), b4(self_e[:, :, :]), ALU.mult))
                        step(V.tensor_tensor(agg[:, :, :], agg[:, :, :], sums[:, :, 0:HK], ALU.add))
                        step(V.tensor_tensor(den[:, :, :], sums[:, :, HK:TW], self_e[:, :, :], ALU.add))
                        step(V.tensor_scalar(den[:, :, :], den[:, :, :], 1e-16, None, ALU.add))
                        step(V.reciprocal(den[:, :, :], den[:, :, :]))
                        step(V.tensor_tensor(v4(agg[:, :, :]), v4(agg[:, :, :]), b4(den[:, :, :]), ALU.mult))
                        step(V.tensor_tensor(agg[:, :, :], agg[:, :, :], rb(2), ALU.add))
                        step(V.tensor_reduce(s1[:, :, 0], agg[:, :, :], AX.X, ALU.add))
                        step(V.tensor_scalar(s1[:, :, :], s1[:, :, :], 1.0 / HK, None, ALU.mult))
                        step(V.tensor_tensor(agg[:, :, :], agg[:, :, :], nb(s1[:, :, :], HK), ALU.subtract))
                        step(V.tensor_tensor(prod[:, :, :], agg[:, :, :], agg[:, :, :], ALU.mult))
                        step(V.tensor_reduce(s1[:, :, 0], prod[:, :, :], AX.X, ALU.add))
                        V.tensor_scalar(s1[:, :, :], s1[:, :, :], 1.0 / HK, EPS, ALU.mult, ALU.add).then_inc(s_sq, 1)
                        dve.wait_ge(s_q, 1)
                        step(V.reciprocal(s1[:, :, :], s1[:, :, :]))
                        step(V.tensor_tensor(agg[:, :, :], agg[:, :, :], nb(s1[:, :, :], HK), ALU.mult))
                        step(V.tensor_tensor(agg[:, :, :], agg[:, :, :], rb(3), ALU.mult))
                        step(V.tensor_tensor(agg[:, :, :], agg[:, :, :], rb(4), ALU.add))
                        step(V.tensor_reduce(sc[:, :, :], agg[:, :, :].rearrange("p t (h k) -> p t k h", k=NE), AX.X, ALU.add))
                        step(V.tensor_scalar(sc[:, :, :], sc[:, :, :], 1.0 / HEADS, None, ALU.mult))
                        of_j = sc[:, :, :].unsqueeze(2).to_broadcast([P, NT, NE, NE])
                        of_i = sc[:, :, :].unsqueeze(3).to_broadcast([P, NT, NE, NE])
                        V.tensor_tensor(over[:, 0], of_j, of_i, ALU.is_gt)
                        V.tensor_tensor(before[:, :, :], iota[:, 0:NE].unsqueeze(1).to_broadcast([P, NE, NE]),
                                        iota[:, 0:NE].unsqueeze(2).to_broadcast([P, NE, NE]), ALU.is_lt)
                        step(V.tensor_tensor(over[:, 1], of_j, of_i, ALU.is_equal))
                        step(V.tensor_tensor(over[:, 1], over[:, 1], before[:, :, :].unsqueeze(1).to_broadcast([P, NT, NE, NE]), ALU.mult))
                        step(V.tensor_tensor(over[:, 0], over[:, 0], over[:, 1], ALU.add))
                        step(V.tensor_reduce(rank[:, :, :], over[:, 0], AX.X, ALU.add))
                        step(V.tensor_reduce(s1[:, :, 0], sc[:, :, :], AX.X, ALU.max))
                        V.tensor_tensor(sc[:, :, :], sc[:, :, :], nb(s1[:, :, :], NE), ALU.subtract).then_inc(s_e2, 1)
                        step(V.tensor_scalar(rank[:, :, :], rank[:, :, :], 1.5, None, ALU.is_lt))
                        dve.wait_ge(s_ex2, 1)
                        step(V.tensor_tensor(gate[:, :, :], gate[:, :, :], rank[:, :, :], ALU.mult))
                        step(V.tensor_reduce(s1[:, :, 0], gate[:, :, :], AX.X, ALU.add))
                        step(V.reciprocal(s1[:, :, :], s1[:, :, :]))
                        step(V.tensor_tensor(gate[:, :, :], gate[:, :, :], nb(s1[:, :, :], NE), ALU.mult))
                        dve.sem_inc(s_pg, 1)
                        for g in range(DG):
                            dve.wait_ge(s_y[g], 16)
                            for e in range(NE):
                                dve.drain()
                                for k in range(GT):
                                    i = g * GT + k
                                    V.scalar_tensor_tensor(X[:, i, :], yst[g][:, e, k * D:(k + 1) * D], gate[:, i, e:e + 1],
                                                           X[:, i, :], ALU.mult, ALU.add)
                            dve.drain()
                            for k in range(GT):
                                row_stats(g * GT + k)
                        for g in range(DG, NG):
                            dve.wait_ge(s_xg, g - DG + 1)
                            for k in range(GT):
                                row_stats(g * GT + k)

                    @block.gpsimd
                    def _(pool):
                        for g in range(DG, NG):
                            xs = X[:, g * GT:(g + 1) * GT, :].rearrange("p t d -> p (t d)")
                            for e in range(NE):
                                pool.wait_ge(s_gy, (g - DG) * NE + e + 1)
                                pool.drain()
                                last = nc.gpsimd.tensor_tensor(xs, xs, yst[g][:, e, :], ALU.add)
                            last.then_inc(s_xg, 1)

                    @block.scalar
                    def _(act):
                        act.wait_ge(s_sq, 1)
                        nc.scalar.activation(s1[:, :, :], s1[:, :, :], ACT.Sqrt).then_inc(s_q, 1)
                        act.wait_ge(s_e2, 1)
                        nc.scalar.activation(gate[:, :, :], sc[:, :, :], ACT.Exp).then_inc(s_ex2, 1)
                        act.wait_ge(s_pg, 1)
                        for g in range(DG, NG):
                            act.wait_ge(s_y[g], 16)
                            for e in range(NE):
                                for k in range(GT):
                                    ys = yst[g][:, e, k * D:(k + 1) * D]
                                    last = nc.scalar.activation(ys, ys, ACT.Copy, scale=gate[:, g * GT + k, e:e + 1])
                                last.then_inc(s_gy, 1)

                    @block.sync
                    def _(sp):
                        for g in (0, DG, 1, DG + 1, 2):
                            sp.dma_start(yst[g], y_d[:, :, g * (GT * D):(g + 1) * (GT * D)].rearrange("e p n -> p e n")).then_inc(s_y[g], 16)

        def stage_lin(acc):
            tmp = ExitStack()

            def t(name, shape, dt=f32):
                return tmp.enter_context(nc.sbuf_tensor(name, shape, dt))

            with tmp:
                wt = t("lin_wt", [P, KD, D])
                br = t("lin_b", [P, D])
                sth = t("lin_sth", [P, GT, D])
                stt = t("lin_stt", [P, GT, D])
                bn = t("lin_bn", [P, GT, D])
                to = t("lin_out", [P, NT, D])
                s_mv, s_std = sem("lin_row_stats"), sem("lin_row_std")
                s_w, s_h, s_t, s_c, s_y, s_o, s_d, s_b = (sem("lin_" + v) for v in (
                    "w", "rows", "transposed", "staged", "made", "out", "stored", "bias"))
                with nc.psum_tensor("lin_pt", [P, 3, 512], f32) as pt, nc.psum_tensor("lin_py", [P, GT, 512], f32) as py, \
                        nc.Block() as block:
                    @block.sync
                    def _(sp):
                        sp.dma_start(wt[:, :, :], a["L1_gnn_Wt"].rearrange("(c p) f -> p c f", p=P)).then_inc(s_w, 16)
                        sp.dma_start(br[:, :], a["L1_gnn_b"].partition_broadcast(P)).then_inc(s_w, 16)
                        with sp.Fori(0, NG) as g:
                            sp.wait_ge(s_o, g * GT + (GT + 1))
                            tl = bass.ds(g * GT, GT)
                            sp.dma_start(rows_d.rearrange("(t p) d -> p t d", p=P)[:, tl, :], to[:, tl, :]).then_inc(s_d, 16)
                        sp.wait_ge(s_d, 16 * NG)

                    @block.gpsimd
                    def _(pool):
                        nc.gpsimd.memset(acc[:, :], 0.0)

                    @block.vector
                    def _(dve):
                        dve.sem_inc(s_o, 1)
                        row_moments(dve, "lin", s_mv, s_std, have_stats=True)
                        for k in range(GT):
                            normalise(sth[:, k, :], k).then_inc(s_h, 1)
                        with dve.Fori(0, NG) as g:
                            for k in range(GT):
                                i = g * GT + k
                                dve.wait_ge(s_t, i + 1)
                                normalise(sth[:, k, :], ((g + 1) % NG) * GT + k).then_inc(s_h, 1)
                                dve.wait_ge(s_b, i + 1)
                                dve.wait_ge(s_y, i + GT + 1)
                                nc.vector.scalar_tensor_tensor(tile_of(to, i), py[:, k, 0:D], norm[:, bass.ds(i, 1)],
                                                               bn[:, k, :], ALU.mult, ALU.add).then_inc(s_o, 1)

                    @block.scalar
                    def _(act):
                        act.sem_inc(s_c, 2)
                        row_deviations(act, s_mv, s_std)
                        act.wait_ge(s_w, 32)

                        def bias(k, i):
                            nc.scalar.activation(bn[:, k, :], br[:, :], ACT.Copy, scale=norm[:, bass.ds(i, 1)]).then_inc(s_b, 1)

                        for k in range(GT):
                            bias(k, k)
                        with act.Fori(0, NG) as g:
                            for k in range(GT):
                                i = g * GT + k
                                act.wait_ge(s_y, i + 1)
                                act.wait_ge(s_t, i + 1)
                                nc.scalar.copy(stt[:, k, :], pt[:, BANK[k], 0:D]).then_inc(s_c, 1)
                                if k >= 2:
                                    act.wait_ge(s_o, i)
                                    bias(k - 2, ((g + 1) % NG) * GT + (k - 2))
                            for k in range(GT - 2, GT):
                                act.wait_ge(s_o, g * GT + (k + 2))
                                bias(k, ((g + 1) % NG) * GT + k)

                    @block.tensor
                    def _(pe):
                        pe.sem_inc(s_y, GT)
                        pe.wait_ge(s_w, 32)

                        def turn(k, i):
                            pe.wait_ge(s_h, i + 1)
                            transpose_tile(pt[:, BANK[k], :], sth[:, k, :]).then_inc(s_t, 1)

                        turn(0, 0)
                        with pe.Fori(0, NG) as g:
                            pe.wait_ge(s_o, g * GT + 1)
                            for k in range(GT):
                                i = g * GT + k
                                turn((k + 1) % GT, i + 1)
                                pe.wait_ge(s_c, i + 3)
                                for c in range(KD):
                                    last = nc.tensor.matmul(py[:, k, 0:D], stt[:, k, c * P:(c + 1) * P], wt[:, c, :],
                                                            start=(c == 0), stop=(c == KD - 1))
                                last.then_inc(s_y, 1)

        def stage_add(acc):
            accv = acc[:, :].rearrange("p (t d) -> p t d", d=RW)
            s_sc, s_ad = sem("add_scaled"), sem("add_added")
            DG = 3
            with nc.Block() as block:
                @block.vector
                def _(dve):
                    with dve.Fori(0, DG) as g:
                        for k in range(GT):
                            i = g * GT + k
                            nc.vector.scalar_tensor_tensor(tile_of(X, i), accv[:, bass.ds(i, 1), 0:D].rearrange("p a b -> p (a b)"),
                                                           norm[:, bass.ds(i, 1)], tile_of(X, i), ALU.mult, ALU.add)
                        dve.drain()
                        for k in range(GT):
                            row_stats(g * GT + k)
                    for g in range(DG, NG):
                        dve.wait_ge(s_ad, g - DG + 1)
                        for k in range(GT):
                            row_stats(g * GT + k)

                @block.scalar
                def _(act):
                    for g in range(DG, NG):
                        for k in range(GT):
                            i = g * GT + k
                            last = nc.scalar.activation(accv[:, i, 0:D], accv[:, i, 0:D], ACT.Copy, scale=norm[:, i:i + 1])
                        last.then_inc(s_sc, 1)

                @block.gpsimd
                def _(pool):
                    for g in range(DG, NG):
                        tl = slice(g * GT, (g + 1) * GT)
                        pool.wait_ge(s_sc, g - DG + 1)
                        nc.gpsimd.tensor_tensor(X[:, tl, :], X[:, tl, :], accv[:, tl, 0:D], ALU.add).then_inc(s_ad, 1)

        def stage_moe():
            tmp = ExitStack()

            def t(name, shape, dt=f32):
                return tmp.enter_context(nc.sbuf_tensor(name, shape, dt))

            with tmp:
                HT = t("moe_ht", [P, KD, NP])
                sth = t("moe_sth", [P, GT, D])
                tsum = t("moe_tsum", [P, NT, KD])
                wr = t("moe_wr", [P, KD, NE1])
                rw = t("moe_row", [1, 10, NE1])
                top = t("moe_top", [1, 8])
                topi = t("moe_topi", [1, 8], mybir.dt.uint32)
                wts = t("moe_wts", [1, 2])
                wcol = t("moe_wcol", [P, 2])
                mean = t("moe_mean", [P, KD])
                w1 = t("moe_w1", [P, 2, KD, F])
                w2 = t("moe_w2", [P, 2, KF, D])
                b1 = t("moe_b1", [P, 2, KF])
                b2 = t("moe_b2", [P, 2, D])
                bs = t("moe_bs", [P, D])
                gb = t("moe_gb", [P, 2, D])
                s_mv, s_std = sem("moe_row_stats"), sem("moe_row_std")
                s_w, s_h, s_t, s_c = sem("moe_small"), sem("moe_rows"), sem("moe_transposed"), sem("moe_ht_copied")
                s_mc, s_lg, s_rt = sem("moe_mean_copied"), sem("moe_logits"), sem("moe_routed")
                s_st, s_x, s_xd = sem("moe_step"), sem("moe_exp_in"), sem("moe_exp")
                s_wc, s_wcd, s_ld = sem("moe_weight_col"), sem("moe_pad2"), sem("moe_experts_loaded")
                with nc.psum_tensor("moe_pt", [P, GT, 512], f32) as pt, nc.psum_tensor("moe_pm", [P, 512], f32) as pm, \
                        nc.psum_tensor("moe_pw", [P, 512], f32) as pw, nc.Block() as block:
                    @block.sync
                    def _(sp):
                        sp.dma_start(wr[:, :, :], a["L1_ffn_Wr"].rearrange("(c p) e -> p c e", p=P)).then_inc(s_w, 16)
                        sp.dma_start(rw[:, 0, :], a["L1_ffn_br"].unsqueeze(0)).then_inc(s_w, 16)
                        sp.dma_start(gb[:, 0, :], a["L1_ffn_gamma"].partition_broadcast(P)).then_inc(s_w, 16)
                        sp.dma_start(gb[:, 1, :], a["L1_ffn_beta"].partition_broadcast(P)).then_inc(s_w, 16)
                        sp.wait_ge(s_rt, 1)
                        for j in range(2):
                            e = sp.value_load(topi[0:1, j:j + 1], min_val=0, max_val=NE1 - 1)
                            sp.dma_start(w1[:, j, :, :], a["L1_ffn_W1"][bass.ds(e, 1)].rearrange("o (c p) f -> p (o c) f", p=P)).then_inc(s_ld, 16)
                            sp.dma_start(w2[:, j, :, :], a["L1_ffn_W2"][bass.ds(e, 1)].rearrange("o (c p) f -> p (o c) f", p=P)).then_inc(s_ld, 16)
                            with nc.allow_non_contiguous_dma(reason="bias by feature"):
                                sp.dma_start(b1[:, j, :], a["L1_ffn_b1"][bass.ds(e, 1)].rearrange("o (c p) -> p (o c)", p=P)).then_inc(s_ld, 16)
                            sp.dma_start(b2[:, j, :], a["L1_ffn_b2"][bass.ds(e, 1)].to_broadcast([P, D])).then_inc(s_ld, 16)
                        sp.wait_ge(s_ld, 16 * 8)

                    @block.tensor
                    def _(pe):
                        with pe.Fori(0, NG) as g:
                            pe.wait_ge(s_c, g * GT + 1)
                            for k in range(GT):
                                pe.wait_ge(s_h, g * GT + (k + 1))
                                transpose_tile(pt[:, k, :], sth[:, k, :]).then_inc(s_t, 1)
                        pe.wait_ge(s_w, 64)
                        pe.wait_ge(s_mc, 1)
                        for c in range(KD):
                            last = nc.tensor.matmul(pw[0:1, 0:NE1], mean[:, c:c + 1], wr[:, c, :], start=(c == 0), stop=(c == KD - 1))
                        last.then_inc(s_lg, 1)
                        pe.wait_ge(s_wc, 1)
                        nc.tensor.matmul(pm[:, 0:2], ones[0:1, :], wts[0:1, :], start=True, stop=True).then_inc(s_wcd, 1)

                    @block.vector
                    def _(dve):
                        V = nc.vector
                        row_moments(dve, "moe", s_mv, s_std, have_stats=True)
                        V.tensor_tensor(rstd[:, FULL:NT], rstd[:, FULL:NT], valid[:, 1:2], ALU.mult)
                        dve.drain()
                        for k in range(GT):
                            normalise(sth[:, k, :], k).then_inc(s_h, 1)
                        with dve.Fori(0, NG) as g:
                            for k in range(GT):
                                dve.wait_ge(s_t, g * GT + (k + 1))
                                normalise(sth[:, k, :], ((g + 1) % NG) * GT + k).then_inc(s_h, 1)
                                dve.wait_ge(s_c, g * GT + (k + 2))
                                V.tensor_reduce(tile_of(tsum, g * GT + k), columns_of(HT, g * GT + k), AX.X, ALU.add)
                        dve.drain()
                        V.tensor_reduce(mean[:, :], tsum[:, :, :].rearrange("p t c -> p c t"), AX.X, ALU.add)
                        dve.drain()
                        V.tensor_scalar(mean[:, :], mean[:, :], 1.0 / N, None, ALU.mult).then_inc(s_mc, 1)
                        step = Chain(dve, s_st)

                        def softmax(src, dst, n, count):
                            step(V.tensor_reduce(rw[:, 9, 0:1], src, AX.X, ALU.max))
                            V.tensor_scalar(dst, src, rw[0:1, 9, 0:1], None, ALU.subtract).then_inc(s_x, 1)
                            dve.wait_ge(s_xd, count)
                            step(V.tensor_reduce(rw[:, 9, 0:1], dst, AX.X, ALU.add))
                            step(V.reciprocal(rw[:, 9, 1:2], rw[:, 9, 0:1]))
                            step(V.tensor_scalar(dst, dst, rw[0:1, 9, 1:2], None, ALU.mult))

                        dve.wait_ge(s_lg, 1)
                        step(V.tensor_tensor(rw[:, 1, :], rw[:, 0, :], pw[0:1, 0:NE1], ALU.add))
                        softmax(rw[:, 1, :], rw[:, 2, :], NE1, 1)
                        step(V.tensor_scalar(rw[:, 3, :], rw[:, 2, :], float(N), None, ALU.mult))
                        step(V.tensor_scalar(rw[:, 4, :], rw[:, 3, :], CAPACITY, None, ALU.is_gt))
                        step(V.tensor_scalar(rw[:, 3, :], rw[:, 3, :], CAPACITY, None, ALU.max))
                        step(V.reciprocal(rw[:, 5, :], rw[:, 3, :]))
                        step(V.tensor_scalar(rw[:, 5, :], rw[:, 5, :], CAPACITY, -1.0, ALU.mult, ALU.add))
                        step(V.tensor_tensor(rw[:, 5, :], rw[:, 5, :], rw[:, 4, :], ALU.mult))
                        step(V.tensor_scalar(rw[:, 5, :], rw[:, 5, :], 1.0, None, ALU.add))
                        step(V.tensor_tensor(rw[:, 6, :], rw[:, 2, :], rw[:, 5, :], ALU.mult))
                        softmax(rw[:, 6, :], rw[:, 7, :], NE1, 2)
                        step(V.max(top[:, :], rw[:, 7, :]))
                        V.max_index(topi[:, :], top[:, :], rw[:, 7, :]).then_inc(s_rt, 1)
                        softmax(top[:, 0:2], wts[:, :], 2, 3)
                        step(V.tensor_copy(wts[:, :], wts[:, :]))
                        V.tensor_copy(rw[:, 8, 0:2], wts[:, :]).then_inc(s_wc, 1)
                        dve.wait_ge(s_wcd, 1)
                        step(V.tensor_copy(wcol[:, :], pm[:, 0:2]))

                    @block.scalar
                    def _(act):
                        act.sem_inc(s_c, 1)
                        row_deviations(act, s_mv, s_std)
                        with act.Fori(0, NG) as g:
                            for k in range(GT):
                                act.wait_ge(s_t, g * GT + (k + 1))
                                nc.scalar.copy(columns_of(HT, g * GT + k), by_chunk(pt[:, k, 0:D])).then_inc(s_c, 1)
                        for k, v in enumerate((rw[:, 2, :], rw[:, 7, :], wts[:, :])):
                            act.wait_ge(s_x, k + 1)
                            nc.scalar.activation(v, v, ACT.Exp).then_inc(s_xd, 1)

                hh = t("moe_hh", [P, 2, KF, GN])
                os_ = t("moe_os", [P, 2, GT, D])
                xb = t("moe_xb", [P, GT, D])
                HN = GN // 2
                mst = t("moe_st", [P, GT, 6])
                mmv = t("moe_mv", [P, GT, 2])
                msd = t("moe_sd", [P, GT])
                s_a, s_g, s_y, s_ye, s_sq, s_sr, s_o = (sem("moe_" + v) for v in (
                    "hidden", "gelu", "out", "out_added", "var", "std", "finished"))
                s_u, s_free, s_fold = sem("moe_stored"), sem("moe_out_free"), sem("moe_folded")
                with nc.psum_tensor("moe_ps1", [P, 2, 2, 512], f32) as p1, nc.psum_tensor("moe_ps2", [P, 4, 512], f32) as p2, \
                        nc.Block() as block:
                    @block.tensor
                    def _(pe):
                        pe.sem_inc(s_y, 1)
                        with pe.Fori(0, NG) as g:
                            for e in range(2):
                                for m in range(KF):
                                    u = e * KF + m
                                    if u >= 2:
                                        pe.wait_ge(s_g, g * (2 * KF) + (u - 1) + 1)
                                    else:
                                        pe.wait_ge(s_g, g * (2 * KF) + 1)
                                    for n in range(2):
                                        for c in range(KD):
                                            last = nc.tensor.matmul(p1[:, u % 2, n, 0:HN], w1[:, e, c, m * P:(m + 1) * P],
                                                                    HT[:, c, bass.ds(g * GN + n * HN, HN)],
                                                                    start=(c == 0), stop=(c == KD - 1))
                                    last.then_inc(s_a, 1)
                            pe.wait_ge(s_fold, 1)
                            pe.wait_ge(s_g, (g + 1) * (2 * KF) + 1)
                            for k in range(GT):
                                if k >= 4:
                                    pe.wait_ge(s_ye, g * GT + (k - 3) + 1)
                                else:
                                    pe.wait_ge(s_ye, g * GT + 1)
                                for e in range(2):
                                    for c in range(KF):
                                        last = nc.tensor.matmul(p2[:, k % 4, 0:D], hh[:, e, c, k * P:(k + 1) * P], w2[:, e, c, :],
                                                                start=(e == 0 and c == 0), stop=(e == 1 and c == KF - 1))
                                last.then_inc(s_y, 1)

                    @block.scalar
                    def _(act):
                        act.sem_inc(s_g, 1)
                        with act.Fori(0, NG) as g:
                            act.wait_ge(s_y, g * GT + 1)
                            for e in range(2):
                                for m in range(KF):
                                    u = e * KF + m
                                    act.wait_ge(s_a, g * (2 * KF) + (u + 1))
                                    nc.scalar.activation(hh[:, e, m, :].rearrange("p (n k) -> p n k", n=2), p1[:, u % 2, :, 0:HN], ACT.Gelu,
                                                         bias=b1[:, e, m:m + 1]).then_inc(s_g, 1)
                            for k in range(GT):
                                act.wait_ge(s_sq, g * GT + (k + 1))
                                nc.scalar.activation(msd[:, k:k + 1], mmv[:, k, 1:2], ACT.Sqrt).then_inc(s_sr, 1)

                    @block.vector
                    def _(dve):
                        dve.sem_inc(s_ye, 1)
                        V = nc.vector
                        for j in range(2):
                            V.tensor_scalar(w2[:, j, :, :].rearrange("p c f -> p (c f)"), w2[:, j, :, :].rearrange("p c f -> p (c f)"),
                                            wcol[:, j:j + 1], None, ALU.mult)
                        V.tensor_scalar(bs[:, :], b2[:, 0, :], wcol[:, 0:1], None, ALU.mult)
                        dve.drain()
                        V.scalar_tensor_tensor(bs[:, :], b2[:, 1, :], wcol[:, 1:2], bs[:, :], ALU.mult, ALU.add).then_inc(s_fold, 1)
                        dve.drain()
                        with dve.Fori(0, NG) as g:
                            ot = os_[:, 0, :, :]
                            dve.wait_ge(s_free, g + 1)
                            tl = bass.ds(g * GT, GT)
                            for k in range(GT):
                                normalise(os_[:, 1, k, :], g * GT + k)
                            dve.drain()
                            V.tensor_tensor(os_[:, 1, :, :], os_[:, 1, :, :], bs[:, :].unsqueeze(1).to_broadcast([P, GT, D]), ALU.add)
                            V.tensor_tensor(xb[:, :, :], X[:, tl, :], gb[:, 1, :].unsqueeze(1).to_broadcast([P, GT, D]), ALU.add)
                            dve.drain()

                            def finish(k):
                                dve.wait_ge(s_sr, g * GT + (k + 1))
                                V.reciprocal(msd[:, k:k + 1], msd[:, k:k + 1])
                                V.scalar_tensor_tensor(ot[:, k, :], ot[:, k, :], mmv[:, k, 0:1], gb[:, 0, :], ALU.subtract, ALU.mult)
                                dve.drain()
                                V.scalar_tensor_tensor(ot[:, k, :], ot[:, k, :], msd[:, k:k + 1], xb[:, k, :],
                                                       ALU.mult, ALU.add).then_inc(s_o, 1)

                            for k in range(GT):
                                dve.wait_ge(s_y, g * GT + (k + 1) + 1)
                                V.tensor_tensor(ot[:, k, :], p2[:, k % 4, 0:D], os_[:, 1, k, :], ALU.add).then_inc(s_ye, 1)
                                dve.drain()
                                V.bn_stats(mst[:, k, :], ot[:, k, :])
                                dve.drain()
                                V.bn_aggr(mmv[:, k, :], mst[:, k, :])
                                dve.drain()
                                V.tensor_scalar(mmv[:, k, 1:2], mmv[:, k, 1:2], EPS, None, ALU.add).then_inc(s_sq, 1)
                                if k > 0:
                                    finish(k - 1)
                            finish(GT - 1)

                    @block.sync
                    def _(sp):
                        sp.sem_inc(s_free, 1)
                        of = out[0:FULL * P, :].rearrange("(t p) d -> p t d", p=P)
                        with sp.Fori(0, NG - 1) as g:
                            sp.wait_ge(s_o, g * GT + GT)
                            sp.dma_start(of[:, bass.ds(g * GT, GT), :], os_[:, 0, :, :]).then_inc(s_u, 32)
                            sp.wait_ge(s_u, (g + 1) * 32)
                            sp.sem_inc(s_free, 1)
                        g = NG - 1
                        sp.wait_ge(s_o, NG * GT)
                        sp.dma_start(of[:, g * GT:FULL, :], os_[:, 0, 0:GT - 1, :]).then_inc(s_u, 16)
                        sp.dma_start(out[FULL * P:N, :], os_[0:TAIL, 0, GT - 1, :]).then_inc(s_u, 16)
                        sp.wait_ge(s_u, 32 * NG)

        stage_consts()
        with nc.sbuf_tensor("acc0", [P, NT * RW], f32) as acc:
            stage_start(acc)
            end_stage()
            message_pass("mp0", acc)
            stage_gin(acc)
        end_stage()
        stage_gat()
        end_stage()
        with nc.sbuf_tensor("acc1", [P, NT * RW], f32) as acc:
            stage_lin(acc)
            message_pass("mp1", acc)
            stage_add(acc)
        end_stage()
        stage_moe()


_INS = ['x', 'src', 'dst', 'L0_gnn_W1', 'L0_gnn_b1', 'L0_gnn_g1', 'L0_gnn_bt1', 'L0_gnn_W2', 'L0_gnn_b2',
        'L0_gnn_g2', 'L0_gnn_bt2', 'L0_gnn_eps_gin', 'L0_ffn_W_gat', 'L0_ffn_att_src', 'L0_ffn_att_dst',
        'L0_ffn_b_gat', 'L0_ffn_ln_gamma', 'L0_ffn_ln_beta', 'L0_ffn_W1', 'L0_ffn_b1', 'L0_ffn_W2', 'L0_ffn_b2',
        'L0_ffn_edge_index', 'L1_gnn_W', 'L1_gnn_b', 'L1_ffn_Wr', 'L1_ffn_br', 'L1_ffn_W1', 'L1_ffn_b1',
        'L1_ffn_W2', 'L1_ffn_b2', 'L1_ffn_gamma', 'L1_ffn_beta']


def kernel(**inputs):
    import numpy as _np
    import concourse.bacc as _bacc
    from concourse import mybir as _mybir
    from concourse.bass_utils import run_bass_kernel_spmd as _run

    nc = _bacc.Bacc("TRN2", target_bir_lowering=False, num_devices=1)
    arrays, aps = {}, {}
    for name in _INS:
        v = _np.asarray(inputs[name])
        if name == "L1_gnn_W":
            name, v = "L1_gnn_Wt", v.T
        if name == "L0_gnn_eps_gin":
            v = v.reshape(1)
        v = _np.ascontiguousarray(v)
        arrays["in_" + name] = v
        aps[name] = nc.dram_tensor("in_" + name, v.shape, _mybir.dt.from_np(v.dtype), kind="ExternalInput").ap()
    out = nc.dram_tensor("out_0", (N, D), _mybir.dt.float32, kind="ExternalOutput").ap()
    build(nc, aps, out)
    r = _run(nc, [arrays], core_ids=[0])
    return r.results[0]["out_0"]
```
